# Optimizing a Trainium2 kernel written in Bass

```python
import numpy as np
import jax
import jax.numpy as jnp

def _softmax(x, axis=-1):
    return jax.nn.softmax(x, axis=axis)

def _gelu(x):
    return jax.nn.gelu(x, approximate=True)

def _silu(x):
    return jax.nn.silu(x)

def _sigmoid(x):
    return jax.nn.sigmoid(x)

def _layernorm(x, axis=-1, eps=1e-05):
    m = jnp.mean(x, axis=axis, keepdims=True)
    v = jnp.var(x, axis=axis, keepdims=True)
    return (x - m) / jnp.sqrt(v + eps)

def _scatter_add(tgt, idx, src, axis=0):
    return tgt.at[idx].add(src)

def _segment_sum(src, seg, n):
    return jax.ops.segment_sum(src, seg, n)
kernel_name = 'mk_cond_resid_d4_seqx_r2_d5ba03'

def setup_inputs(seed: int=0):
    np.random.seed(seed)
    _w = jnp.asarray

    def _rec_inputs():
        import jax
        import jax.numpy as jnp
        _rk = jax.random.key(seed)
        x = -0.0002928 + 1 * jax.random.normal(jax.random.fold_in(_rk, 1), (32, 128, 512), jnp.float32)
        _lenS = 128 - jax.random.randint(jax.random.fold_in(_rk, 7), (32,), 0, max(1, 128 // 4) + 1, jnp.int32)
        _lenS2 = 128 - jax.random.randint(jax.random.fold_in(_rk, 8), (32,), 0, max(1, 128 // 4) + 1, jnp.int32)
        cond_256 = -0.0209273 + 1.04763 * jax.random.normal(jax.random.fold_in(_rk, 11), (32, 128), jnp.float32)
        _validS = jnp.arange(128)[None, :] < _lenS[:, None]
        _validS2 = jnp.arange(128)[None, :] < _lenS2[:, None]
        _causal = jnp.tril(jnp.ones((128, 128), dtype=bool))
        mask_SxS_bk1 = jnp.broadcast_to(_validS[0:1, :], (128, 128))
        return (x, cond_256, mask_SxS_bk1)
    x, cond_256, mask_SxS_bk1 = _rec_inputs()

    def _L0_cond_setup():
        import jax, jax.numpy as jnp
        import numpy as np
        B, S, E, H, CD = (4, 512, 512, 16, 128)
        HD = E // H
        FIELD_COHERENCE = 0.7
        COH_THRESHOLD = 0.5
        FIELD_COUPLING = 0.3

        def _layernorm(x, g, b, eps=1e-05):
            mu = x.mean(-1, keepdims=True)
            var = ((x - mu) ** 2).mean(-1, keepdims=True)
            return (x - mu) * jax.lax.rsqrt(var + eps) * g + b
        key = jax.random.key(seed)
        ks = jax.random.split(key, 10)
        s = 0.02
        f32 = jnp.float32
        return {'x': jax.random.normal(ks[0], (B, S, E), f32), 'consciousness_state': jax.random.normal(ks[1], (B, CD), f32), 'Wqkv': jax.random.normal(ks[2], (3 * E, E), f32) * s, 'bqkv': jnp.zeros((3 * E,), f32), 'Wout': jax.random.normal(ks[3], (E, E), f32) * s, 'bout': jnp.zeros((E,), f32), 'Wc1': jax.random.normal(ks[4], (E, E + CD), f32) * s, 'bc1': jnp.zeros((E,), f32), 'Wc2': jax.random.normal(ks[5], (H, E), f32) * s, 'bc2': jnp.zeros((H,), f32), 'We1': jax.random.normal(ks[6], (E, CD), f32) * s, 'be1': jnp.zeros((E,), f32), 'We2': jax.random.normal(ks[7], (E, E), f32) * s, 'be2': jnp.zeros((E,), f32), 'ln_g': jnp.ones((E,), f32), 'ln_b': jnp.zeros((E,), f32)}
    _L0_cond_all = _L0_cond_setup()
    _L0_cond_in = {k: v for k, v in _L0_cond_all.items() if k in ('Wqkv', 'bqkv', 'Wout', 'bout', 'Wc1', 'bc1', 'Wc2', 'bc2', 'We1', 'be1', 'We2', 'be2', 'ln_g', 'ln_b')}
    del _L0_cond_all

    def _L1_cond_setup():
        import jax, jax.numpy as jnp
        import numpy as np
        EPS = 1e-06
        key = jax.random.key(seed)
        ks = jax.random.split(key, 8)
        B, S, E, C = (2, 1024, 512, 128)
        x = jax.random.normal(ks[0], (B, S, E), dtype=jnp.float32)
        mask = jnp.triu(jnp.ones((S, S), dtype=bool), k=1)
        conditioning = jax.random.normal(ks[1], (B, C), dtype=jnp.float32)
        sc = 1.0 / np.sqrt(E)
        Wq = jax.random.normal(ks[2], (E, E), dtype=jnp.float32) * sc
        Wk = jax.random.normal(ks[3], (E, E), dtype=jnp.float32) * sc
        Wv = jax.random.normal(ks[4], (E, E), dtype=jnp.float32) * sc
        Wo = jax.random.normal(ks[5], (E, E), dtype=jnp.float32) * sc
        rms_scale = jnp.ones((E,), dtype=jnp.float32)
        Wc = jax.random.normal(ks[6], (2 * E, C), dtype=jnp.float32) * 0.02
        bc = jax.random.normal(ks[7], (2 * E,), dtype=jnp.float32) * 0.02
        return {'x': x, 'mask': mask, 'conditioning': conditioning, 'Wq': Wq, 'Wk': Wk, 'Wv': Wv, 'Wo': Wo, 'rms_scale': rms_scale, 'Wc': Wc, 'bc': bc}
    _L1_cond_all = _L1_cond_setup()
    _L1_cond_in = {k: v for k, v in _L1_cond_all.items() if k in ('Wq', 'Wk', 'Wv', 'Wo', 'rms_scale', 'Wc', 'bc')}
    del _L1_cond_all

    def _L2_cond_setup():
        import jax, jax.numpy as jnp
        import numpy as np
        D_MODEL = 512
        D_T = 128
        N_HEADS = 16
        HIDDEN = 4 * D_MODEL
        EPS = 1e-06

        def _tc_rmsnorm(x, t, gw, gb, bw, bb):
            g = (t @ gw.T + gb)[:, None, :]
            b = (t @ bw.T + bb)[:, None, :]
            inv_rms = jax.lax.rsqrt(jnp.mean(x * x, axis=-1, keepdims=True) + EPS)
            return g * x * inv_rms + b

        def _attention(x, Wq, Wk, Wv, Wo):
            B, L, D = x.shape
            H = N_HEADS
            dh = D // H
            scale = np.sqrt(dh).astype(np.float32)
            q = (x @ Wq.T).reshape(B, L, H, dh)
            k = (x @ Wk.T).reshape(B, L, H, dh)
            v = (x @ Wv.T).reshape(B, L, H, dh)
            attn = jnp.einsum('blhd,bmhd->bhlm', q, k) / scale
            p = jax.nn.softmax(attn, axis=-1)
            o = jnp.einsum('bhlm,bmhd->blhd', p, v).reshape(B, L, D)
            return o @ Wo.T

        def _swiglu(x, gate_w, hid_w, out_w):
            return jax.nn.silu(x @ gate_w.T) * (x @ hid_w.T) @ out_w.T
        key = jax.random.key(seed)
        ks = jax.random.split(key, 20)
        B, L = (8, 512)
        s_d = 1.0 / np.sqrt(D_MODEL)
        s_t = 1.0 / np.sqrt(D_T)
        s_h = 1.0 / np.sqrt(HIDDEN)
        return {'x': jax.random.normal(ks[0], (B, L, D_MODEL), jnp.float32), 't': jax.random.normal(ks[1], (B, D_T), jnp.float32), 'Wq': jax.random.normal(ks[2], (D_MODEL, D_MODEL), jnp.float32) * s_d, 'Wk': jax.random.normal(ks[3], (D_MODEL, D_MODEL), jnp.float32) * s_d, 'Wv': jax.random.normal(ks[4], (D_MODEL, D_MODEL), jnp.float32) * s_d, 'Wo': jax.random.normal(ks[5], (D_MODEL, D_MODEL), jnp.float32) * s_d, 'g1w': jax.random.normal(ks[6], (D_MODEL, D_T), jnp.float32) * s_t, 'g1b': jnp.ones((D_MODEL,), jnp.float32), 'b1w': jax.random.normal(ks[7], (D_MODEL, D_T), jnp.float32) * s_t, 'b1b': jnp.zeros((D_MODEL,), jnp.float32), 'g2w': jax.random.normal(ks[8], (D_MODEL, D_T), jnp.float32) * s_t, 'g2b': jnp.ones((D_MODEL,), jnp.float32), 'b2w': jax.random.normal(ks[9], (D_MODEL, D_T), jnp.float32) * s_t, 'b2b': jnp.zeros((D_MODEL,), jnp.float32), 'gate_w': jax.random.normal(ks[10], (HIDDEN, D_MODEL), jnp.float32) * s_d, 'hid_w': jax.random.normal(ks[11], (HIDDEN, D_MODEL), jnp.float32) * s_d, 'out_w': jax.random.normal(ks[12], (D_MODEL, HIDDEN), jnp.float32) * s_h}
    _L2_cond_all = _L2_cond_setup()
    _L2_cond_in = {k: v for k, v in _L2_cond_all.items() if k in ('Wq', 'Wk', 'Wv', 'Wo', 'g1w', 'g1b', 'b1w', 'b1b', 'g2w', 'g2b', 'b2w', 'b2b', 'gate_w', 'hid_w', 'out_w')}
    del _L2_cond_all

    def _L3_cond_setup():
        import jax, jax.numpy as jnp
        import numpy as np
        EPS = 1e-08

        def hamilton(q1, q2):
            w1, x1, y1, z1 = (q1[..., i, :] for i in range(4))
            w2, x2, y2, z2 = (q2[..., i, :] for i in range(4))
            w = w1 * w2 - x1 * x2 - y1 * y2 - z1 * z2
            x = w1 * x2 + x1 * w2 + y1 * z2 - z1 * y2
            y = w1 * y2 - x1 * z2 + y1 * w2 + z1 * x2
            z = w1 * z2 + x1 * y2 - y1 * x2 + z1 * w2
            return jnp.stack([w, x, y, z], axis=-2)

        def _normalize(q):
            return q / jnp.sqrt(jnp.sum(q * q, axis=0, keepdims=True) + EPS)
        key = jax.random.key(seed)
        k1, k2, k3, k4 = jax.random.split(key, 4)
        B, T, d_model = (4, 2048, 512)
        quat_dim = d_model // 4
        x = jax.random.normal(k1, (B, T, d_model), dtype=jnp.float32)
        q_left = jax.random.normal(k2, (4, quat_dim), dtype=jnp.float32)
        q_right = jax.random.normal(k3, (4, quat_dim), dtype=jnp.float32)
        spectral_gate = jax.random.uniform(k4, (1, 1, 1, quat_dim), dtype=jnp.float32)
        return {'x': x, 'q_left': q_left, 'q_right': q_right, 'spectral_gate': spectral_gate}
    _L3_cond_all = _L3_cond_setup()
    _L3_cond_in = {k: v for k, v in _L3_cond_all.items() if k in ('q_right', 'spectral_gate')}
    del _L3_cond_all
    return {'x': x, 'cond_256': cond_256, 'mask_SxS_bk1': mask_SxS_bk1, 'L0_cond_Wqkv': _L0_cond_in['Wqkv'], 'L0_cond_bqkv': _L0_cond_in['bqkv'], 'L0_cond_Wout': _L0_cond_in['Wout'], 'L0_cond_bout': _L0_cond_in['bout'], 'L0_cond_Wc1': _L0_cond_in['Wc1'], 'L0_cond_bc1': _L0_cond_in['bc1'], 'L0_cond_Wc2': _L0_cond_in['Wc2'], 'L0_cond_bc2': _L0_cond_in['bc2'], 'L0_cond_We1': _L0_cond_in['We1'], 'L0_cond_be1': _L0_cond_in['be1'], 'L0_cond_We2': _L0_cond_in['We2'], 'L0_cond_be2': _L0_cond_in['be2'], 'L0_cond_ln_g': _L0_cond_in['ln_g'], 'L0_cond_ln_b': _L0_cond_in['ln_b'], 'L1_cond_Wq': _L1_cond_in['Wq'], 'L1_cond_Wk': _L1_cond_in['Wk'], 'L1_cond_Wv': _L1_cond_in['Wv'], 'L1_cond_Wo': _L1_cond_in['Wo'], 'L1_cond_rms_scale': _L1_cond_in['rms_scale'], 'L1_cond_Wc': _L1_cond_in['Wc'], 'L1_cond_bc': _L1_cond_in['bc'], 'L2_cond_Wq': _L2_cond_in['Wq'], 'L2_cond_Wk': _L2_cond_in['Wk'], 'L2_cond_Wv': _L2_cond_in['Wv'], 'L2_cond_Wo': _L2_cond_in['Wo'], 'L2_cond_g1w': _L2_cond_in['g1w'], 'L2_cond_g1b': _L2_cond_in['g1b'], 'L2_cond_b1w': _L2_cond_in['b1w'], 'L2_cond_b1b': _L2_cond_in['b1b'], 'L2_cond_g2w': _L2_cond_in['g2w'], 'L2_cond_g2b': _L2_cond_in['g2b'], 'L2_cond_b2w': _L2_cond_in['b2w'], 'L2_cond_b2b': _L2_cond_in['b2b'], 'L2_cond_gate_w': _L2_cond_in['gate_w'], 'L2_cond_hid_w': _L2_cond_in['hid_w'], 'L2_cond_out_w': _L2_cond_in['out_w'], 'L3_cond_q_right': _L3_cond_in['q_right'], 'L3_cond_spectral_gate': _L3_cond_in['spectral_gate']}

def reference(x, cond_256, mask_SxS_bk1, L0_cond_Wqkv, L0_cond_bqkv, L0_cond_Wout, L0_cond_bout, L0_cond_Wc1, L0_cond_bc1, L0_cond_Wc2, L0_cond_bc2, L0_cond_We1, L0_cond_be1, L0_cond_We2, L0_cond_be2, L0_cond_ln_g, L0_cond_ln_b, L1_cond_Wq, L1_cond_Wk, L1_cond_Wv, L1_cond_Wo, L1_cond_rms_scale, L1_cond_Wc, L1_cond_bc, L2_cond_Wq, L2_cond_Wk, L2_cond_Wv, L2_cond_Wo, L2_cond_g1w, L2_cond_g1b, L2_cond_b1w, L2_cond_b1b, L2_cond_g2w, L2_cond_g2b, L2_cond_b2w, L2_cond_b2b, L2_cond_gate_w, L2_cond_hid_w, L2_cond_out_w, L3_cond_q_right, L3_cond_spectral_gate):
    import jax
    import jax.numpy as jnp

    def _L0_cond_ref(x, consciousness_state, Wqkv, bqkv, Wout, bout, Wc1, bc1, Wc2, bc2, We1, be1, We2, be2, ln_g, ln_b):
        import jax, jax.numpy as jnp
        import numpy as np
        B, S, E, H, CD = (4, 512, 512, 16, 128)
        HD = E // H
        FIELD_COHERENCE = 0.7
        COH_THRESHOLD = 0.5
        FIELD_COUPLING = 0.3

        def _layernorm(x, g, b, eps=1e-05):
            mu = x.mean(-1, keepdims=True)
            var = ((x - mu) ** 2).mean(-1, keepdims=True)
            return (x - mu) * jax.lax.rsqrt(var + eps) * g + b
        Bb, Ss, Ee = x.shape
        qkv = (x @ Wqkv.T + bqkv).reshape(Bb, Ss, 3, H, HD).transpose(2, 0, 3, 1, 4)
        q, k, v = (qkv[0], qkv[1], qkv[2])
        attn = jax.nn.softmax(jnp.einsum('bhid,bhjd->bhij', q, k) / jnp.sqrt(jnp.float32(HD)), axis=-1)
        cs_exp = jnp.broadcast_to(consciousness_state[:, None, :], (Bb, Ss, CD))
        comb = jnp.concatenate([x, cs_exp], axis=-1)
        coh = jax.nn.sigmoid(jnp.tanh(comb @ Wc1.T + bc1) @ Wc2.T + bc2).transpose(0, 2, 1)
        mod = attn * coh[..., None]
        mod = mod / (mod.sum(-1, keepdims=True) + 1e-08)
        fp = _layernorm(jax.nn.relu(consciousness_state @ We1.T + be1) @ We2.T + be2, ln_g, ln_b)
        pos = jnp.arange(Ss, dtype=jnp.float32)
        inv = 10000.0 ** jnp.repeat(jnp.arange(0, Ee, 2, dtype=jnp.float32) / Ee, 2)
        pe = jnp.sin(pos[:, None] / inv[None, :])
        fa = jax.nn.softmax(jnp.einsum('be,se->bs', fp, pe), axis=-1)
        fi = FIELD_COUPLING * FIELD_COHERENCE
        mod = (1.0 - fi) * mod + fi * fa[:, None, :, None]
        out = jnp.einsum('bhij,bhjd->bhid', mod, v).transpose(0, 2, 1, 3).reshape(Bb, Ss, Ee)
        return out @ Wout.T + bout

    def _L1_cond_ref(x, mask, conditioning, Wq, Wk, Wv, Wo, rms_scale, Wc, bc):
        import jax, jax.numpy as jnp
        import numpy as np
        EPS = 1e-06
        B, S, E = x.shape
        H = 16
        D = E // H
        scale = D ** (-0.5)

        def proj(W):
            return (x @ W.T).reshape(B, S, H, D).transpose(0, 2, 1, 3)
        q, k, v = (proj(Wq), proj(Wk), proj(Wv))
        scores = jnp.einsum('bhsd,bhtd->bhst', q, k) * scale
        scores = jnp.where(mask[None, None, :, :], -jnp.inf, scores)
        attn = jax.nn.softmax(scores, axis=-1)
        out = jnp.einsum('bhst,bhtd->bhsd', attn, v)
        out = out.transpose(0, 2, 1, 3).reshape(B, S, E)
        out = out @ Wo.T
        rms = jnp.sqrt(jnp.mean(out * out, axis=-1, keepdims=True) + EPS)
        xn = out / rms * rms_scale
        mod = jax.nn.silu(conditioning) @ Wc.T + bc
        shift, sc = jnp.split(mod, 2, axis=-1)
        xn = xn * (1.0 + sc[:, None, :]) + shift[:, None, :]
        return xn

    def _L2_cond_ref(x, t, Wq, Wk, Wv, Wo, g1w, g1b, b1w, b1b, g2w, g2b, b2w, b2b, gate_w, hid_w, out_w):
        import jax, jax.numpy as jnp
        import numpy as np
        D_MODEL = 512
        D_T = 128
        N_HEADS = 16
        HIDDEN = 4 * D_MODEL
        EPS = 1e-06

        def _tc_rmsnorm(x, t, gw, gb, bw, bb):
            g = (t @ gw.T + gb)[:, None, :]
            b = (t @ bw.T + bb)[:, None, :]
            inv_rms = jax.lax.rsqrt(jnp.mean(x * x, axis=-1, keepdims=True) + EPS)
            return g * x * inv_rms + b

        def _attention(x, Wq, Wk, Wv, Wo):
            B, L, D = x.shape
            H = N_HEADS
            dh = D // H
            scale = np.sqrt(dh).astype(np.float32)
            q = (x @ Wq.T).reshape(B, L, H, dh)
            k = (x @ Wk.T).reshape(B, L, H, dh)
            v = (x @ Wv.T).reshape(B, L, H, dh)
            attn = jnp.einsum('blhd,bmhd->bhlm', q, k) / scale
            p = jax.nn.softmax(attn, axis=-1)
            o = jnp.einsum('bhlm,bmhd->blhd', p, v).reshape(B, L, D)
            return o @ Wo.T

        def _swiglu(x, gate_w, hid_w, out_w):
            return jax.nn.silu(x @ gate_w.T) * (x @ hid_w.T) @ out_w.T
        x = x + _attention(_tc_rmsnorm(x, t, g1w, g1b, b1w, b1b), Wq, Wk, Wv, Wo)
        return x + _swiglu(_tc_rmsnorm(x, t, g2w, g2b, b2w, b2b), gate_w, hid_w, out_w)

    def _L3_cond_ref(x, q_left, q_right, spectral_gate):
        import jax, jax.numpy as jnp
        import numpy as np
        EPS = 1e-08

        def hamilton(q1, q2):
            w1, x1, y1, z1 = (q1[..., i, :] for i in range(4))
            w2, x2, y2, z2 = (q2[..., i, :] for i in range(4))
            w = w1 * w2 - x1 * x2 - y1 * y2 - z1 * z2
            x = w1 * x2 + x1 * w2 + y1 * z2 - z1 * y2
            y = w1 * y2 - x1 * z2 + y1 * w2 + z1 * x2
            z = w1 * z2 + x1 * y2 - y1 * x2 + z1 * w2
            return jnp.stack([w, x, y, z], axis=-2)

        def _normalize(q):
            return q / jnp.sqrt(jnp.sum(q * q, axis=0, keepdims=True) + EPS)
        B, T, d_model = x.shape
        quat_dim = d_model // 4
        x_quat = x.reshape(B, T, 4, quat_dim)
        x_spectral = jnp.fft.fft(x_quat, axis=1)
        x_filtered = jnp.fft.ifft(x_spectral * spectral_gate, axis=1).real.astype(x.dtype)
        q_left_n = _normalize(q_left)
        q_right_n = _normalize(q_right)
        conj_sign = jnp.array([1.0, -1.0, -1.0, -1.0], dtype=x.dtype)[:, None]
        q_right_conj = q_right_n * conj_sign
        x_right = hamilton(x_filtered, q_right_conj)
        x_rotated = hamilton(q_left_n, x_right)
        return x_rotated.reshape(B, T, d_model)
    x = x + _L0_cond_ref(x, cond_256, L0_cond_Wqkv, L0_cond_bqkv, L0_cond_Wout, L0_cond_bout, L0_cond_Wc1, L0_cond_bc1, L0_cond_Wc2, L0_cond_bc2, L0_cond_We1, L0_cond_be1, L0_cond_We2, L0_cond_be2, L0_cond_ln_g, L0_cond_ln_b)
    x = x + _L1_cond_ref(x, mask_SxS_bk1, cond_256, L1_cond_Wq, L1_cond_Wk, L1_cond_Wv, L1_cond_Wo, L1_cond_rms_scale, L1_cond_Wc, L1_cond_bc)
    x = x + _L2_cond_ref(x, cond_256, L2_cond_Wq, L2_cond_Wk, L2_cond_Wv, L2_cond_Wo, L2_cond_g1w, L2_cond_g1b, L2_cond_b1w, L2_cond_b1b, L2_cond_g2w, L2_cond_g2b, L2_cond_b2w, L2_cond_b2b, L2_cond_gate_w, L2_cond_hid_w, L2_cond_out_w)
    x = x + _L3_cond_ref(x, cond_256, L3_cond_q_right, L3_cond_spectral_gate)
    return x

_drawn_inputs = setup_inputs


def setup_inputs(seed=0):
    import zlib

    import numpy as np

    out = dict(_drawn_inputs(seed))
    spreads = {'L0_cond_bqkv': (0.0, 0.1),
     'L0_cond_bout': (0.0, 0.1),
     'L0_cond_bc1': (0.0, 2.0),
     'L0_cond_bc2': (0.0, 2.0),
     'L0_cond_be1': (0.0, 0.1),
     'L0_cond_be2': (0.0, 0.1),
     'L0_cond_ln_g': (1.0, 0.2),
     'L0_cond_ln_b': (0.0, 0.487),
     'L1_cond_rms_scale': (1.0, 0.2),
     'L2_cond_g1b': (1.0, 0.2),
     'L2_cond_b1b': (0.0, 0.1),
     'L2_cond_g2b': (1.0, 0.2),
     'L2_cond_b2b': (0.0, 0.1)}
    factors = {'L0_cond_Wc1': 190.62, 'L0_cond_Wc2': 185.008, 'L1_cond_bc': 2.694}
    for name, (base, spread) in spreads.items():
        noise = np.random.default_rng([zlib.crc32(name.encode()), seed]).standard_normal(out[name].shape)
        drawn = base * np.exp(spread * noise) if base else spread * noise
        out[name] = jnp.asarray(drawn.astype(out[name].dtype))
    for name, factor in factors.items():
        out[name] = (out[name] * factor).astype(out[name].dtype)
    return out
```

```python
from contextlib import ExitStack

import numpy as np

import concourse.bass as bass
from concourse import mybir


ALU = mybir.AluOpType
ACT = mybir.ActivationFunctionType
F32 = mybir.dt.float32
F32R = mybir.dt.float32r
AX_X = mybir.AxisListType.X

P = 128
B = 32
E = 512
CH = E // P
H = 16
HD = E // H
VW = HD + 2
T = 256
NB = T // P
G = B // NB
UNITS = NB * CH
SLOTS = UNITS + 4
HID = 4 * E
FT = 512
FG = B * P // FT
SWEEPS = 2
HC = HID // P // SWEEPS
SCALE = float(HD) ** -0.5
FIELD = 0.3 * 0.7
MASKED = -1e30
KB_DONE = 2 * 4 * 16


def f32(ap):
    return ap.bitcast(F32)


def need(eng, sem, value):
    if isinstance(value, int) and value <= 0:
        return
    eng.wait_ge(sem, value)


def need_pool(eng, sem, value, waited):
    need(eng, sem, value)
    if not isinstance(value, int):
        eng.sem_inc(waited, 1)


def held(nc, hold, name):
    s = nc.alloc_semaphore(name)
    hold.append(s)
    return s


def bcast_mid(ap, n):
    return ap.unsqueeze(1).broadcast_to([ap.shape[0], n, ap.shape[1]])


def bcast_last(ap, n):
    return ap.unsqueeze(2).broadcast_to([ap.shape[0], ap.shape[1], n])


def split_weights(nc, ctx, hold, tag, loads, stage_cols):
    stage = [ctx.enter_context(nc.sbuf_tensor(f"{tag}_stage{k}", [P, stage_cols], F32)) for k in range(2)]
    w_loaded = [held(nc, hold, f"{tag}_w_loaded{k}") for k in range(2)]
    w_high = held(nc, hold, f"{tag}_w_high")
    w_low = held(nc, hold, f"{tag}_w_low")
    block = ctx.enter_context(nc.Block())

    @block.sync
    def _(sp):
        for n, (src, _, _) in enumerate(loads):
            need(sp, w_low, n - 1)
            sp.dma_start(stage[n % 2][:, 0:src.shape[1]], src).then_inc(w_loaded[n % 2], 16)

    @block.scalar
    def _(act):
        for n, (src, high, _) in enumerate(loads):
            act.wait_ge(w_loaded[n % 2], 16 * (n // 2 + 1))
            nc.scalar.activation(high, stage[n % 2][:, 0:src.shape[1]], ACT.Copy).then_inc(w_high, 1)

    @block.vector
    def _(dve):
        for n, (src, high, low) in enumerate(loads):
            dve.wait_ge(w_high, n + 1)
            nc.vector.tensor_tensor(low, stage[n % 2][:, 0:src.shape[1]], f32(high), ALU.subtract).then_inc(w_low, 1)


def prepare(nc, hold, k, a):
    with ExitStack() as ctx:
        def sb(name, shape, dt=F32):
            return ctx.enter_context(nc.sbuf_tensor("prep_" + name, shape, dt))

        def sem(name):
            return held(nc, hold, "prep_" + name)

        w_c1c = sb("w_c1c", [P, E])
        w_e1 = sb("w_e1", [P, E])
        w_e2 = sb("w_e2", [P, CH, E])
        w_c = sb("w_c", [P, 2 * E])
        w_gb = sb("w_gb", [P, 4, E])
        pe_t = sb("pe_t", [P, CH, P])
        col = {n: sb(n, [P, s]) for n, s in (("bc1", CH), ("be1", CH), ("bc", 2 * CH), ("rms", CH), ("g1b", CH), ("b1b", CH), ("g2b", CH), ("b2b", CH))}
        rows = {n: sb(n, [B, E]) for n in ("be2", "ln_g", "ln_b")}
        cond = sb("cond", [P, B])
        qr = sb("qr", [P, 4])
        gate = sb("gate", [P, 1])
        mask8 = sb("mask8", [P, P], mybir.dt.uint8)
        maskf = sb("maskf", [P, P])
        ones_f = sb("ones_f", [P, P])
        silu_c = sb("silu_c", [P, B])
        relu1 = sb("relu1", [P, CH, B])
        fp = sb("fp", [B, E])
        fp_t = sb("fp_t", [P, CH, B])
        sq = sb("sq", [P, E])
        s1 = sb("s1", [P, 8])
        fa = sb("fa", [B, P])
        sc1 = sb("sc1", [P, CH, B])
        lq = sb("lq", [P, 4])
        rq = sb("rq", [P, 4])
        lm = sb("lm", [P, 16])
        rm = sb("rm", [P, 16])
        tq = sb("tq", [P, 4])
        ps = [ctx.enter_context(nc.psum_tensor(f"prep_ps{n}", [P, 512], F32)) for n in range(8)]
        loaded = sem("loaded")
        dve_step = sem("dve_step")
        pool_step = sem("pool_step")
        act_step = sem("act_step")
        pe_step = sem("pe_step")
        block = ctx.enter_context(nc.Block())
        loads = [(w_c1c[:], a["w_c1c"]), (w_e1[:], a["w_e1"]), (w_e2[:], a["w_e2"]), (w_c[:], a["w_c"]),
                 (w_gb[:], a["w_gb"]), (pe_t[:], a["pe_t"]), (cond[:], a["cond_t"]), (qr[:], a["qr_t"]),
                 (gate[:], a["gate_t"]), (mask8[:], a["mask"]), (k["bq"][:], a["bq_c"]), (k["bk"][:], a["bk_c"]),
                 (k["bout"][:], a["bout_c"]), (k["bv"][:], a["bv"].partition_broadcast(P)),
                 (k["bc2"][:], a["bc2"].partition_broadcast(P)), (k["ident"][:], a["eye"])]
        loads += [(col[n][:], a[n + "_c"]) for n in col]
        loads += [(rows[n][:], a[n].partition_broadcast(B)) for n in rows]

        @block.sync
        def _(sp):
            for dst, src in loads:
                sp.dma_start(dst, src).then_inc(loaded, 16)

        @block.tensor
        def _(pe):
            pe.wait_ge(loaded, 16 * len(loads))
            for c in range(CH):
                nc.tensor.matmul(ps[0][:, c * B:(c + 1) * B], w_c1c[:, c * P:(c + 1) * P], cond[:], start=True, stop=True)
            for c in range(CH):
                mm = nc.tensor.matmul(ps[1][:, c * B:(c + 1) * B], w_e1[:, c * P:(c + 1) * P], cond[:], start=True, stop=True)
            mm.then_inc(pe_step, 1)
            for n in range(4):
                for c in range(CH):
                    mm = nc.tensor.matmul(ps[2][:, (n * CH + c) * B:(n * CH + c + 1) * B], w_gb[:, n, c * P:(c + 1) * P], cond[:], start=True, stop=True)
            mm.then_inc(pe_step, 1)
            pe.wait_ge(act_step, 2)
            pe.wait_ge(dve_step, 3)
            for c in range(2 * CH):
                mm = nc.tensor.matmul(ps[3][:, c * B:(c + 1) * B], w_c[:, c * P:(c + 1) * P], silu_c[:], start=True, stop=True)
            mm.then_inc(pe_step, 1)
            for c in range(CH):
                mm = nc.tensor.matmul(ps[4][0:B, :], relu1[:, c, :], w_e2[:, c, :], start=(c == 0), stop=(c == CH - 1))
            mm.then_inc(pe_step, 1)
            pe.wait_ge(dve_step, 13)
            for c in range(CH):
                mm = nc.tensor.transpose(ps[5][:, c * B:(c + 1) * B], fp[:, c * P:(c + 1) * P], k["ident"][0:B, 0:B])
            mm.then_inc(pe_step, 1)
            pe.wait_ge(dve_step, 14)
            for c in range(CH):
                mm = nc.tensor.matmul(ps[6][0:B, 0:P], fp_t[:, c, :], pe_t[:, c, :], start=(c == 0), stop=(c == CH - 1))
            mm.then_inc(pe_step, 1)
            pe.wait_ge(dve_step, 18)
            nc.tensor.transpose(ps[7][:, 0:B], fa[:], k["ident"][0:B, 0:B]).then_inc(pe_step, 1)

        @block.scalar
        def _(act):
            act.wait_ge(loaded, 16 * len(loads))
            nc.scalar.activation(silu_c[:], cond[:], ACT.Exp, scale=-1.0).then_inc(act_step, 1)
            act.wait_ge(pe_step, 1)
            for c in range(CH):
                last = nc.scalar.activation(relu1[:, c, :], ps[1][:, c * B:(c + 1) * B], ACT.Relu, bias=col["be1"][:, c:c + 1])
            last.then_inc(act_step, 1)
            act.wait_ge(dve_step, 10)
            nc.scalar.activation(s1[0:B, 2:3], s1[0:B, 1:2], ACT.Sqrt).then_inc(act_step, 1)
            act.wait_ge(dve_step, 16)
            nc.scalar.activation(fa[:], fa[:], ACT.Exp, accum_out=s1[0:B, 5:6]).then_inc(act_step, 1)
            act.wait_ge(dve_step, 20)
            nc.scalar.activation(s1[:, 6:8], s1[:, 6:8], ACT.Sqrt).then_inc(act_step, 1)

        @block.vector
        def _(dve):
            count = [0]

            def done(ins):
                count[0] += 1
                ins.then_inc(dve_step, 1)
                dve.wait_ge(dve_step, count[0])

            dve.wait_ge(loaded, 16 * len(loads))
            dve.wait_ge(act_step, 1)
            done(nc.vector.tensor_scalar_add(silu_c[:], silu_c[:], 1.0))
            done(nc.vector.reciprocal(silu_c[:], silu_c[:]))
            done(nc.vector.tensor_tensor(silu_c[:], silu_c[:], cond[:], ALU.mult))
            dve.wait_ge(pe_step, 2)
            for c in range(CH):
                nc.vector.tensor_scalar_add(k["tanh_bias"][:, c, :], ps[0][:, c * B:(c + 1) * B], col["bc1"][:, c:c + 1])
            for n, (name, bias) in enumerate((("g1", "g1b"), ("b1", "b1b"), ("g2", "g2b"), ("b2", "b2b"))):
                for c in range(CH):
                    o = (n * CH + c) * B
                    last = nc.vector.tensor_scalar_add(k[name][:, c, :], ps[2][:, o:o + B], col[bias][:, c:c + 1])
            done(last)
            dve.wait_ge(pe_step, 3)
            for c in range(CH):
                nc.vector.tensor_scalar_add(k["shift"][:, c, :], ps[3][:, c * B:(c + 1) * B], col["bc"][:, c:c + 1])
            for c in range(CH):
                o = (CH + c) * B
                last = nc.vector.tensor_scalar(sc1[:, c, :], ps[3][:, o:o + B], col["bc"][:, CH + c:CH + c + 1], 1.0, ALU.add, ALU.add)
            done(last)
            for c in range(CH):
                last = nc.vector.tensor_scalar(k["gain"][:, c, :], sc1[:, c, :], col["rms"][:, c:c + 1], None, ALU.mult)
            done(last)
            dve.wait_ge(pe_step, 4)
            done(nc.vector.tensor_tensor(fp[:], ps[4][0:B, :], rows["be2"][:], ALU.add))
            done(nc.vector.tensor_reduce(s1[0:B, 0:1], fp[:], AX_X, ALU.add))
            nc.vector.tensor_scalar(s1[0:B, 0:1], s1[0:B, 0:1], -1.0 / E, None, ALU.mult).then_inc(pool_step, 1)
            dve.wait_ge(pool_step, 1)
            nc.vector.tensor_scalar(fp[:], fp[:], s1[0:B, 0:1], None, ALU.add).then_inc(pool_step, 1)
            dve.wait_ge(pool_step, 2)
            nc.vector.tensor_tensor(sq[0:B, :], fp[:], fp[:], ALU.mult).then_inc(pool_step, 1)
            dve.wait_ge(pool_step, 3)
            done(nc.vector.tensor_reduce(s1[0:B, 1:2], sq[0:B, :], AX_X, ALU.add))
            done(nc.vector.tensor_scalar(s1[0:B, 1:2], s1[0:B, 1:2], 1.0 / E, 1e-5, ALU.mult, ALU.add))
            dve.wait_ge(act_step, 3)
            done(nc.vector.reciprocal(s1[0:B, 3:4], s1[0:B, 2:3]))
            done(nc.vector.scalar_tensor_tensor(out=fp[:], in0=fp[:], scalar=s1[0:B, 3:4], in1=rows["ln_g"][:], op0=ALU.mult, op1=ALU.mult))
            done(nc.vector.tensor_tensor(fp[:], fp[:], rows["ln_b"][:], ALU.add))
            dve.wait_ge(pe_step, 5)
            done(nc.vector.tensor_copy(fp_t[:], ps[5][:, 0:CH * B].rearrange("p (c b) -> p c b", c=CH)))
            dve.wait_ge(pe_step, 6)
            done(nc.vector.reduce_max(s1[0:B, 4:5], ps[6][0:B, 0:P], AX_X))
            done(nc.vector.tensor_scalar(fa[:], ps[6][0:B, 0:P], s1[0:B, 4:5], None, ALU.subtract))
            dve.wait_ge(act_step, 4)
            done(nc.vector.reciprocal(s1[0:B, 4:5], s1[0:B, 5:6]))
            done(nc.vector.tensor_scalar(fa[:], fa[:], s1[0:B, 4:5], FIELD, ALU.mult, ALU.mult))
            dve.wait_ge(pe_step, 7)
            nc.vector.tensor_copy(k["field"][:], ps[7][:, 0:B])
            nc.vector.tensor_tensor(sq[:, 0:B], cond[:], cond[:], ALU.mult)
            done(nc.vector.tensor_tensor(sq[:, B:B + 4], qr[:], qr[:], ALU.mult))
            nc.vector.tensor_reduce(s1[:, 6:7], sq[:, 0:B], AX_X, ALU.add)
            nc.vector.tensor_reduce(s1[:, 7:8], sq[:, B:B + 4], AX_X, ALU.add).then_inc(pool_step, 1)
            dve.wait_ge(pool_step, 4)
            done(nc.vector.tensor_scalar_add(s1[:, 6:8], s1[:, 6:8], 1e-8))
            dve.wait_ge(act_step, 5)
            done(nc.vector.reciprocal(s1[:, 6:8], s1[:, 6:8]))
            nc.vector.tensor_scalar(lq[:], cond[:, 0:4], s1[:, 6:7], None, ALU.mult)
            done(nc.vector.tensor_scalar(rq[:], qr[:], s1[:, 7:8], gate[:, 0:1], ALU.mult, ALU.mult))
            sl = [[1, -1, -1, -1], [1, 1, -1, 1], [1, 1, 1, -1], [1, -1, 1, 1]]
            il = [[0, 1, 2, 3], [1, 0, 3, 2], [2, 3, 0, 1], [3, 2, 1, 0]]
            sr = [[1, 1, 1, 1], [-1, 1, -1, 1], [-1, 1, 1, -1], [-1, -1, 1, 1]]
            for i in range(4):
                for j in range(4):
                    nc.vector.tensor_scalar(lm[:, 4 * i + j:4 * i + j + 1], lq[:, il[i][j]:il[i][j] + 1], float(sl[i][j]), None, ALU.mult)
                    last = nc.vector.tensor_scalar(rm[:, 4 * i + j:4 * i + j + 1], rq[:, il[i][j]:il[i][j] + 1], float(sr[i][j]), None, ALU.mult)
            done(last)
            for i in range(4):
                done(nc.vector.tensor_scalar(k["mix"][:, 4 * i:4 * i + 4], rm[:, 0:4], lm[:, 4 * i:4 * i + 1], None, ALU.mult))
                for m in range(1, 4):
                    done(nc.vector.scalar_tensor_tensor(out=k["mix"][:, 4 * i:4 * i + 4], in0=rm[:, 4 * m:4 * m + 4], scalar=lm[:, 4 * i + m:4 * i + m + 1],
                                                        in1=k["mix"][:, 4 * i:4 * i + 4], op0=ALU.mult, op1=ALU.add))
                done(nc.vector.tensor_scalar_add(k["mix"][:, 5 * i:5 * i + 1], k["mix"][:, 5 * i:5 * i + 1], 1.0))
            done(nc.vector.tensor_copy(maskf[:], mask8[:]))
            nc.vector.tensor_scalar(k["mask"][:], maskf[:], MASKED, None, ALU.mult)
            done(nc.vector.tensor_reduce(tq[:, 0:1], maskf[:], AX_X, ALU.add))
            done(nc.vector.tensor_scalar(tq[:, 0:1], tq[:, 0:1], -1.0, float(P), ALU.mult, ALU.add))
            done(nc.vector.tensor_scalar_min(tq[:, 0:1], tq[:, 0:1], 1.0))
            done(nc.vector.reciprocal(tq[:, 1:2], tq[:, 0:1]))
            nc.vector.tensor_tensor(k["any_key"][:], tq[:, 0:1], tq[:, 1:2], ALU.mult)
            nc.vector.memset(k["ones"][:], 1.0)
            nc.vector.memset(ones_f[:], 1.0).then_inc(pool_step, 1)
            dve.wait_ge(pool_step, 5)
            nc.vector.tensor_copy(k["ones_r"][:], ones_f[:])
            done(nc.vector.tensor_copy(k["ident_r"][:], k["ident"][:]))


def attention(nc, hold, k, tag, x_in, x_out, weights, w_c2):
    L0, L1, L2 = (tag == t for t in ("L0", "L1", "L2"))
    names = ["k", "v", "q", "o"] + (["c"] if L0 else [])
    with ExitStack() as ctx:
        def sb(name, shape, dt=F32):
            return ctx.enter_context(nc.sbuf_tensor(f"{tag}_{name}", shape, dt))

        def sem(name):
            return held(nc, hold, f"{tag}_{name}")

        def bank(name):
            return ctx.enter_context(nc.psum_tensor(f"{tag}_{name}", [P, 512], F32))

        wh = {n: sb(f"w{n}h", [P, CH, E], F32R) for n in names}
        wl = {n: sb(f"w{n}l", [P, CH, E], F32R) for n in names}
        if L0:
            wh["c2"], wl["c2"] = sb("wc2h", [P, CH, H], F32R), sb("wc2l", [P, CH, H], F32R)
        with ExitStack() as wctx:
            flat = [(weights[n], wh[n][:].rearrange("p c e -> p (c e)"), wl[n][:].rearrange("p c e -> p (c e)")) for n in names]
            if L0:
                flat.append((w_c2, wh["c2"][:].rearrange("p c e -> p (c e)"), wl["c2"][:].rearrange("p c e -> p (c e)")))
            split_weights(nc, wctx, hold, tag, flat, CH * E)

        xf = sb("xf", [P, CH, T])
        xh, xl = sb("xh", [P, CH, T], F32R), sb("xl", [P, CH, T], F32R)
        xres = sb("xres", [P, CH, T])
        qh, ql = sb("qh", [P, CH, T], F32R), sb("ql", [P, CH, T], F32R)
        kh, kl = sb("kh", [P, CH, T], F32R), sb("kl", [P, CH, T], F32R)
        kbh = [sb(f"kbh{b}", [P, CH, 4, P], F32R) for b in range(NB)]
        kbl = [sb(f"kbl{b}", [P, CH, 4, P], F32R) for b in range(NB)]
        vf = sb("vf", [P, NB, E])
        vh, vl = sb("vh", [P, NB, H, VW], F32R), sb("vl", [P, NB, H, VW], F32R)
        shifted = sb("shifted", [P, 2, 4, P])
        top = sb("top", [P, 2, 4])
        pth, ptl = sb("pth", [P, 2, 4, P], F32R), sb("ptl", [P, 2, 4, P], F32R)
        rz = sb("rz", [P, 2, 8])
        of = sb("of", [P, NB, E])
        oth, otl = sb("oth", [P, CH, T], F32R), sb("otl", [P, CH, T], F32R)
        if L0:
            tf = sb("tf", [P, 2, 2, T])
            th, tl = sb("th", [P, CH, T], F32R), sb("tl", [P, CH, T], F32R)
            tb = sb("tb", [P, CH, NB])
            fd = sb("fd", [P, NB])
            cz, ce, cc, c8, cf = (sb(n, [P, NB * H]) for n in ("cz", "ce", "cc", "c8", "cf"))
        if L1:
            af = sb("af", [P, CH, T])
        if L1 or L2:
            sq = sb("sq", [P, CH, T])
            half = sb("half", [P, 2, T])
            quarter = sb("quarter", [P, T])
            sd, rs = sb("sd", [P, T]), sb("rs", [P, T])
            gt, bt = sb("gt", [P, CH, NB]), sb("bt", [P, CH, NB])
            eps = sb("eps", [P, 1])

        bank_a = [bank("bank_a0"), bank("bank_a1")]
        bank_s = [bank("bank_s0"), bank("bank_s1")]
        bank_t = [bank("bank_t0"), bank("bank_t1")]
        bank_o = bank("bank_o")
        bank_b = bank("bank_b")

        x_loaded, x_high, x_split, x_normed = sem("x_loaded"), sem("x_high"), sem("x_split"), sem("x_normed")
        res_loaded, res_ready, stored = sem("res_loaded"), sem("res_ready"), sem("stored")
        a_full, a_free = [sem("a_full0"), sem("a_full1")], [sem("a_free0"), sem("a_free1")]
        k_high, q_high = sem("k_high"), sem("q_high")
        kb_ready = [sem("kb_ready0"), sem("kb_ready1")]
        v_copied, v_high, v_split = sem("v_copied"), sem("v_high"), sem("v_split")
        t_high, t_split, tb_ready = sem("t_high"), sem("t_split"), sem("tb_ready")
        coh_z, coh_e, coh_step, fd_ready = sem("coh_z"), sem("coh_e"), sem("coh_step"), sem("fd_ready")
        s_full, top_ready, shift_done, exp_done = sem("s_full"), sem("top_ready"), sem("shift_done"), sem("exp_done")
        t_full, p_high, p_low = sem("t_full"), sem("p_high"), sem("p_low")
        pv_done, rz_step, o_free = sem("pv_done"), sem("rz_step"), sem("o_free")
        b_full, b_free, ot_high = sem("b_full"), sem("b_free"), sem("ot_high")
        out_full, sq_ready, sum_step = sem("out_full"), sem("sq_ready"), sem("sum_step")
        norm_step, y_ready, pool_waited, zeroed = sem("norm_step"), sem("y_ready"), sem("pool_waited"), sem("zeroed")

        fills = [("k", 0), ("k", 1), ("v", 0), ("v", 1)] + ([("c", 0), ("c", 1)] if L0 else []) + [("q", 0), ("q", 1)]
        a_per = len(fills) // 2
        if L0:
            spans = [1] * 8 + [2] * 4
        else:
            spans = [1] * 12
        pieces, at = [], 0
        for n in spans:
            pieces.append([(fills[m // 2], m % 2) for m in range(at, at + n)])
            at += n
        assert at == 2 * len(fills) and len(spans) == SLOTS

        def a_turn(p, fill):
            n = fills.index(fill)
            return n % 2, p * a_per + n // 2

        def ended(slot):
            return [fill for fill, part in pieces[slot] if part == 1]

        def b_turn(i, name):
            if L0:
                return 6 * i + ["coh", "vsum0", "ot0", "vsum1", "ot1", "out"].index(name)
            order = ["norm", "ot0", "ot1", "out"].index(name)
            if L1:
                return 4 * i - 1 + order
            return 2 + 4 * i + order - (max(0, i - (G - 3)) if isinstance(i, int) else 0)

        def o_turn(i, name):
            return 5 * i + ["pair0", "pair1", "pair2", "pair3", "out"].index(name)

        def iterate(eng, body):
            body(0)
            with eng.Fori(1, G - 2) as i:
                body(i)
            body(G - 2)
            body(G - 1)

        def has(i, ahead):
            return not isinstance(i, int) or i + ahead < G

        block = ctx.enter_context(nc.Block())

        @block.sync
        def _(sp):
            def load(n):
                need(sp, x_split, n)
                sp.dma_start(xf[:], x_in[bass.ds(n, 1)].rearrange("g p c t -> (g p) c t")).then_inc(x_loaded, 16)

            def store(n):
                if L1:
                    need(sp, res_ready, n + 1)
                else:
                    need(sp, b_free, b_turn(n, "out") + 1)
                    need(sp, o_free, o_turn(n, "out") + 1)
                sp.dma_start(x_out[bass.ds(n, 1)].rearrange("g p c t -> (g p) c t"), xres[:]).then_inc(stored, 16)

            def spread_keys(p, b):
                need(sp, s_full, UNITS * (p - 1) + 4 * (b + 1))
                for m in range(2):
                    need(sp, a_free[m], a_per * p + 1)
                for dst, src in ((kbh, kh), (kbl, kl)):
                    for h in range(4):
                        rows = slice(HD * h, HD * (h + 1))
                        sp.dma_start(f32(dst[b][rows, :, h, :]), f32(src[rows, :, b * P:(b + 1) * P])).then_inc(kb_ready[b], 16)

            load(0)
            load(1)
            sp.wait_ge(zeroed, 4)
            spread_keys(0, 0)
            spread_keys(0, 1)

            def body(i):
                if L1 and not (isinstance(i, int) and i == 0):
                    store(i - 1)
                need(sp, stored, 16 * i)
                sp.dma_start(xres[:], x_in[bass.ds(i, 1)].rearrange("g p c t -> (g p) c t")).then_inc(res_loaded, 16)
                if has(i, 2):
                    load(i + 2)
                if has(i, 1):
                    spread_keys(i + 1, 0)
                    spread_keys(i + 1, 1)
                if not L1:
                    store(i)

            iterate(sp, body)
            if L1:
                store(G - 1)
            sp.wait_ge(stored, 16 * G)

        @block.tensor
        def _(pe):
            def mm3(out, w_h, w_l, x_h, x_l, first=True, last=True):
                nc.tensor.matmul(out, w_h, x_h, start=first, stop=False)
                nc.tensor.matmul(out, w_l, x_h, start=False, stop=False)
                return nc.tensor.matmul(out, w_h, x_l, start=False, stop=last)

            def project(p, fill, part):
                kind, m = fill
                bk, n = a_turn(p, fill)
                if part == 0:
                    need(pe, a_free[bk], n)
                    if fill == fills[0]:
                        need(pe, x_split, p + 1)
                if kind == "v":
                    for c in (2 * part, 2 * part + 1):
                        mm = mm3(bank_a[bk][:], xh[:, c, m * P:(m + 1) * P], xl[:, c, m * P:(m + 1) * P], wh["v"][:, c, :], wl["v"][:, c, :],
                                 first=(c == 0), last=(c == CH - 1))
                else:
                    o = 2 * m + part
                    for c in range(CH):
                        mm = mm3(bank_a[bk][:, part * T:(part + 1) * T], wh[kind][:, c, o * P:(o + 1) * P], wl[kind][:, c, o * P:(o + 1) * P],
                                 xh[:, c, :], xl[:, c, :], first=(c == 0), last=(c == CH - 1))
                if part == 1:
                    mm.then_inc(a_full[bk], 1)

            def scores(i, u):
                b, c = divmod(u, CH)
                n = UNITS * i + u
                need(pe, shift_done, n - 1)
                if u == 0:
                    for m in range(2):
                        need(pe, a_free[m], a_per * (i + 1))
                if c == 0:
                    need(pe, kb_ready[b], KB_DONE * (i + 1))
                out = bank_s[u % 2][:]
                q_h, q_l = qh[:, c, b * P:(b + 1) * P], ql[:, c, b * P:(b + 1) * P]
                k_h, k_l = (t[b][:, c].rearrange("p h j -> p (h j)") for t in (kbh, kbl))
                mm = mm3(out, q_h, q_l, k_h, k_l, last=not L1)
                if L1:
                    mm = nc.tensor.matmul(out.rearrange("p (h j) -> p h j", h=4), k["ident_r"][:], bcast_mid(k["mask"][:], 4), start=False, stop=True)
                mm.then_inc(s_full, 1)

            def turn_probs(i, u):
                n = UNITS * i + u
                need(pe, exp_done, n + 1)
                need(pe, p_low, n - 1)
                for h in range(4):
                    mm = nc.tensor.transpose(bank_t[u % 2][:, h * P:(h + 1) * P], shifted[:, u % 2, h, :], k["ident"][:])
                mm.then_inc(t_full, 1)

            def weigh_values(i, u):
                b, c = divmod(u, CH)
                n = UNITS * i + u
                if u == 0:
                    need(pe, v_split, i + 1)
                if u % 2 == 0:
                    need(pe, o_free, o_turn(i, f"pair{u // 2}"))
                need(pe, p_low, n + 1)
                for h in range(4):
                    o = ((u % 2) * 4 + h) * VW
                    head = 4 * c + h
                    mm = mm3(bank_o[:, o:o + VW], pth[:, u % 2, h, :], ptl[:, u % 2, h, :], vh[:, b, head, :], vl[:, b, head, :])
                mm.then_inc(pv_done, 1)

            def coherence(i):
                need(pe, b_free, b_turn(i, "coh"))
                need(pe, t_split, 2 * (i + 1))
                for b in range(NB):
                    for c in range(CH):
                        mm = mm3(bank_b[:, b * H:(b + 1) * H], th[:, c, b * P:(b + 1) * P], tl[:, c, b * P:(b + 1) * P],
                                 wh["c2"][:, c, :], wl["c2"][:, c, :], first=(c == 0), last=(c == CH - 1))
                mm.then_inc(b_full, 1)

            def sum_values(i, b):
                need(pe, b_free, b_turn(i, f"vsum{b}"))
                out = bank_b[:].rearrange("p (h d) -> p h d", h=H)
                nc.tensor.matmul(out, k["ones_r"][:], vh[:, b, :, 0:HD], start=True, stop=False)
                nc.tensor.matmul(out, k["ones_r"][:], vl[:, b, :, 0:HD], start=False, stop=True).then_inc(b_full, 1)

            def turn_output(i, b):
                need(pe, b_free, b_turn(i, f"ot{b}"))
                if not L0:
                    need(pe, o_free, o_turn(i, f"pair{2 * b + 1}") + 1)
                for c in range(CH):
                    mm = nc.tensor.transpose(bank_b[:, c * P:(c + 1) * P], of[:, b, c * P:(c + 1) * P], k["ident"][:])
                mm.then_inc(b_full, 1)

            def output(i):
                for m, (bk, free, turn) in enumerate(((bank_b, b_free, b_turn(i, "out")), (bank_o, o_free, o_turn(i, "out")))):
                    need(pe, free, turn)
                    for part in range(2):
                        o = 2 * m + part
                        for c in range(CH):
                            mm = mm3(bk[:, part * T:(part + 1) * T], wh["o"][:, c, o * P:(o + 1) * P], wl["o"][:, c, o * P:(o + 1) * P],
                                     oth[:, c, :], otl[:, c, :], first=(c == 0), last=(c == CH - 1))
                    mm.then_inc(b_full if m == 0 else out_full, 1)

            def norm_sum(turn, n):
                need(pe, b_free, turn)
                need(pe, sum_step, 2 * (n + 1))
                nc.tensor.matmul(bank_b[:, 0:T], k["ones"][:], quarter[:], start=True, stop=True).then_inc(b_full, 1)

            if L2:
                norm_sum(0, 0)
                norm_sum(1, 1)
            pe.wait_ge(zeroed, 4)
            for s in range(SLOTS):
                for piece in pieces[s]:
                    project(0, *piece)

            def body(i):
                for s in range(SLOTS):
                    if s == 0 and L0:
                        coherence(i)
                    if s == 2 and L1 and not (isinstance(i, int) and i == 0):
                        norm_sum(b_turn(i, "norm"), i - 1)
                    if s == 4 and L0:
                        sum_values(i, 0)
                    if s == 5 and L2 and has(i, 2):
                        norm_sum(b_turn(i, "norm"), i + 2)
                    if s == 8 and L0:
                        sum_values(i, 1)
                    if s == 7:
                        turn_output(i, 0)
                    if s == 11:
                        turn_output(i, 1)
                    if s < UNITS:
                        scores(i, s)
                    if 1 <= s <= UNITS:
                        turn_probs(i, s - 1)
                    if has(i, 1):
                        for piece in pieces[s]:
                            project(i + 1, *piece)
                    if 2 <= s <= UNITS + 1:
                        weigh_values(i, s - 2)
                output(i)

            iterate(pe, body)
            if L1:
                norm_sum(4 * G - 1, G - 1)

        @block.scalar
        def _(act):
            def read_fill(p, fill):
                kind, m = fill
                if kind == "v":
                    return
                bk, n = a_turn(p, fill)
                need(act, a_full[bk], n + 1)
                src = bank_a[bk][:].rearrange("p (c t) -> p c t", c=2)
                if kind == "c":
                    need(act, t_split, 2 * p + m - 1)
                    if m == 0:
                        need(act, tb_ready, p + 1)
                    for c in range(2):
                        for b in range(NB):
                            last = nc.scalar.activation(tf[:, m, c, b * P:(b + 1) * P], src[:, c, b * P:(b + 1) * P], ACT.Tanh, bias=tb[:, 2 * m + c, b:b + 1])
                            if c == 1 and b == NB - 1:
                                last.then_inc(a_free[bk], 1)
                    return
                dst = (kh if kind == "k" else qh)
                if m == 0:
                    if kind == "k":
                        need(act, kb_ready[0], KB_DONE * p)
                        need(act, kb_ready[1], KB_DONE * p)
                    else:
                        need(act, s_full, UNITS * p)
                if L0:
                    bias = k["bk"] if kind == "k" else k["bq"]
                    for c in range(2):
                        last = nc.scalar.activation(dst[:, 2 * m + c, :], src[:, c, :], ACT.Identity, bias=bias[:, 2 * m + c:2 * m + c + 1])
                else:
                    last = nc.scalar.activation(dst[:, 2 * m:2 * m + 2, :], src, ACT.Copy)
                last.then_inc(k_high if kind == "k" else q_high, 1)

            def high_probs(i, u):
                n = UNITS * i + u
                need(act, t_full, n + 1)
                need(act, pv_done, n - 1)
                nc.scalar.activation(pth[:, u % 2], bank_t[u % 2][:].rearrange("p (h j) -> p h j", h=4), ACT.Copy).then_inc(p_high, 1)

            def exponentials(i, u):
                need(act, shift_done, UNITS * i + u + 1)
                nc.scalar.activation(shifted[:, u % 2], shifted[:, u % 2], ACT.Exp, scale=SCALE).then_inc(exp_done, 1)

            def high_output(i, b):
                need(act, b_full, b_turn(i, f"ot{b}") + 1)
                if b == 0:
                    need(act, out_full, i)
                nc.scalar.activation(oth[:, :, b * P:(b + 1) * P], bank_b[:].rearrange("p (c t) -> p c t", c=CH), ACT.Copy).then_inc(ot_high, 1)

            def squares(n, src):
                need(act, sum_step, 2 * n)
                nc.scalar.activation(sq[:], src[:], ACT.Square).then_inc(sq_ready, 1)

            def deviation(turn, n):
                need(act, b_full, turn + 1)
                need(act, norm_step, 2 * n)
                nc.scalar.activation(sd[:], bank_b[:, 0:T], ACT.Sqrt, bias=eps[:, 0:1], scale=1.0 / E).then_inc(b_free, 1)

            if L2:
                act.wait_ge(zeroed, 4)
                for n in range(2):
                    need(act, x_loaded, 16 * (n + 1))
                    squares(n, xf)
                    deviation(n, n)
            if L1:
                act.wait_ge(zeroed, 4)
            for s in range(SLOTS):
                for fill in ended(s):
                    read_fill(0, fill)

            def body(i):
                for s in range(SLOTS):
                    if s == 1 and L0:
                        need(act, coh_z, i + 1)
                        need(act, coh_step, 5 * i)
                        nc.scalar.activation(ce[:], cz[:], ACT.Exp, scale=-1.0).then_inc(coh_e, 1)
                    if 1 <= s <= UNITS:
                        high_probs(i, s - 1)
                    if s < UNITS:
                        exponentials(i, s)
                    if s == 2 and L1 and not (isinstance(i, int) and i == 0):
                        deviation(b_turn(i, "norm"), i - 1)
                    if s == 2 and L2 and has(i, 2):
                        need(act, x_loaded, 16 * (i + 3))
                        squares(i + 2, xf)
                    if s == 5 and L2 and has(i, 2):
                        deviation(b_turn(i, "norm"), i + 2)
                    if s == 7:
                        high_output(i, 0)
                    if s == 11:
                        high_output(i, 1)
                    if has(i, 1):
                        for fill in ended(s):
                            read_fill(i + 1, fill)
                if L1:
                    need(act, b_full, b_turn(i, "out") + 1)
                    need(act, res_ready, i)
                    nc.scalar.activation(af[:, 0:2, :], bank_b[:].rearrange("p (c t) -> p c t", c=2), ACT.Copy).then_inc(b_free, 1)
                    need(act, out_full, i + 1)
                    nc.scalar.activation(af[:, 2:4, :], bank_o[:].rearrange("p (c t) -> p c t", c=2), ACT.Copy).then_inc(o_free, 1)
                    need(act, b_free, b_turn(i, "out") + 1)
                    need(act, o_free, o_turn(i, "out") + 1)
                    squares(i, af)

            iterate(act, body)
            if L1:
                deviation(4 * G - 1, G - 1)

        @block.vector
        def _(dve):
            def read_fill(p, fill):
                kind, m = fill
                bk, n = a_turn(p, fill)
                if kind == "c":
                    return
                src = bank_a[bk][:].rearrange("p (c t) -> p c t", c=2)
                if kind == "v":
                    need(dve, a_full[bk], n + 1)
                    need(dve, v_split, p)
                    if L0:
                        nc.vector.tensor_tensor(vf[:, m, :], bank_a[bk][:], k["bv"][:], ALU.add).then_inc(a_free[bk], 1)
                    else:
                        nc.vector.tensor_copy(vf[:, m, :], bank_a[bk][:]).then_inc(a_free[bk], 1)
                    return
                high, low = (kh, kl) if kind == "k" else (qh, ql)
                need(dve, k_high if kind == "k" else q_high, 2 * p + m + 1)
                if L0:
                    bias = k["bk"] if kind == "k" else k["bq"]
                    for c in range(2):
                        o = 2 * m + c
                        last = nc.vector.scalar_tensor_tensor(out=low[:, o, :], in0=src[:, c, :], scalar=bias[:, o:o + 1], in1=f32(high[:, o, :]),
                                                              op0=ALU.add, op1=ALU.subtract)
                else:
                    last = nc.vector.tensor_tensor(low[:, 2 * m:2 * m + 2, :], src, f32(high[:, 2 * m:2 * m + 2, :]), ALU.subtract)
                last.then_inc(a_free[bk], 1)

            def shift_scores(i, u):
                n = UNITS * i + u
                src = bank_s[u % 2][:].rearrange("p (h j) -> p h j", h=4)
                need(dve, s_full, n + 1)
                nc.vector.reduce_max(top[:, u % 2, :], src, AX_X).then_inc(top_ready, 1)
                need(dve, top_ready, n + 1)
                need(dve, t_full, n - 1)
                nc.vector.tensor_tensor(shifted[:, u % 2], src, bcast_last(top[:, u % 2, :], P), ALU.subtract).then_inc(shift_done, 1)

            def low_probs(i, u):
                need(dve, p_high, UNITS * i + u + 1)
                nc.vector.tensor_tensor(ptl[:, u % 2], bank_t[u % 2][:].rearrange("p (h j) -> p h j", h=4), f32(pth[:, u % 2]), ALU.subtract).then_inc(p_low, 1)

            def normalise(i, j):
                b = j // 2
                src = bank_o[:, 0:8 * VW].rearrange("p (h d) -> p h d", h=8)
                r = rz[:, j % 2, :]
                steps = 1 if L2 else 2
                need(dve, pv_done, UNITS * i + 2 * j + 2)
                nc.vector.reciprocal(r, src[:, :, HD]).then_inc(rz_step, 1)
                need(dve, rz_step, steps * (4 * i + j) + 1)
                if L0:
                    if j == 0:
                        need(dve, coh_step, 5 * (i + 1))
                    nc.vector.tensor_tensor(r, r, cf[:, b * H + (j % 2) * 8:b * H + (j % 2) * 8 + 8], ALU.mult).then_inc(rz_step, 1)
                if L1:
                    nc.vector.tensor_scalar(r, r, k["any_key"][:, 0:1], None, ALU.mult).then_inc(rz_step, 1)
                if not L2:
                    need(dve, rz_step, steps * (4 * i + j) + 2)
                if j % 2 == 0:
                    need(dve, b_full, b_turn(i - 1, f"ot{b}") + 1 if not (isinstance(i, int) and i == 0) else 0)
                dst = of[:, b, (j % 2) * 256:(j % 2) * 256 + 256].rearrange("p (h d) -> p h d", h=8)
                nc.vector.tensor_tensor(dst, src[:, :, 0:HD], bcast_last(r, HD), ALU.mult).then_inc(o_free, 1)

            def add_field(i, b):
                need(dve, b_full, b_turn(i, f"vsum{b}") + 1)
                need(dve, fd_ready, i + 1)
                need(dve, o_free, o_turn(i, f"pair{2 * b + 1}") + 1)
                nc.vector.scalar_tensor_tensor(out=of[:, b, :], in0=bank_b[:], scalar=fd[:, b:b + 1], in1=of[:, b, :], op0=ALU.mult, op1=ALU.add).then_inc(b_free, 1)

            def low_output(i, b):
                need(dve, ot_high, NB * i + b + 1)
                part = slice(b * P, (b + 1) * P)
                nc.vector.tensor_tensor(otl[:, :, part], bank_b[:].rearrange("p (c t) -> p c t", c=CH), f32(oth[:, :, part]), ALU.subtract).then_inc(b_free, 1)

            def add_squares(n):
                need(dve, sq_ready, n + 1)
                nc.vector.tensor_tensor(half[:], sq[:, 0:2, :], sq[:, 2:4, :], ALU.add).then_inc(sum_step, 1)
                need(dve, sum_step, 2 * n + 1)
                nc.vector.tensor_tensor(quarter[:], half[:, 0, :], half[:, 1, :], ALU.add).then_inc(sum_step, 1)

            def norm(n, turn, tile, gains, biases, out_sem):
                need(dve, b_free, turn + 1)
                nc.vector.tensor_copy(gt[:], gains[:, :, bass.ds(NB * n, NB)])
                nc.vector.tensor_copy(bt[:], biases[:, :, bass.ds(NB * n, NB)])
                nc.vector.reciprocal(rs[:], sd[:]).then_inc(norm_step, 1)
                need(dve, norm_step, 2 * n + 1)
                nc.vector.tensor_tensor(tile[:], tile[:], bcast_mid(rs[:], CH), ALU.mult).then_inc(norm_step, 1)
                need(dve, norm_step, 2 * n + 2)
                for c in range(CH):
                    for b in range(NB):
                        part = tile[:, c, b * P:(b + 1) * P]
                        last = nc.vector.tensor_scalar(part, part, gt[:, c, b:b + 1], bt[:, c, b:b + 1], ALU.mult, ALU.add)
                last.then_inc(out_sem, 1)

            for t in kbh + kbl:
                nc.vector.memset(f32(t[:]), 0.0)
            nc.vector.memset(f32(vl[:]), 0.0)
            if L1 or L2:
                nc.vector.memset(eps[:], 1e-6)
            nc.vector.memset(f32(vh[:]), 1.0).then_inc(zeroed, 4)
            if L2:
                for n in range(2):
                    add_squares(n)
                    norm(n, n, xf, k["g1"], k["b1"], x_normed)
            if L0:
                nc.vector.tensor_copy(tb[:], k["tanh_bias"][:, :, 0:NB]).then_inc(tb_ready, 1)
            for s in range(SLOTS):
                for fill in ended(s):
                    read_fill(0, fill)

            def body(i):
                first = isinstance(i, int) and i == 0
                for s in range(SLOTS):
                    if s < UNITS:
                        shift_scores(i, s)
                    if 1 <= s <= UNITS:
                        low_probs(i, s - 1)
                    if s == 0 and L0:
                        need(dve, b_full, b_turn(i, "coh") + 1)
                        nc.vector.tensor_copy(fd[:], k["field"][:, bass.ds(NB * i, NB)]).then_inc(fd_ready, 1)
                        need(dve, coh_e, i)
                        nc.vector.tensor_tensor(cz[:], bank_b[:, 0:NB * H], k["bc2"][:], ALU.add).then_inc(b_free, 1)
                        need(dve, b_free, b_turn(i, "coh") + 1)
                        nc.vector.tensor_scalar_max(cz[:], cz[:], -88.0).then_inc(coh_z, 1)
                    if s == 1 and L0:
                        need(dve, coh_e, i + 1)
                        nc.vector.tensor_scalar_add(ce[:], ce[:], 1.0).then_inc(coh_step, 1)
                        need(dve, coh_step, 5 * i + 1)
                        nc.vector.reciprocal(cc[:], ce[:]).then_inc(coh_step, 1)
                        need(dve, coh_step, 5 * i + 2)
                        nc.vector.tensor_scalar_add(c8[:], cc[:], 1e-8).then_inc(coh_step, 1)
                        need(dve, coh_step, 5 * i + 3)
                        nc.vector.reciprocal(c8[:], c8[:]).then_inc(coh_step, 1)
                        need(dve, coh_step, 5 * i + 4)
                        nc.vector.scalar_tensor_tensor(out=cf[:], in0=cc[:], scalar=1.0 - FIELD, in1=c8[:], op0=ALU.mult, op1=ALU.mult).then_inc(coh_step, 1)
                    if 4 <= s <= 10 and s % 2 == 0:
                        normalise(i, s // 2 - 2)
                    if s == 6 and L0:
                        add_field(i, 0)
                    if s == 10 and L0:
                        add_field(i, 1)
                    if s == 7:
                        low_output(i, 0)
                    if s == 11:
                        low_output(i, 1)
                    if s == 0 and L1 and not first:
                        add_squares(i - 1)
                    if s == 3 and L1 and not first:
                        norm(i - 1, b_turn(i, "norm"), af, k["gain"], k["shift"], y_ready)
                    if s == 4 and L2 and has(i, 2):
                        add_squares(i + 2)
                    if s == 8 and L2 and has(i, 2):
                        norm(i + 2, b_turn(i, "norm"), xf, k["g1"], k["b1"], x_normed)
                    if has(i, 1):
                        if s == 7 and L0:
                            need(dve, a_free[1], a_per * i + 3)
                            nc.vector.tensor_copy(tb[:], k["tanh_bias"][:, :, bass.ds(NB * (i + 1), NB)]).then_inc(tb_ready, 1)
                        for fill in ended(s):
                            read_fill(i + 1, fill)
                if L1:
                    return
                need(dve, res_loaded, 16 * (i + 1))
                need(dve, b_full, b_turn(i, "out") + 1)
                for m, (bk, free) in enumerate(((bank_b, b_free), (bank_o, o_free))):
                    if m == 1:
                        need(dve, out_full, i + 1)
                    if L0:
                        for c in range(2):
                            o = 2 * m + c
                            last = nc.vector.scalar_tensor_tensor(out=xres[:, o, :], in0=bk[:, c * T:(c + 1) * T], scalar=k["bout"][:, o:o + 1],
                                                                  in1=xres[:, o, :], op0=ALU.add, op1=ALU.add)
                    else:
                        part = xres[:, 2 * m:2 * m + 2, :]
                        last = nc.vector.tensor_tensor(part, bk[:].rearrange("p (c t) -> p c t", c=2), part, ALU.add)
                    last.then_inc(free, 1)

            iterate(dve, body)
            if L1:
                add_squares(G - 1)
                norm(G - 1, 4 * G - 1, af, k["gain"], k["shift"], y_ready)

        @block.gpsimd
        def _(pool):
            def split(n, b, src, high, low, high_sem, low_sem, value):
                nc.gpsimd.tensor_copy(high, src).then_inc(high_sem, 1)
                need_pool(pool, high_sem, value, pool_waited)
                return nc.gpsimd.tensor_tensor(low, src, f32(high), ALU.subtract).then_inc(low_sem, 1)

            def split_x(n):
                need_pool(pool, x_normed if L2 else x_loaded, n + 1 if L2 else 16 * (n + 1), pool_waited)
                need_pool(pool, a_full[1], a_per * n, pool_waited)
                split(n, 0, xf[:], xh[:], xl[:], x_high, x_split, n + 1)

            def split_v(p):
                need_pool(pool, pv_done, UNITS * p, pool_waited)
                if L0 and not (isinstance(p, int) and p == 0):
                    need_pool(pool, b_full, b_turn(p - 1, "vsum1") + 1, pool_waited)
                for m in range(2):
                    need_pool(pool, a_free[m], a_per * p + 2, pool_waited)
                src = vf[:].rearrange("p b (h d) -> p b h d", h=H)
                for b in range(NB):
                    last = nc.gpsimd.tensor_copy(vh[:, b, :, 0:HD], src[:, b])
                last.then_inc(v_high, 1)
                need_pool(pool, v_high, p + 1, pool_waited)
                for b in range(NB):
                    last = nc.gpsimd.tensor_tensor(vl[:, b, :, 0:HD], src[:, b], f32(vh[:, b, :, 0:HD]), ALU.subtract)
                last.then_inc(v_split, 1)

            def split_t(p):
                for m in range(2):
                    need_pool(pool, a_free[m], a_per * p + 3, pool_waited)
                    if m == 0 and not (isinstance(p, int) and p == 0):
                        need_pool(pool, b_full, b_turn(p - 1, "coh") + 1, pool_waited)
                    split(p, m, tf[:, m], th[:, 2 * m:2 * m + 2, :], tl[:, 2 * m:2 * m + 2, :], t_high, t_split, 2 * p + m + 1)

            pool.wait_ge(zeroed, 4)
            split_x(0)
            split_v(0)
            if L0:
                split_t(0)
            split_x(1)

            def body(i):
                if L1 and not (isinstance(i, int) and i == 0):
                    add_residual(i - 1)
                if has(i, 1):
                    if L0:
                        split_t(i + 1)
                    split_v(i + 1)
                if has(i, 2):
                    split_x(i + 2)

            def add_residual(n):
                need_pool(pool, y_ready, n + 1, pool_waited)
                need_pool(pool, res_loaded, 16 * (n + 1), pool_waited)
                nc.gpsimd.tensor_tensor(xres[:], xres[:], af[:], ALU.add).then_inc(res_ready, 1)

            iterate(pool, body)
            if L1:
                add_residual(G - 1)


def gated_mlp(nc, hold, k, sweep, x_in, layer_in, partial, x_out, w_gate, w_hid, w_out):
    last_sweep = sweep == SWEEPS - 1
    HS = HC * P
    tag = f"mlp{sweep}"
    with ExitStack() as ctx:
        def sb(name, shape, dt=F32):
            return ctx.enter_context(nc.sbuf_tensor(f"{tag}_{name}", shape, dt))

        def sem(name):
            return held(nc, hold, f"{tag}_{name}")

        def bank(name):
            return ctx.enter_context(nc.psum_tensor(f"{tag}_{name}", [P, FT], F32))

        wg = [sb("wgh", [P, CH, HS], F32R), sb("wgl", [P, CH, HS], F32R)]
        wu = [sb("wuh", [P, CH, HS], F32R), sb("wul", [P, CH, HS], F32R)]
        wo = [sb("woh", [P, HC, E], F32R), sb("wol", [P, HC, E], F32R)]
        with ExitStack() as wctx:
            pieces = []
            for c in range(CH):
                for dram, tiles in ((w_gate, wg), (w_hid, wu)):
                    pieces.append((dram[:, c, sweep * HS:(sweep + 1) * HS], tiles[0][:, c, :], tiles[1][:, c, :]))
            for n in range(HC // 2):
                o = slice(2 * n, 2 * n + 2)
                pieces.append((w_out[:, sweep * HC + 2 * n:sweep * HC + 2 * n + 2, :].rearrange("p c e -> p (c e)"),
                               wo[0][:, o, :].rearrange("p c e -> p (c e)"), wo[1][:, o, :].rearrange("p c e -> p (c e)")))
            split_weights(nc, wctx, hold, tag, pieces, HS)

        xf = sb("xf", [P, CH, FT])
        hh = [sb(f"hh{n}", [P, CH, FT], F32R) for n in range(2)]
        hl = [sb(f"hl{n}", [P, CH, FT], F32R) for n in range(2)]
        res = sb("res", [P, CH, FT])
        yt = sb("yt", [P, CH, FT])
        ot = sb("ot", [P, CH, FT]) if last_sweep else yt
        res2 = res if last_sweep else sb("res2", [P, CH, FT])
        half, quarter = sb("half", [P, 2, FT]), sb("quarter", [P, FT])
        sd, rs = sb("sd", [P, FT]), sb("rs", [P, FT])
        gt, bt = sb("gt", [P, CH, FT // P]), sb("bt", [P, CH, FT // P])
        sqb = sb("sqb", [P, 2, FT])
        eps = sb("eps", [P, 1])
        sg, act_t = sb("sg", [P, 2, FT]), sb("act_t", [P, 2, FT])
        ah, al = sb("ah", [P, 2, FT], F32R), sb("al", [P, 2, FT], F32R)
        bank_g, bank_u = [bank("bank_g0"), bank("bank_g1")], [bank("bank_u0"), bank("bank_u1")]
        bank_y = [bank(f"bank_y{n}") for n in range(CH)]

        x_loaded, res_loaded, stored = sem("x_loaded"), sem("res_loaded"), sem("stored")
        res2_loaded, res_added = sem("res2_loaded"), sem("res_added")
        sq_ready, sum_step, sd_ready, norm_step, h_high, h_low = (sem(n) for n in ("sq_ready", "sum_step", "sd_ready", "norm_step", "h_high", "h_low"))
        turn_full, silu_done, prod_done, a_high, a_low, down_done = (sem(n) for n in ("turn_full", "silu_done", "prod_done", "a_high", "a_low", "down_done"))
        y_read, mix_step, eps_set, h_ready, pool_waited = sem("y_read"), sem("mix_step"), sem("eps_set"), sem("h_ready"), sem("pool_waited")

        TURNS = HC + 1
        NORM_AT = 5

        def pos(j, c):
            return c + 1 if c >= NORM_AT and has(j, 1) else c

        def turn(j, at):
            return 1 + TURNS * j + at

        def par(odd, at):
            return (1 + TURNS * odd + at) % 2

        def has(j, ahead):
            return not isinstance(j, int) or 0 <= j + ahead < FG

        def wait_bank_free(eng, j, at):
            back = at - 2
            if back < 0:
                if isinstance(j, int) and j == 0:
                    if back == -1:
                        need(eng, sd_ready, 1)
                    return
                j, back = j - 1, back + TURNS
            if has(j, 1) and back == NORM_AT:
                need(eng, sd_ready, j + 2)
            else:
                need(eng, prod_done, HC * j + (back - 1 if has(j, 1) and back > NORM_AT else back) + 1)

        def iterate(eng, body):
            body(0, 0)
            body(1, 1)
            with eng.Fori(2, FG - 2, 2) as j:
                body(j, 0)
                body(j + 1, 1)
            body(FG - 2, 0)
            body(FG - 1, 1)

        block = ctx.enter_context(nc.Block())

        @block.sync
        def _(sp):
            def move(n, dram, tile, out, done):
                for g in range(FT // T):
                    d = dram[bass.ds((FT // T) * n + g, 1)].rearrange("g p c t -> (g p) c t")
                    t = tile[:, :, g * T:(g + 1) * T]
                    sp.dma_start(d if out else t, t if out else d).then_inc(done, 16)

            move(0, x_in, xf, False, x_loaded)

            def body(j, odd):
                if has(j, 1):
                    need(sp, h_low, j + 1)
                    move(j + 1, x_in, xf, False, x_loaded)
                need(sp, y_read, CH * j)
                move(j, partial if last_sweep else x_in, res, False, res_loaded)
                if not last_sweep:
                    move(j, layer_in, res2, False, res2_loaded)
                if last_sweep:
                    if has(j, -1):
                        need(sp, mix_step, 4 * CH * j)
                        move(j - 1, x_out, ot, True, stored)
                else:
                    need(sp, y_read, CH * (j + 1))
                    move(j, partial, yt, True, stored)

            iterate(sp, body)
            if last_sweep:
                need(sp, mix_step, 4 * CH * FG)
                move(FG - 1, x_out, ot, True, stored)
            sp.wait_ge(stored, 32 * FG)

        @block.tensor
        def _(pe):
            def mm3(out, w, x_h, x_l, first, last):
                nc.tensor.matmul(out, w[0], x_h, start=first, stop=False)
                nc.tensor.matmul(out, w[1], x_h, start=False, stop=False)
                return nc.tensor.matmul(out, w[0], x_l, start=False, stop=last)

            def norm_sum(n, b):
                need(pe, sum_step, 2 * (n + 1))
                nc.tensor.matmul(bank_g[b][:], k["ones"][:], quarter[:], start=True, stop=True).then_inc(turn_full, 1)

            norm_sum(0, 0)

            def down(j, c):
                need(pe, a_low, HC * j + c + 1)
                if c == 0:
                    need(pe, y_read, CH * j)
                for o in range(CH):
                    mm = mm3(bank_y[o][:], [w[:, c, o * P:(o + 1) * P] for w in wo], ah[:, c % 2, :], al[:, c % 2, :], c == 0, c == HC - 1)
                mm.then_inc(down_done, 1)

            def body(j, odd):
                need(pe, h_low, j + 1)
                for c in range(HC):
                    if c == NORM_AT and has(j, 1):
                        wait_bank_free(pe, j, NORM_AT)
                        norm_sum(j + 1, par(odd, NORM_AT))
                    wait_bank_free(pe, j, pos(j, c))
                    b = par(odd, pos(j, c))
                    for w, bk in ((wg, bank_g[b]), (wu, bank_u[b])):
                        for e in range(CH):
                            mm = mm3(bk[:], [t[:, e, c * P:(c + 1) * P] for t in w], hh[odd][:, e, :], hl[odd][:, e, :], e == 0, e == CH - 1)
                    mm.then_inc(turn_full, 1)
                    if c > 0:
                        down(j, c - 1)
                down(j, HC - 1)

            iterate(pe, body)

        @block.scalar
        def _(act):
            def squares(n):
                need(act, x_loaded, 32 * (n + 1))
                need(act, sum_step, 2 * n)
                nc.scalar.activation(half[:], xf[:, 0:2, :], ACT.Square)
                nc.scalar.activation(sqb[:], xf[:, 2:4, :], ACT.Square).then_inc(sq_ready, 1)

            def deviation(n, b, count):
                need(act, turn_full, count)
                need(act, norm_step, 2 * n)
                nc.scalar.activation(sd[:], bank_g[b][:], ACT.Sqrt, bias=eps[:, 0:1], scale=1.0 / E).then_inc(sd_ready, 1)

            def high_h(n, odd):
                need(act, h_ready, n + 1)
                if not (isinstance(n, int) and n < 2):
                    need(act, turn_full, turn(n - 2, HC) + 1)
                nc.scalar.activation(hh[odd][:], xf[:], ACT.Copy).then_inc(h_high, 1)

            act.wait_ge(eps_set, 1)
            squares(0)
            deviation(0, 0, 1)
            high_h(0, 0)

            def body(j, odd):
                for c in range(HC):
                    if c == 0 and has(j, 1):
                        squares(j + 1)
                    if c == NORM_AT and has(j, 1):
                        deviation(j + 1, par(odd, NORM_AT), turn(j, NORM_AT) + 1)
                    n = HC * j + c
                    need(act, turn_full, turn(j, pos(j, c)) + 1)
                    need(act, prod_done, n - 1)
                    nc.scalar.activation(sg[:, c % 2, :], bank_g[par(odd, pos(j, c))][:], ACT.Silu).then_inc(silu_done, 1)
                    if c == HC - 2 and has(j, 1):
                        high_h(j + 1, 1 - odd)

            iterate(act, body)

        @block.vector
        def _(dve):
            def norm(n, odd):
                need(dve, sd_ready, n + 1)
                nc.vector.tensor_copy(gt[:], k["g2"][:, :, bass.ds((FT // P) * n, FT // P)])
                nc.vector.tensor_copy(bt[:], k["b2"][:, :, bass.ds((FT // P) * n, FT // P)])
                nc.vector.reciprocal(rs[:], sd[:]).then_inc(norm_step, 1)
                need(dve, norm_step, 2 * n + 1)
                nc.vector.tensor_tensor(xf[:], xf[:], bcast_mid(rs[:], CH), ALU.mult).then_inc(norm_step, 1)
                need(dve, norm_step, 2 * n + 2)
                for c in range(CH):
                    for b in range(FT // P):
                        part = xf[:, c, b * P:(b + 1) * P]
                        last = nc.vector.tensor_scalar(part, part, gt[:, c, b:b + 1], bt[:, c, b:b + 1], ALU.mult, ALU.add)
                last.then_inc(h_ready, 1)

            def low_h(n, odd):
                need(dve, h_high, n + 1)
                nc.vector.tensor_tensor(hl[odd][:], xf[:], f32(hh[odd][:]), ALU.subtract).then_inc(h_low, 1)

            def add_squares(n):
                need(dve, sq_ready, n + 1)
                nc.vector.tensor_tensor(half[:], half[:], sqb[:], ALU.add).then_inc(sum_step, 1)
                need(dve, sum_step, 2 * n + 1)
                nc.vector.tensor_tensor(quarter[:], half[:, 0, :], half[:, 1, :], ALU.add).then_inc(sum_step, 1)

            def mix_row(n, i):
                at = 4 * CH * n + 4 * i
                if i == 0:
                    need(dve, stored, 32 * n)
                nc.vector.tensor_scalar(ot[:, i, :], yt[:, 0, :], k["mix"][:, 4 * i:4 * i + 1], None, ALU.mult).then_inc(mix_step, 1)
                for m in range(1, 4):
                    need(dve, mix_step, at + m)
                    nc.vector.scalar_tensor_tensor(out=ot[:, i, :], in0=yt[:, m, :], scalar=k["mix"][:, 4 * i + m:4 * i + m + 1], in1=ot[:, i, :],
                                                   op0=ALU.mult, op1=ALU.add).then_inc(mix_step, 1)

            nc.vector.memset(eps[:], 1e-6).then_inc(eps_set, 1)
            add_squares(0)
            norm(0, 0)
            low_h(0, 0)

            def body(j, odd):
                for c in range(HC):
                    n = HC * j + c
                    if c == 1 and has(j, 1):
                        add_squares(j + 1)
                    need(dve, silu_done, n + 1)
                    need(dve, a_low, n - 1)
                    nc.vector.tensor_tensor(act_t[:, c % 2, :], bank_u[par(odd, pos(j, c))][:], sg[:, c % 2, :], ALU.mult).then_inc(prod_done, 1)
                    if last_sweep and c < CH and has(j, -1):
                        mix_row(j - 1, c)
                    if c == NORM_AT and has(j, 1):
                        norm(j + 1, 1 - odd)
                    if c == HC - 1 and has(j, 1):
                        low_h(j + 1, 1 - odd)
                need(dve, down_done, HC * (j + 1))
                if last_sweep:
                    need(dve, res_loaded, 32 * (j + 1))
                else:
                    need(dve, res_added, j + 1)
                if not last_sweep:
                    need(dve, stored, 32 * j)
                for o in range(CH):
                    nc.vector.tensor_tensor(yt[:, o, :], bank_y[o][:], res[:, o, :], ALU.add).then_inc(y_read, 1)
                if last_sweep:
                    need(dve, y_read, CH * (j + 1))

            iterate(dve, body)
            if last_sweep:
                for i in range(CH):
                    mix_row(FG - 1, i)

        @block.gpsimd
        def _(pool):
            def body(j, odd):
                for c in range(HC):
                    n = HC * j + c
                    if c == 4 and not last_sweep:
                        need_pool(pool, res_loaded, 32 * (j + 1), pool_waited)
                        need_pool(pool, res2_loaded, 32 * (j + 1), pool_waited)
                        nc.gpsimd.tensor_tensor(res[:], res[:], res2[:], ALU.add).then_inc(res_added, 1)
                    need_pool(pool, prod_done, n + 1, pool_waited)
                    need_pool(pool, down_done, n - 1, pool_waited)
                    nc.gpsimd.tensor_copy(ah[:, c % 2, :], act_t[:, c % 2, :]).then_inc(a_high, 1)
                    need_pool(pool, a_high, n + 1, pool_waited)
                    nc.gpsimd.tensor_tensor(al[:, c % 2, :], act_t[:, c % 2, :], f32(ah[:, c % 2, :]), ALU.subtract).then_inc(a_low, 1)

            iterate(pool, body)


def build(nc, a, out):
    scratch = [nc.dram_tensor(f"resid{n}", (G, P, CH, T), F32, kind="Internal").ap() for n in range(4)]
    with ExitStack() as ctx:
        def keep(name, shape, dt=F32):
            return ctx.enter_context(nc.sbuf_tensor("keep_" + name, shape, dt))

        k = {n: keep(n, [P, CH, B]) for n in ("tanh_bias", "gain", "shift", "g1", "b1", "g2", "b2")}
        k |= {n: keep(n, [P, CH]) for n in ("bq", "bk", "bout")}
        k["bv"] = keep("bv", [P, E])
        k["bc2"] = keep("bc2", [P, NB * H])
        k["field"] = keep("field", [P, B])
        k["mix"] = keep("mix", [P, 16])
        k["any_key"] = keep("any_key", [P, 1])
        k["ones"] = keep("ones", [P, P])
        k["ident"] = keep("ident", [P, P])
        k["ones_r"], k["ident_r"], k["mask"] = (keep(n, [P, P], F32R) for n in ("ones_r", "ident_r", "mask"))
        def phase(make, *args):
            hold = []
            make(nc, hold, k, *args)
            nc.clear_and_free_semaphores(hold)
            with nc.Block():
                pass

        phase(prepare, a)
        phase(attention, "L0", a["x"], scratch[0], {n: a["L0_" + n] for n in "kvqoc"}, a["L0_c2"])
        phase(attention, "L1", scratch[0], scratch[1], {n: a["L1_" + n] for n in "kvqo"}, None)
        phase(attention, "L2", scratch[1], scratch[2], {n: a["L2_" + n] for n in "kvqo"}, None)
        phase(gated_mlp, 0, scratch[2], scratch[1], scratch[3], None, a["gate_w"], a["hid_w"], a["out_w"])
        phase(gated_mlp, 1, scratch[2], scratch[1], scratch[3], out, a["gate_w"], a["hid_w"], a["out_w"])


def kernel(**inputs):
    import numpy as _np
    import concourse.bacc as _bacc
    from concourse import mybir as _mybir
    from concourse.bass_utils import run_bass_kernel_spmd as _run

    def cols(w):
        w = _np.asarray(w).T
        return w.reshape(w.shape[0] // P, P, w.shape[1]).transpose(1, 0, 2)

    def flat(w):
        w = cols(w)
        return w.reshape(P, -1)

    def by_chunk(v):
        return _np.asarray(v).reshape(-1, P).T

    g = {n.replace("_cond", ""): _np.asarray(v) for n, v in inputs.items()}
    arrays = {}
    arrays["x"] = g["x"].reshape(G, T, CH, P).transpose(0, 3, 2, 1)
    arrays["cond_t"] = g["cond_256"].T
    arrays["mask"] = g["mask_SxS_bk1"]
    wqkv = g["L0_Wqkv"].reshape(3, E, E)
    bqkv = g["L0_bqkv"].reshape(3, E)
    for n, w in zip("qkvoc", (wqkv[0], wqkv[1], wqkv[2], g["L0_Wout"], g["L0_Wc1"][:, 0:E])):
        arrays["L0_" + n] = flat(w)
    arrays["L0_c2"] = flat(g["L0_Wc2"])
    for layer in ("L1", "L2"):
        for n in "qkvo":
            arrays[f"{layer}_{n}"] = flat(g[f"{layer}_W{n}"])
    arrays["w_c1c"] = g["L0_Wc1"][:, E:].T
    arrays["w_e1"] = g["L0_We1"].T
    arrays["w_e2"] = cols(g["L0_We2"])
    arrays["w_c"] = g["L1_Wc"].T
    arrays["w_gb"] = _np.stack([g[f"L2_{n}w"].T for n in ("g1", "b1", "g2", "b2")], axis=1)
    inv = _np.float32(10000.0) ** _np.repeat(_np.arange(0, E, 2, dtype=_np.float32) / _np.float32(E), 2)
    code = _np.sin(_np.arange(P, dtype=_np.float32)[:, None] / inv[None, :])
    arrays["pe_t"] = cols(code.astype(_np.float32))
    arrays["eye"] = _np.eye(P, dtype=_np.float32)
    arrays["bq_c"], arrays["bk_c"], arrays["bv"] = by_chunk(bqkv[0]), by_chunk(bqkv[1]), bqkv[2]
    arrays["bout_c"] = by_chunk(g["L0_bout"])
    arrays["bc2"] = _np.concatenate([g["L0_bc2"]] * NB)
    for n, v in (("bc1", "L0_bc1"), ("be1", "L0_be1"), ("bc", "L1_bc"), ("rms", "L1_rms_scale"), ("g1b", "L2_g1b"),
                 ("b1b", "L2_b1b"), ("g2b", "L2_g2b"), ("b2b", "L2_b2b")):
        arrays[n + "_c"] = by_chunk(g[v])
    arrays["be2"], arrays["ln_g"], arrays["ln_b"] = g["L0_be2"], g["L0_ln_g"], g["L0_ln_b"]
    arrays["gate_w"], arrays["hid_w"], arrays["out_w"] = cols(g["L2_gate_w"]), cols(g["L2_hid_w"]), cols(g["L2_out_w"])
    arrays["qr_t"] = g["L3_q_right"].T
    arrays["gate_t"] = g["L3_spectral_gate"].reshape(1, P).T
    arrays = {n: _np.ascontiguousarray(v) for n, v in arrays.items()}

    nc = _bacc.Bacc("TRN2", target_bir_lowering=False, num_devices=1)
    args = {n: nc.dram_tensor("in_" + n, v.shape, _mybir.dt.from_np(v.dtype), kind="ExternalInput").ap() for n, v in arrays.items()}
    out = nc.dram_tensor("out", (G, P, CH, T), F32, kind="ExternalOutput").ap()
    build(nc, args, out)
    r = _run(nc, [{"in_" + n: v for n, v in arrays.items()}], core_ids=[0])
    y = _np.asarray(r.results[0]["out"])
    return _np.ascontiguousarray(y.transpose(0, 3, 2, 1).reshape(B, P, E))
```

```python
from contextlib import ExitStack

import numpy as np

import concourse.bass as bass
from concourse import mybir


ALU = mybir.AluOpType
ACT = mybir.ActivationFunctionType
F32 = mybir.dt.float32
F32R = mybir.dt.float32r
F16 = mybir.dt.float16
BF16 = mybir.dt.bfloat16
AX_X = mybir.AxisListType.X

P = 128
B = 32
E = 512
CH = E // P
H = 16
HD = E // H
VW = HD + 2
T = 256
NB = T // P
G = B // NB
UNITS = NB * CH
SLOTS = UNITS + 4
HID = 4 * E
FT = 512
FG = B * P // FT
SWEEPS = 2
HC = HID // P // SWEEPS
SCALE = float(HD) ** -0.5
LIFT = 14 * float(np.log(2.0))
FIELD = 0.3 * 0.7
MASKED = -1e30
KB_DONE = 2 * 4 * 16


def f32(ap):
    return ap.bitcast(F32)


def need(eng, sem, value):
    if isinstance(value, int) and value <= 0:
        return
    eng.wait_ge(sem, value)


def held(nc, hold, name):
    s = nc.alloc_semaphore(name)
    hold.append(s)
    return s


def bcast_mid(ap, n):
    return ap.unsqueeze(1).broadcast_to([ap.shape[0], n, ap.shape[1]])


def bcast_last(ap, n):
    return ap.unsqueeze(2).broadcast_to([ap.shape[0], ap.shape[1], n])


class Splitter:

    def __init__(self, nc, ctx, hold, tag, loads, stages):
        self.nc, self.loads, self.stages = nc, loads, stages
        cols = max(src.shape[1] for src, _, _ in loads)
        self.stage = [ctx.enter_context(nc.sbuf_tensor(f"{tag}_stage{n}", [P, cols], F32)) for n in range(stages)]
        self.loaded = [held(nc, hold, f"{tag}_w_loaded{n}") for n in range(stages)]
        self.high_done = held(nc, hold, f"{tag}_w_high")
        self.low_done = held(nc, hold, f"{tag}_w_low")

    def load(self, sp, n):
        src = self.loads[n][0]
        need(sp, self.low_done, n + 1 - self.stages)
        sp.dma_start(self.stage[n % self.stages][:, 0:src.shape[1]], src).then_inc(self.loaded[n % self.stages], 16)

    def high(self, act, n):
        src, high, _ = self.loads[n]
        act.wait_ge(self.loaded[n % self.stages], 16 * (n // self.stages + 1))
        self.nc.scalar.activation(high, self.stage[n % self.stages][:, 0:src.shape[1]], ACT.Copy).then_inc(self.high_done, 1)

    def low(self, dve, n):
        src, high, low = self.loads[n]
        dve.wait_ge(self.high_done, n + 1)
        self.nc.vector.tensor_tensor(low, self.stage[n % self.stages][:, 0:src.shape[1]], f32(high), ALU.subtract).then_inc(self.low_done, 1)


def flat3(t):
    return t[:].rearrange("p c e -> p (c e)")


def prepare(nc, hold, k, a, weights):
    with ExitStack() as ctx:
        def sb(name, shape, dt=F32):
            return ctx.enter_context(nc.sbuf_tensor("prep_" + name, shape, dt))

        def sem(name):
            return held(nc, hold, "prep_" + name)

        w_c1c = sb("w_c1c", [P, E])
        w_e1 = sb("w_e1", [P, E])
        w_e2 = sb("w_e2", [P, CH, E])
        w_c = sb("w_c", [P, 2 * E])
        w_gb = sb("w_gb", [P, 4, E])
        pe_t = sb("pe_t", [P, CH, P])
        col = {n: sb(n, [P, s]) for n, s in (("bc1", CH), ("be1", CH), ("bc", 2 * CH), ("rms", CH), ("g1b", CH), ("b1b", CH), ("g2b", CH), ("b2b", CH))}
        rows = {n: sb(n, [B, E]) for n in ("be2", "ln_g", "ln_b")}
        cond = sb("cond", [P, B])
        qr = sb("qr", [P, 4])
        gate = sb("gate", [P, 1])
        w_c2 = sb("w_c2", [P, CH, H])
        mask8 = sb("mask8", [P, P], mybir.dt.uint8)
        maskf = sb("maskf", [P, P])
        ones_f = sb("ones_f", [P, P])
        silu_c = sb("silu_c", [P, B])
        relu1 = sb("relu1", [P, CH, B])
        fp = sb("fp", [B, E])
        fp_t = sb("fp_t", [P, CH, B])
        sq = sb("sq", [P, E])
        s1 = sb("s1", [P, 8])
        fa = sb("fa", [B, P])
        sc1 = sb("sc1", [P, CH, B])
        lq = sb("lq", [P, 4])
        rq = sb("rq", [P, 4])
        lm = sb("lm", [P, 16])
        rm = sb("rm", [P, 16])
        tq = sb("tq", [P, 4])
        ps = [ctx.enter_context(nc.psum_tensor(f"prep_ps{n}", [P, 512], F32)) for n in range(8)]
        ws = Splitter(nc, ctx, hold, "prep", weights, 4)
        loaded = sem("loaded")
        dve_step = sem("dve_step")
        pool_step = sem("pool_step")
        act_step = sem("act_step")
        pe_step = sem("pe_step")
        block = ctx.enter_context(nc.Block())
        loads = [(w_c1c[:], a["w_c1c"]), (w_e1[:], a["w_e1"]), (w_e2[:], a["w_e2"]), (w_c[:], a["w_c"]),
                 (w_gb[:], a["w_gb"]), (pe_t[:], a["pe_t"]), (cond[:], a["cond_t"]), (qr[:], a["qr_t"]),
                 (gate[:], a["gate_t"]), (w_c2[:], a["L0_c2"]), (mask8[:], a["mask"]), (k["bq"][:], a["bq_c"]), (k["bk"][:], a["bk_c"]),
                 (k["bout"][:], a["bout_c"]), (k["bv"][:], a["bv"].partition_broadcast(P)),
                 (k["bc2"][:], a["bc2"].partition_broadcast(P)), (k["ident"][:], a["eye"])]
        loads += [(col[n][:], a[n + "_c"]) for n in col]
        loads += [(rows[n][:], a[n].partition_broadcast(B)) for n in rows]

        @block.sync
        def _(sp):
            for dst, src in loads:
                sp.dma_start(dst, src).then_inc(loaded, 16)
            for n in range(len(weights)):
                ws.load(sp, n)

        @block.gpsimd
        def _(pool):
            for t in k["kbh"] + k["kbl"]:
                nc.gpsimd.memset(f32(t[:]), 0.0)
            for t in (k["v1"], k["v2"], k["v3"]):
                nc.gpsimd.memset(t[:], 1.0 if t is k["v1"] else 0.0)

        @block.tensor
        def _(pe):
            pe.wait_ge(loaded, 16 * len(loads))
            for c in range(CH):
                nc.tensor.matmul(ps[0][:, c * B:(c + 1) * B], w_c1c[:, c * P:(c + 1) * P], cond[:], start=True, stop=True)
            for c in range(CH):
                mm = nc.tensor.matmul(ps[1][:, c * B:(c + 1) * B], w_e1[:, c * P:(c + 1) * P], cond[:], start=True, stop=True)
            mm.then_inc(pe_step, 1)
            for n in range(4):
                for c in range(CH):
                    mm = nc.tensor.matmul(ps[2][:, (n * CH + c) * B:(n * CH + c + 1) * B], w_gb[:, n, c * P:(c + 1) * P], cond[:], start=True, stop=True)
            mm.then_inc(pe_step, 1)
            pe.wait_ge(act_step, 2)
            pe.wait_ge(dve_step, 3)
            for c in range(2 * CH):
                mm = nc.tensor.matmul(ps[3][:, c * B:(c + 1) * B], w_c[:, c * P:(c + 1) * P], silu_c[:], start=True, stop=True)
            mm.then_inc(pe_step, 1)
            for c in range(CH):
                mm = nc.tensor.matmul(ps[4][0:B, :], relu1[:, c, :], w_e2[:, c, :], start=(c == 0), stop=(c == CH - 1))
            mm.then_inc(pe_step, 1)
            pe.wait_ge(dve_step, 13)
            for c in range(CH):
                mm = nc.tensor.transpose(ps[5][:, c * B:(c + 1) * B], fp[:, c * P:(c + 1) * P], k["ident"][0:B, 0:B])
            mm.then_inc(pe_step, 1)
            pe.wait_ge(dve_step, 14)
            for c in range(CH):
                mm = nc.tensor.matmul(ps[6][0:B, 0:P], fp_t[:, c, :], pe_t[:, c, :], start=(c == 0), stop=(c == CH - 1))
            mm.then_inc(pe_step, 1)
            pe.wait_ge(dve_step, 18)
            nc.tensor.transpose(ps[7][:, 0:B], fa[:], k["ident"][0:B, 0:B]).then_inc(pe_step, 1)

        @block.scalar
        def _(act):
            act.wait_ge(loaded, 16 * len(loads))
            nc.scalar.activation(silu_c[:], cond[:], ACT.Exp, scale=-1.0).then_inc(act_step, 1)
            act.wait_ge(pe_step, 1)
            for c in range(CH):
                last = nc.scalar.activation(relu1[:, c, :], ps[1][:, c * B:(c + 1) * B], ACT.Relu, bias=col["be1"][:, c:c + 1])
            last.then_inc(act_step, 1)
            ws.high(act, 0)
            ws.high(act, 1)
            act.wait_ge(dve_step, 10)
            nc.scalar.activation(s1[0:B, 2:3], s1[0:B, 1:2], ACT.Sqrt).then_inc(act_step, 1)
            ws.high(act, 2)
            act.wait_ge(dve_step, 16)
            nc.scalar.activation(fa[:], fa[:], ACT.Exp, accum_out=s1[0:B, 5:6]).then_inc(act_step, 1)
            act.wait_ge(dve_step, 20)
            nc.scalar.activation(s1[:, 6:8], s1[:, 6:8], ACT.Sqrt).then_inc(act_step, 1)
            for n in range(3, len(weights)):
                ws.high(act, n)

        @block.vector
        def _(dve):
            count = [0]

            def done(ins):
                count[0] += 1
                ins.then_inc(dve_step, 1)
                dve.wait_ge(dve_step, count[0])

            dve.wait_ge(loaded, 16 * len(loads))
            dve.wait_ge(act_step, 1)
            done(nc.vector.tensor_scalar_add(silu_c[:], silu_c[:], 1.0))
            done(nc.vector.reciprocal(silu_c[:], silu_c[:]))
            done(nc.vector.tensor_tensor(silu_c[:], silu_c[:], cond[:], ALU.mult))
            dve.wait_ge(pe_step, 2)
            for c in range(CH):
                nc.vector.tensor_scalar_add(k["tanh_bias"][:, c, :], ps[0][:, c * B:(c + 1) * B], col["bc1"][:, c:c + 1])
            for n, (name, bias) in enumerate((("g1", "g1b"), ("b1", "b1b"), ("g2", "g2b"), ("b2", "b2b"))):
                for c in range(CH):
                    o = (n * CH + c) * B
                    last = nc.vector.tensor_scalar_add(k[name][:, c, :], ps[2][:, o:o + B], col[bias][:, c:c + 1])
            done(last)
            dve.wait_ge(pe_step, 3)
            for c in range(CH):
                nc.vector.tensor_scalar_add(k["shift"][:, c, :], ps[3][:, c * B:(c + 1) * B], col["bc"][:, c:c + 1])
            for c in range(CH):
                o = (CH + c) * B
                last = nc.vector.tensor_scalar(sc1[:, c, :], ps[3][:, o:o + B], col["bc"][:, CH + c:CH + c + 1], 1.0, ALU.add, ALU.add)
            done(last)
            for c in range(CH):
                last = nc.vector.tensor_scalar(k["gain"][:, c, :], sc1[:, c, :], col["rms"][:, c:c + 1], None, ALU.mult)
            done(last)
            ws.low(dve, 0)
            dve.wait_ge(pe_step, 4)
            done(nc.vector.tensor_tensor(fp[:], ps[4][0:B, :], rows["be2"][:], ALU.add))
            done(nc.vector.tensor_reduce(s1[0:B, 0:1], fp[:], AX_X, ALU.add))
            nc.vector.tensor_scalar(s1[0:B, 0:1], s1[0:B, 0:1], -1.0 / E, None, ALU.mult).then_inc(pool_step, 1)
            dve.wait_ge(pool_step, 1)
            nc.vector.tensor_scalar(fp[:], fp[:], s1[0:B, 0:1], None, ALU.add).then_inc(pool_step, 1)
            dve.wait_ge(pool_step, 2)
            nc.vector.tensor_tensor(sq[0:B, :], fp[:], fp[:], ALU.mult).then_inc(pool_step, 1)
            dve.wait_ge(pool_step, 3)
            done(nc.vector.tensor_reduce(s1[0:B, 1:2], sq[0:B, :], AX_X, ALU.add))
            done(nc.vector.tensor_scalar(s1[0:B, 1:2], s1[0:B, 1:2], 1.0 / E, 1e-5, ALU.mult, ALU.add))
            dve.wait_ge(act_step, 3)
            done(nc.vector.reciprocal(s1[0:B, 3:4], s1[0:B, 2:3]))
            done(nc.vector.scalar_tensor_tensor(out=fp[:], in0=fp[:], scalar=s1[0:B, 3:4], in1=rows["ln_g"][:], op0=ALU.mult, op1=ALU.mult))
            done(nc.vector.tensor_tensor(fp[:], fp[:], rows["ln_b"][:], ALU.add))
            ws.low(dve, 1)
            dve.wait_ge(pe_step, 5)
            done(nc.vector.tensor_copy(fp_t[:], ps[5][:, 0:CH * B].rearrange("p (c b) -> p c b", c=CH)))
            dve.wait_ge(pe_step, 6)
            done(nc.vector.reduce_max(s1[0:B, 4:5], ps[6][0:B, 0:P], AX_X))
            done(nc.vector.tensor_scalar(fa[:], ps[6][0:B, 0:P], s1[0:B, 4:5], None, ALU.subtract))
            dve.wait_ge(act_step, 4)
            done(nc.vector.reciprocal(s1[0:B, 4:5], s1[0:B, 5:6]))
            done(nc.vector.tensor_scalar(fa[:], fa[:], s1[0:B, 4:5], FIELD, ALU.mult, ALU.mult))
            ws.low(dve, 2)
            dve.wait_ge(pe_step, 7)
            nc.vector.tensor_copy(k["field"][:], ps[7][:, 0:B])
            nc.vector.tensor_tensor(sq[:, 0:B], cond[:], cond[:], ALU.mult)
            done(nc.vector.tensor_tensor(sq[:, B:B + 4], qr[:], qr[:], ALU.mult))
            nc.vector.tensor_reduce(s1[:, 6:7], sq[:, 0:B], AX_X, ALU.add)
            nc.vector.tensor_reduce(s1[:, 7:8], sq[:, B:B + 4], AX_X, ALU.add).then_inc(pool_step, 1)
            dve.wait_ge(pool_step, 4)
            done(nc.vector.tensor_scalar_add(s1[:, 6:8], s1[:, 6:8], 1e-8))
            dve.wait_ge(act_step, 5)
            done(nc.vector.reciprocal(s1[:, 6:8], s1[:, 6:8]))
            nc.vector.tensor_scalar(lq[:], cond[:, 0:4], s1[:, 6:7], None, ALU.mult)
            done(nc.vector.tensor_scalar(rq[:], qr[:], s1[:, 7:8], gate[:, 0:1], ALU.mult, ALU.mult))
            sl = [[1, -1, -1, -1], [1, 1, -1, 1], [1, 1, 1, -1], [1, -1, 1, 1]]
            il = [[0, 1, 2, 3], [1, 0, 3, 2], [2, 3, 0, 1], [3, 2, 1, 0]]
            sr = [[1, 1, 1, 1], [-1, 1, -1, 1], [-1, 1, 1, -1], [-1, -1, 1, 1]]
            for i in range(4):
                for j in range(4):
                    nc.vector.tensor_scalar(lm[:, 4 * i + j:4 * i + j + 1], lq[:, il[i][j]:il[i][j] + 1], float(sl[i][j]), None, ALU.mult)
                    last = nc.vector.tensor_scalar(rm[:, 4 * i + j:4 * i + j + 1], rq[:, il[i][j]:il[i][j] + 1], float(sr[i][j]), None, ALU.mult)
            done(last)
            for i in range(4):
                done(nc.vector.tensor_scalar(k["mix"][:, 4 * i:4 * i + 4], rm[:, 0:4], lm[:, 4 * i:4 * i + 1], None, ALU.mult))
                for m in range(1, 4):
                    done(nc.vector.scalar_tensor_tensor(out=k["mix"][:, 4 * i:4 * i + 4], in0=rm[:, 4 * m:4 * m + 4], scalar=lm[:, 4 * i + m:4 * i + m + 1],
                                                        in1=k["mix"][:, 4 * i:4 * i + 4], op0=ALU.mult, op1=ALU.add))
                done(nc.vector.tensor_scalar_add(k["mix"][:, 5 * i:5 * i + 1], k["mix"][:, 5 * i:5 * i + 1], 1.0))
            done(nc.vector.tensor_copy(maskf[:], mask8[:]))
            nc.vector.tensor_scalar(k["mask"][:], maskf[:], MASKED, None, ALU.mult)
            done(nc.vector.tensor_reduce(tq[:, 0:1], maskf[:], AX_X, ALU.add))
            done(nc.vector.tensor_scalar(tq[:, 0:1], tq[:, 0:1], -1.0, float(P), ALU.mult, ALU.add))
            done(nc.vector.tensor_scalar_min(tq[:, 0:1], tq[:, 0:1], 1.0))
            done(nc.vector.reciprocal(tq[:, 1:2], tq[:, 0:1]))
            nc.vector.tensor_tensor(k["any_key"][:], tq[:, 0:1], tq[:, 1:2], ALU.mult)
            nc.vector.memset(k["ones"][:], 1.0)
            nc.vector.memset(ones_f[:], 1.0).then_inc(pool_step, 1)
            dve.wait_ge(pool_step, 5)
            nc.vector.tensor_copy(k["ones_b"][:], ones_f[:])
            nc.vector.memset(k["lift"][:], LIFT)
            done(nc.vector.tensor_copy(k["ident_r"][:], k["ident"][:]))
            done(nc.vector.tensor_copy(k["wc2"][:, :, 0:H], w_c2[:]))
            done(nc.vector.tensor_tensor(k["wc2"][:, :, H:2 * H], w_c2[:], f32(k["wc2"][:, :, 0:H]), ALU.subtract))
            for n in range(3, len(weights)):
                ws.low(dve, n)


def attention(nc, hold, k, tag, x_in, x_out, wh, wl, weights):
    L0, L1, L2 = (tag == t for t in ("L0", "L1", "L2"))
    with ExitStack() as ctx:
        def sb(name, shape, dt=F32):
            return ctx.enter_context(nc.sbuf_tensor(f"{tag}_{name}", shape, dt))

        def sem(name):
            return held(nc, hold, f"{tag}_{name}")

        def bank(name):
            return ctx.enter_context(nc.psum_tensor(f"{tag}_{name}", [P, 512], F32))

        order = [n for n in "kvqo" if n in weights]
        ws = None if L0 else Splitter(nc, ctx, hold, tag, [(weights[n], flat3(wh[n]), flat3(wl[n])) for n in order], 2)

        xf = sb("xf", [P, CH, T])
        xh, xl = sb("xh", [P, CH, T], F32R), sb("xl", [P, CH, T], F32R)
        xres = sb("xres", [P, CH, T])
        qh, ql = sb("qh", [P, CH, T], F32R), sb("ql", [P, CH, T], F32R)
        kh, kl = sb("kh", [P, CH, T], F32R), sb("kl", [P, CH, T], F32R)
        kbh, kbl = k["kbh"], k["kbl"]
        v1, v2, v3 = k["v1"], k["v2"], k["v3"]
        vf = sb("vf", [P, NB, E])
        vr = sb("vr", [P, NB, E])
        shifted = sb("shifted", [P, 2, 4, P])
        top = sb("top", [P, 2, 4])
        pth, ptl = sb("pth", [P, 2, 4, P], F16), sb("ptl", [P, 2, 4, P], F16)
        rz = sb("rz", [P, 2, 8])
        of = sb("of", [P, NB, E])
        oth, otl = sb("oth", [P, CH, T], F32R), sb("otl", [P, CH, T], F32R)
        if L0:
            tf = sb("tf", [P, 2, 2, T])
            th, tl = sb("th", [P, CH, T], F32R), sb("tl", [P, CH, T], F32R)
            tb = sb("tb", [P, CH, NB])
            fd = sb("fd", [P, NB])
            cz, ce, cc, c8, cf = (sb(n, [P, NB * H]) for n in ("cz", "ce", "cc", "c8", "cf"))
        if L1:
            af = sb("af", [P, CH, T])
        if L1 or L2:
            sq = sb("sq", [P, CH, T])
            half = sb("half", [P, 2, T])
            quarter = sb("quarter", [P, T])
            sd, rs = sb("sd", [P, T]), sb("rs", [P, T])
            gt, bt = sb("gt", [P, CH, NB]), sb("bt", [P, CH, NB])
            eps = sb("eps", [P, 1])

        bank_a = [bank("bank_a0"), bank("bank_a1")]
        bank_s = [bank("bank_s0"), bank("bank_s1")]
        bank_t = [bank("bank_t0"), bank("bank_t1")]
        bank_o = bank("bank_o")
        bank_b = bank("bank_b")

        x_loaded, x_high, x_split, x_normed = sem("x_loaded"), sem("x_high"), sem("x_split"), sem("x_normed")
        res_loaded, res_ready, stored = sem("res_loaded"), sem("res_ready"), sem("stored")
        a_full, a_free = [sem("a_full0"), sem("a_full1")], [sem("a_free0"), sem("a_free1")]
        k_high, q_high = sem("k_high"), sem("q_high")
        kb_ready = [sem("kb_ready0"), sem("kb_ready1")]
        v_first, v_rest, v_second, v_split = sem("v_first"), sem("v_rest"), sem("v_second"), sem("v_split")
        t_high, t_split, tb_ready = sem("t_high"), sem("t_split"), sem("tb_ready")
        coh_sum, coh_z, coh_e, coh_step, fd_ready = sem("coh_sum"), sem("coh_z"), sem("coh_e"), sem("coh_step"), sem("fd_ready")
        s_full, top_ready, shift_done, exp_done = sem("s_full"), sem("top_ready"), sem("shift_done"), sem("exp_done")
        t_full, p_high, p_low = sem("t_full"), sem("p_high"), sem("p_low")
        pv_done, rz_step, o_free = sem("pv_done"), sem("rz_step"), sem("o_free")
        b_full, b_free, ot_high = sem("b_full"), sem("b_free"), sem("ot_high")
        out_full, sq_ready, sum_step = sem("out_full"), sem("sq_ready"), sem("sum_step")
        norm_step, eps_set, y_ready = sem("norm_step"), sem("eps_set"), sem("y_ready")

        fills = [("k", 0), ("k", 1), ("v", 0), ("v", 1)] + ([("c", 0), ("c", 1)] if L0 else []) + [("q", 0), ("q", 1)]
        a_per = len(fills) // 2
        if L0:
            spans = [1] * 8 + [2] * 4
        else:
            spans = [1] * 12
        pieces, at = [], 0
        for n in spans:
            pieces.append([(fills[m // 2], m % 2) for m in range(at, at + n)])
            at += n
        assert at == 2 * len(fills) and len(spans) == SLOTS

        def a_turn(p, fill):
            n = fills.index(fill)
            return n % 2, p * a_per + n // 2

        def ended(slot):
            return [fill for fill, part in pieces[slot] if part == 1]

        def b_turn(i, name):
            if L0:
                return 6 * i + ["coh", "vsum0", "ot0", "vsum1", "ot1", "out"].index(name)
            order = ["ot0", "norm", "ot1", "out"].index(name)
            if L1:
                return 4 * i - (1 if order or not isinstance(i, int) or i else 0) + order
            missing = 0
            if isinstance(i, int) and i >= G - 2:
                missing = i - (G - 2) + (1 if order else 0)
            return 2 + 4 * i + order - missing

        def o_turn(i, name):
            return 5 * i + ["pair0", "pair1", "pair2", "pair3", "out"].index(name)

        def iterate(eng, body):
            body(0)
            with eng.Fori(1, G - 2) as i:
                body(i)
            body(G - 2)
            body(G - 1)

        def has(i, ahead):
            return not isinstance(i, int) or i + ahead < G

        block = ctx.enter_context(nc.Block())

        @block.sync
        def _(sp):
            def load(n):
                need(sp, x_split, n)
                sp.dma_start(xf[:], x_in[bass.ds(n, 1)].rearrange("g p c t -> (g p) c t")).then_inc(x_loaded, 16)

            def store(n):
                if L1:
                    need(sp, res_ready, n + 1)
                else:
                    need(sp, b_free, b_turn(n, "out") + 1)
                    need(sp, o_free, o_turn(n, "out") + 1)
                sp.dma_start(x_out[bass.ds(n, 1)].rearrange("g p c t -> (g p) c t"), xres[:]).then_inc(stored, 16)

            def spread_keys(p, b):
                need(sp, s_full, UNITS * (p - 1) + 4 * (b + 1))
                for m in range(2):
                    need(sp, a_free[m], a_per * p + 1)
                for dst, src in ((kbh, kh), (kbl, kl)):
                    for h in range(4):
                        rows = slice(HD * h, HD * (h + 1))
                        sp.dma_start(f32(dst[b][rows, :, h, :]), f32(src[rows, :, b * P:(b + 1) * P])).then_inc(kb_ready[b], 16)

            load(0)
            if not L0:
                for n in range(2):
                    ws.load(sp, n)
            load(1)
            if not L0:
                for n in range(2, len(order)):
                    ws.load(sp, n)
            spread_keys(0, 0)
            spread_keys(0, 1)

            def load_residual(i):
                need(sp, stored, 16 * i)
                sp.dma_start(xres[:], x_in[bass.ds(i, 1)].rearrange("g p c t -> (g p) c t")).then_inc(res_loaded, 16)

            def body(i):
                if not L1:
                    load_residual(i)
                if has(i, 2):
                    load(i + 2)
                if has(i, 1):
                    spread_keys(i + 1, 0)
                    spread_keys(i + 1, 1)
                if not L1:
                    store(i)
                elif isinstance(i, int) and i == 0:
                    load_residual(0)
                else:
                    store(i - 1)
                    load_residual(i)

            iterate(sp, body)
            if L1:
                store(G - 1)
            sp.wait_ge(stored, 16 * G)

        @block.tensor
        def _(pe):
            def mm3(out, w_h, w_l, x_h, x_l, first=True, last=True):
                nc.tensor.matmul(out, w_h, x_h, start=first, stop=False)
                nc.tensor.matmul(out, w_l, x_h, start=False, stop=False)
                return nc.tensor.matmul(out, w_h, x_l, start=False, stop=last)

            def project(p, fill, part):
                kind, m = fill
                bk, n = a_turn(p, fill)
                if part == 0:
                    need(pe, a_free[bk], n)
                    if isinstance(p, int) and p == 0 and not L0:
                        need(pe, ws.low_done, order.index(kind) + 1)
                    if fill == fills[0]:
                        need(pe, x_split, p + 1)
                if kind == "v":
                    for c in (2 * part, 2 * part + 1):
                        mm = mm3(bank_a[bk][:], xh[:, c, m * P:(m + 1) * P], xl[:, c, m * P:(m + 1) * P], wh["v"][:, c, :], wl["v"][:, c, :],
                                 first=(c == 0), last=(c == CH - 1))
                else:
                    o = 2 * m + part
                    for c in range(CH):
                        mm = mm3(bank_a[bk][:, part * T:(part + 1) * T], wh[kind][:, c, o * P:(o + 1) * P], wl[kind][:, c, o * P:(o + 1) * P],
                                 xh[:, c, :], xl[:, c, :], first=(c == 0), last=(c == CH - 1))
                if part == 1:
                    mm.then_inc(a_full[bk], 1)

            def scores(i, u):
                b, c = divmod(u, CH)
                n = UNITS * i + u
                need(pe, shift_done, n - 1)
                if u == 0:
                    for m in range(2):
                        need(pe, a_free[m], a_per * (i + 1))
                if c == 0:
                    need(pe, kb_ready[b], KB_DONE * (i + 1))
                out = bank_s[u % 2][:]
                q_h, q_l = qh[:, c, b * P:(b + 1) * P], ql[:, c, b * P:(b + 1) * P]
                k_h, k_l = (t[b][:, c].rearrange("p h j -> p (h j)") for t in (kbh, kbl))
                mm = mm3(out, q_h, q_l, k_h, k_l, last=not L1)
                if L1:
                    mm = nc.tensor.matmul(out.rearrange("p (h j) -> p h j", h=4), k["ident_r"][:], bcast_mid(k["mask"][:], 4), start=False, stop=True)
                mm.then_inc(s_full, 1)

            def turn_probs(i, u):
                n = UNITS * i + u
                need(pe, exp_done, n + 1)
                need(pe, p_low, n - 1)
                for h in range(4):
                    mm = nc.tensor.transpose(bank_t[u % 2][:, h * P:(h + 1) * P], shifted[:, u % 2, h, :], k["ident"][:])
                mm.then_inc(t_full, 1)

            def weigh_values(i, u):
                b, c = divmod(u, CH)
                n = UNITS * i + u
                if u == 0:
                    need(pe, v_split, i + 1)
                if u % 2 == 0:
                    need(pe, o_free, o_turn(i, f"pair{u // 2}"))
                need(pe, p_low, n + 1)
                for h in range(4):
                    o = ((u % 2) * 4 + h) * VW
                    passes = [(p, v) for p, parts in ((pth, (v1, v2, v3)), (ptl, (v1, v2))) for v in parts]
                    for n, (p, v) in enumerate(passes):
                        mm = nc.tensor.matmul(bank_o[:, o:o + VW], p[:, u % 2, h, :], v[:, b, 4 * c + h, :], start=(n == 0), stop=(n == len(passes) - 1))
                mm.then_inc(pv_done, 1)

            def coherence(i):
                need(pe, b_free, b_turn(i, "coh"))
                need(pe, t_split, 2 * (i + 1))
                for b in range(NB):
                    both = bank_b[:, 2 * b * H:2 * (b + 1) * H]
                    for c in range(CH):
                        nc.tensor.matmul(both, th[:, c, b * P:(b + 1) * P], k["wc2"][:, c, :], start=(c == 0), stop=(c == CH - 1), skip_group_check=True)
                    for c in range(CH):
                        mm = nc.tensor.matmul(both[:, 0:H], tl[:, c, b * P:(b + 1) * P], k["wc2"][:, c, 0:H], start=False, stop=(c == CH - 1), skip_group_check=True)
                mm.then_inc(b_full, 1)

            def sum_values(i, b):
                need(pe, b_free, b_turn(i, f"vsum{b}"))
                out = bank_b[:].rearrange("p (h d) -> p h d", h=H)
                for n, v in enumerate((v1, v2, v3)):
                    mm = nc.tensor.matmul(out, k["ones_b"][:], v[:, b, :, 0:HD], start=(n == 0), stop=(n == 2))
                mm.then_inc(b_full, 1)

            def turn_output(i, b):
                need(pe, b_free, b_turn(i, f"ot{b}"))
                if not L0:
                    need(pe, o_free, o_turn(i, f"pair{2 * b + 1}") + 1)
                for c in range(CH):
                    mm = nc.tensor.transpose(bank_b[:, c * P:(c + 1) * P], of[:, b, c * P:(c + 1) * P], k["ident"][:])
                mm.then_inc(b_full, 1)

            def output(i):
                if isinstance(i, int) and i == 0 and not L0:
                    need(pe, ws.low_done, len(order))
                for m, (bk, free, turn) in enumerate(((bank_b, b_free, b_turn(i, "out")), (bank_o, o_free, o_turn(i, "out")))):
                    need(pe, free, turn)
                    for part in range(2):
                        o = 2 * m + part
                        for c in range(CH):
                            mm = mm3(bk[:, part * T:(part + 1) * T], wh["o"][:, c, o * P:(o + 1) * P], wl["o"][:, c, o * P:(o + 1) * P],
                                     oth[:, c, :], otl[:, c, :], first=(c == 0), last=(c == CH - 1))
                    mm.then_inc(b_full if m == 0 else out_full, 1)

            def norm_sum(turn, n):
                need(pe, b_free, turn)
                need(pe, sum_step, 2 * (n + 1))
                nc.tensor.matmul(bank_b[:, 0:T], k["ones"][:], quarter[:], start=True, stop=True).then_inc(b_full, 1)

            if L2:
                norm_sum(0, 0)
                norm_sum(1, 1)
            for s in range(SLOTS):
                for piece in pieces[s]:
                    project(0, *piece)

            def body(i):
                for s in range(SLOTS):
                    if s == 0 and L0:
                        coherence(i)
                    if s == 8 and L1 and not (isinstance(i, int) and i == 0):
                        norm_sum(b_turn(i, "norm"), i - 1)
                    if s == 4 and L0:
                        sum_values(i, 0)
                    if s == 9 and L2 and has(i, 2):
                        norm_sum(b_turn(i, "norm"), i + 2)
                    if s == 8 and L0:
                        sum_values(i, 1)
                    if s == 7:
                        turn_output(i, 0)
                    if s == 11:
                        turn_output(i, 1)
                    if s < UNITS:
                        scores(i, s)
                    if 1 <= s <= UNITS:
                        turn_probs(i, s - 1)
                    if has(i, 1):
                        for piece in pieces[s]:
                            project(i + 1, *piece)
                    if 2 <= s <= UNITS + 1:
                        weigh_values(i, s - 2)
                output(i)

            iterate(pe, body)
            if L1:
                norm_sum(4 * G - 1, G - 1)

        @block.scalar
        def _(act):
            def read_fill(p, fill):
                kind, m = fill
                bk, n = a_turn(p, fill)
                if kind == "v" and L0:
                    return
                need(act, a_full[bk], n + 1)
                if kind == "v":
                    need(act, v_split, p)
                    nc.scalar.activation(vf[:, m, :], bank_a[bk][:], ACT.Copy).then_inc(a_free[bk], 1)
                    return
                src = bank_a[bk][:].rearrange("p (c t) -> p c t", c=2)
                if kind == "c":
                    need(act, t_split, 2 * p + m - 1)
                    if m == 0:
                        need(act, tb_ready, p + 1)
                    for c in range(2):
                        for b in range(NB):
                            last = nc.scalar.activation(tf[:, m, c, b * P:(b + 1) * P], src[:, c, b * P:(b + 1) * P], ACT.Tanh, bias=tb[:, 2 * m + c, b:b + 1])
                            if c == 1 and b == NB - 1:
                                last.then_inc(a_free[bk], 1)
                    if m == 0 and not (isinstance(p, int) and p == 0):
                        need(act, b_full, b_turn(p - 1, "coh") + 1)
                    need(act, a_free[bk], n + 1)
                    nc.scalar.activation(th[:, 2 * m:2 * m + 2, :], tf[:, m], ACT.Copy).then_inc(t_high, 1)
                    return
                dst = (kh if kind == "k" else qh)
                if m == 0:
                    if kind == "k":
                        need(act, kb_ready[0], KB_DONE * p)
                        need(act, kb_ready[1], KB_DONE * p)
                    else:
                        need(act, s_full, UNITS * p)
                if L0:
                    bias = k["bk"] if kind == "k" else k["bq"]
                    for c in range(2):
                        last = nc.scalar.activation(dst[:, 2 * m + c, :], src[:, c, :], ACT.Identity, bias=bias[:, 2 * m + c:2 * m + c + 1])
                else:
                    last = nc.scalar.activation(dst[:, 2 * m:2 * m + 2, :], src, ACT.Copy)
                last.then_inc(k_high if kind == "k" else q_high, 1)

            def high_probs(i, u):
                n = UNITS * i + u
                need(act, t_full, n + 1)
                need(act, pv_done, n - 1)
                nc.scalar.activation(pth[:, u % 2], bank_t[u % 2][:].rearrange("p (h j) -> p h j", h=4), ACT.Copy).then_inc(p_high, 1)

            def exponentials(i, u):
                need(act, shift_done, UNITS * i + u + 1)
                nc.scalar.activation(shifted[:, u % 2], shifted[:, u % 2], ACT.Exp, bias=k["lift"][:, 0:1], scale=SCALE).then_inc(exp_done, 1)

            def high_output(i, b):
                need(act, b_full, b_turn(i, f"ot{b}") + 1)
                if b == 0:
                    need(act, out_full, i)
                nc.scalar.activation(oth[:, :, b * P:(b + 1) * P], bank_b[:].rearrange("p (c t) -> p c t", c=CH), ACT.Copy).then_inc(ot_high, 1)

            if not L0:
                act.wait_ge(eps_set, 1)

            def squares(n, src):
                need(act, sum_step, 2 * n)
                nc.scalar.activation(sq[:], src[:], ACT.Square).then_inc(sq_ready, 1)

            def deviation(turn, n):
                need(act, b_full, turn + 1)
                need(act, norm_step, 2 * n)
                nc.scalar.activation(sd[:], bank_b[:, 0:T], ACT.Sqrt, bias=eps[:, 0:1], scale=1.0 / E).then_inc(b_free, 1)

            def first_values(p):
                need(act, pv_done, UNITS * p)
                if L0 and not (isinstance(p, int) and p == 0):
                    need(act, b_full, b_turn(p - 1, "vsum1") + 1)
                for m in range(2):
                    need(act, a_free[m], a_per * p + 2)
                nc.scalar.activation(v1[:, :, :, 0:HD], vf[:].rearrange("p b (h d) -> p b h d", h=H), ACT.Copy).then_inc(v_first, 1)

            def second_values(p):
                need(act, v_rest, p + 1)
                nc.scalar.activation(v2[:, :, :, 0:HD], vr[:].rearrange("p b (h d) -> p b h d", h=H), ACT.Copy).then_inc(v_second, 1)

            def high_x(n):
                need(act, x_normed if L2 else x_loaded, n + 1 if L2 else 16 * (n + 1))
                need(act, a_full[1], a_per * n)
                nc.scalar.activation(xh[:], xf[:], ACT.Copy).then_inc(x_high, 1)

            if L2:
                need(act, x_loaded, 16)
                squares(0, xf)
                deviation(0, 0)
            high_x(0)
            if L2:
                need(act, x_loaded, 32)
                squares(1, xf)
                deviation(1, 1)
            for s in range(SLOTS):
                if not L0 and s % 2 == 0 and s // 2 < len(order):
                    ws.high(act, s // 2)
                for fill in ended(s):
                    read_fill(0, fill)
                if s == 8:
                    first_values(0)
            high_x(1)
            second_values(0)

            def body(i):
                for s in range(SLOTS):
                    if s == 1 and L0:
                        need(act, coh_z, i + 1)
                        need(act, coh_step, 5 * i)
                        nc.scalar.activation(ce[:], cz[:], ACT.Exp, scale=-1.0).then_inc(coh_e, 1)
                    if 1 <= s <= UNITS:
                        high_probs(i, s - 1)
                    if s < UNITS:
                        exponentials(i, s)
                    if s == 8 and L1 and not (isinstance(i, int) and i == 0):
                        deviation(b_turn(i, "norm"), i - 1)
                    if s == 2 and L2 and has(i, 2):
                        need(act, x_loaded, 16 * (i + 3))
                        squares(i + 2, xf)
                    if s == 9 and L2 and has(i, 2):
                        deviation(b_turn(i, "norm"), i + 2)
                    if s == 7:
                        high_output(i, 0)
                    if s == 11:
                        high_output(i, 1)
                    if has(i, 1):
                        for fill in ended(s):
                            read_fill(i + 1, fill)
                        if s == 10:
                            first_values(i + 1)
                if has(i, 2):
                    high_x(i + 2)
                if has(i, 1):
                    second_values(i + 1)
                if L1:
                    need(act, b_full, b_turn(i, "out") + 1)
                    need(act, res_ready, i)
                    nc.scalar.activation(af[:, 0:2, :], bank_b[:].rearrange("p (c t) -> p c t", c=2), ACT.Copy).then_inc(b_free, 1)
                    need(act, out_full, i + 1)
                    nc.scalar.activation(af[:, 2:4, :], bank_o[:].rearrange("p (c t) -> p c t", c=2), ACT.Copy).then_inc(o_free, 1)
                    need(act, b_free, b_turn(i, "out") + 1)
                    need(act, o_free, o_turn(i, "out") + 1)
                    squares(i, af)

            iterate(act, body)
            if L1:
                deviation(4 * G - 1, G - 1)

        @block.vector
        def _(dve):
            def read_fill(p, fill):
                kind, m = fill
                bk, n = a_turn(p, fill)
                if kind == "c":
                    return
                src = bank_a[bk][:].rearrange("p (c t) -> p c t", c=2)
                if kind == "v":
                    if L0:
                        need(dve, a_full[bk], n + 1)
                        need(dve, v_split, p)
                        nc.vector.tensor_tensor(vf[:, m, :], bank_a[bk][:], k["bv"][:], ALU.add).then_inc(a_free[bk], 1)
                    return
                high, low = (kh, kl) if kind == "k" else (qh, ql)
                need(dve, k_high if kind == "k" else q_high, 2 * p + m + 1)
                if L0:
                    bias = k["bk"] if kind == "k" else k["bq"]
                    for c in range(2):
                        o = 2 * m + c
                        last = nc.vector.scalar_tensor_tensor(out=low[:, o, :], in0=src[:, c, :], scalar=bias[:, o:o + 1], in1=f32(high[:, o, :]),
                                                              op0=ALU.add, op1=ALU.subtract)
                else:
                    last = nc.vector.tensor_tensor(low[:, 2 * m:2 * m + 2, :], src, f32(high[:, 2 * m:2 * m + 2, :]), ALU.subtract)
                last.then_inc(a_free[bk], 1)

            def shift_scores(i, u):
                n = UNITS * i + u
                src = bank_s[u % 2][:].rearrange("p (h j) -> p h j", h=4)
                need(dve, s_full, n + 1)
                nc.vector.reduce_max(top[:, u % 2, :], src, AX_X).then_inc(top_ready, 1)
                need(dve, top_ready, n + 1)
                need(dve, t_full, n - 1)
                nc.vector.tensor_tensor(shifted[:, u % 2], src, bcast_last(top[:, u % 2, :], P), ALU.subtract).then_inc(shift_done, 1)

            def low_probs(i, u):
                need(dve, p_high, UNITS * i + u + 1)
                nc.vector.tensor_tensor(ptl[:, u % 2], bank_t[u % 2][:].rearrange("p (h j) -> p h j", h=4), pth[:, u % 2], ALU.subtract).then_inc(p_low, 1)

            def normalise(i, j):
                b = j // 2
                src = bank_o[:, 0:8 * VW].rearrange("p (h d) -> p h d", h=8)
                r = rz[:, j % 2, :]
                steps = 1 if L2 else 2
                need(dve, pv_done, UNITS * i + 2 * j + 2)
                nc.vector.reciprocal(r, src[:, :, HD]).then_inc(rz_step, 1)
                need(dve, rz_step, steps * (4 * i + j) + 1)
                if L0:
                    if j == 0:
                        need(dve, coh_step, 5 * (i + 1))
                    nc.vector.tensor_tensor(r, r, cf[:, b * H + (j % 2) * 8:b * H + (j % 2) * 8 + 8], ALU.mult).then_inc(rz_step, 1)
                if L1:
                    nc.vector.tensor_scalar(r, r, k["any_key"][:, 0:1], None, ALU.mult).then_inc(rz_step, 1)
                if not L2:
                    need(dve, rz_step, steps * (4 * i + j) + 2)
                if j % 2 == 0:
                    need(dve, b_full, b_turn(i - 1, f"ot{b}") + 1 if not (isinstance(i, int) and i == 0) else 0)
                dst = of[:, b, (j % 2) * 256:(j % 2) * 256 + 256].rearrange("p (h d) -> p h d", h=8)
                nc.vector.tensor_tensor(dst, src[:, :, 0:HD], bcast_last(r, HD), ALU.mult).then_inc(o_free, 1)

            def add_field(i, b):
                need(dve, b_full, b_turn(i, f"vsum{b}") + 1)
                need(dve, fd_ready, i + 1)
                need(dve, o_free, o_turn(i, f"pair{2 * b + 1}") + 1)
                nc.vector.scalar_tensor_tensor(out=of[:, b, :], in0=bank_b[:], scalar=fd[:, b:b + 1], in1=of[:, b, :], op0=ALU.mult, op1=ALU.add).then_inc(b_free, 1)

            def low_output(i, b):
                need(dve, ot_high, NB * i + b + 1)
                part = slice(b * P, (b + 1) * P)
                nc.vector.tensor_tensor(otl[:, :, part], bank_b[:].rearrange("p (c t) -> p c t", c=CH), f32(oth[:, :, part]), ALU.subtract).then_inc(b_free, 1)

            def add_squares(n):
                need(dve, sq_ready, n + 1)
                nc.vector.tensor_tensor(half[:], sq[:, 0:2, :], sq[:, 2:4, :], ALU.add).then_inc(sum_step, 1)
                need(dve, sum_step, 2 * n + 1)
                nc.vector.tensor_tensor(quarter[:], half[:, 0, :], half[:, 1, :], ALU.add).then_inc(sum_step, 1)

            def norm(n, turn, tile, gains, biases, out_sem):
                need(dve, b_free, turn + 1)
                nc.vector.tensor_copy(gt[:], gains[:, :, bass.ds(NB * n, NB)])
                nc.vector.tensor_copy(bt[:], biases[:, :, bass.ds(NB * n, NB)])
                nc.vector.reciprocal(rs[:], sd[:]).then_inc(norm_step, 1)
                need(dve, norm_step, 2 * n + 1)
                nc.vector.tensor_tensor(tile[:], tile[:], bcast_mid(rs[:], CH), ALU.mult).then_inc(norm_step, 1)
                need(dve, norm_step, 2 * n + 2)
                for c in range(CH):
                    for b in range(NB):
                        part = tile[:, c, b * P:(b + 1) * P]
                        last = nc.vector.tensor_scalar(part, part, gt[:, c, b:b + 1], bt[:, c, b:b + 1], ALU.mult, ALU.add)
                last.then_inc(out_sem, 1)

            if L1 or L2:
                nc.vector.memset(eps[:], 1e-6).then_inc(eps_set, 1)
            if L2:
                for n in range(2):
                    add_squares(n)
                    norm(n, n, xf, k["g1"], k["b1"], x_normed)
            if L0:
                nc.vector.tensor_copy(tb[:], k["tanh_bias"][:, :, 0:NB]).then_inc(tb_ready, 1)
            for s in range(SLOTS):
                if not L0 and s % 2 == 0 and s // 2 < len(order):
                    ws.low(dve, s // 2)
                for fill in ended(s):
                    read_fill(0, fill)

            def body(i):
                first = isinstance(i, int) and i == 0
                for s in range(SLOTS):
                    if s < UNITS:
                        shift_scores(i, s)
                    if 1 <= s <= UNITS:
                        low_probs(i, s - 1)
                    if s == 0 and L0:
                        need(dve, b_full, b_turn(i, "coh") + 1)
                        nc.vector.tensor_copy(fd[:], k["field"][:, bass.ds(NB * i, NB)]).then_inc(fd_ready, 1)
                        need(dve, coh_e, i)
                        z = bank_b[:, 0:2 * NB * H].rearrange("p (b s h) -> p b s h", b=NB, s=2)
                        cz3, bias3 = (t[:].rearrange("p (b h) -> p b h", b=NB) for t in (cz, k["bc2"]))
                        nc.vector.tensor_tensor(cz3, z[:, :, 0, :], bias3, ALU.add).then_inc(coh_sum, 1)
                        need(dve, coh_sum, i + 1)
                        nc.vector.tensor_tensor(cz3, z[:, :, 1, :], cz3, ALU.add).then_inc(b_free, 1)
                        need(dve, b_free, b_turn(i, "coh") + 1)
                        nc.vector.tensor_scalar_max(cz[:], cz[:], -88.0).then_inc(coh_z, 1)
                    if s == 1 and L0:
                        need(dve, coh_e, i + 1)
                        nc.vector.tensor_scalar_add(ce[:], ce[:], 1.0).then_inc(coh_step, 1)
                        need(dve, coh_step, 5 * i + 1)
                        nc.vector.reciprocal(cc[:], ce[:]).then_inc(coh_step, 1)
                        need(dve, coh_step, 5 * i + 2)
                        nc.vector.tensor_scalar_add(c8[:], cc[:], 1e-8).then_inc(coh_step, 1)
                        need(dve, coh_step, 5 * i + 3)
                        nc.vector.reciprocal(c8[:], c8[:]).then_inc(coh_step, 1)
                        need(dve, coh_step, 5 * i + 4)
                        nc.vector.scalar_tensor_tensor(out=cf[:], in0=cc[:], scalar=1.0 - FIELD, in1=c8[:], op0=ALU.mult, op1=ALU.mult).then_inc(coh_step, 1)
                    if 4 <= s <= 10 and s % 2 == 0:
                        normalise(i, s // 2 - 2)
                    if s == 6 and L0:
                        add_field(i, 0)
                    if s == 10 and L0:
                        add_field(i, 1)
                    if s == 7:
                        low_output(i, 0)
                    if s == 11:
                        low_output(i, 1)
                    if s == 6 and L1 and not first:
                        add_squares(i - 1)
                    if s == 9 and L1 and not first:
                        norm(i - 1, b_turn(i, "norm"), af, k["gain"], k["shift"], y_ready)
                    if s == 8 and L2 and has(i, 2):
                        add_squares(i + 2)
                    if s == 10 and L2 and has(i, 2):
                        norm(i + 2, b_turn(i, "norm"), xf, k["g1"], k["b1"], x_normed)
                    if has(i, 1):
                        if s == 7 and L0:
                            need(dve, a_free[1], a_per * i + 3)
                            nc.vector.tensor_copy(tb[:], k["tanh_bias"][:, :, bass.ds(NB * (i + 1), NB)]).then_inc(tb_ready, 1)
                        for fill in ended(s):
                            read_fill(i + 1, fill)
                if L1:
                    return
                need(dve, res_loaded, 16 * (i + 1))
                need(dve, b_full, b_turn(i, "out") + 1)
                for m, (bk, free) in enumerate(((bank_b, b_free), (bank_o, o_free))):
                    if m == 1:
                        need(dve, out_full, i + 1)
                    if L0:
                        for c in range(2):
                            o = 2 * m + c
                            last = nc.vector.scalar_tensor_tensor(out=xres[:, o, :], in0=bk[:, c * T:(c + 1) * T], scalar=k["bout"][:, o:o + 1],
                                                                  in1=xres[:, o, :], op0=ALU.add, op1=ALU.add)
                    else:
                        part = xres[:, 2 * m:2 * m + 2, :]
                        last = nc.vector.tensor_tensor(part, bk[:].rearrange("p (c t) -> p c t", c=2), part, ALU.add)
                    last.then_inc(free, 1)

            iterate(dve, body)
            if L1:
                add_squares(G - 1)
                norm(G - 1, 4 * G - 1, af, k["gain"], k["shift"], y_ready)

        @block.gpsimd
        def _(pool):
            def low_x(n):
                need(pool, x_high, n + 1)
                nc.gpsimd.tensor_tensor(xl[:], xf[:], f32(xh[:]), ALU.subtract).then_inc(x_split, 1)

            def parts(t):
                return t[:].rearrange("p b (h d) -> p b h d", h=H)

            def rest_of_values(p):
                need(pool, v_first, p + 1)
                nc.gpsimd.tensor_tensor(parts(vr), parts(vf), v1[:, :, :, 0:HD], ALU.subtract).then_inc(v_rest, 1)

            def third_values(p):
                need(pool, v_second, p + 1)
                nc.gpsimd.tensor_tensor(v3[:, :, :, 0:HD], parts(vr), v2[:, :, :, 0:HD], ALU.subtract).then_inc(v_split, 1)

            def low_t(p):
                for m in range(2):
                    need(pool, t_high, 2 * p + m + 1)
                    nc.gpsimd.tensor_tensor(tl[:, 2 * m:2 * m + 2, :], tf[:, m], f32(th[:, 2 * m:2 * m + 2, :]), ALU.subtract).then_inc(t_split, 1)

            low_x(0)
            if L0:
                low_t(0)
            rest_of_values(0)
            low_x(1)
            third_values(0)

            def body(i):
                if has(i, 1):
                    if L0:
                        low_t(i + 1)
                    rest_of_values(i + 1)
                if L1 and not (isinstance(i, int) and i == 0):
                    add_residual(i - 1)
                if has(i, 2):
                    low_x(i + 2)
                if has(i, 1):
                    third_values(i + 1)

            def add_residual(n):
                need(pool, y_ready, n + 1)
                need(pool, res_loaded, 16 * (n + 1))
                nc.gpsimd.tensor_tensor(xres[:], xres[:], af[:], ALU.add).then_inc(res_ready, 1)

            iterate(pool, body)
            if L1:
                add_residual(G - 1)


def gated_mlp(nc, hold, k, sweep, x_in, layer_in, partial, x_out, w_gate, w_hid, w_out):
    last_sweep = sweep == SWEEPS - 1
    tag = f"mlp{sweep}"
    with ExitStack() as ctx:
        def sb(name, shape, dt=F32):
            return ctx.enter_context(nc.sbuf_tensor(f"{tag}_{name}", shape, dt))

        def sem(name):
            return held(nc, hold, f"{tag}_{name}")

        def bank(name):
            return ctx.enter_context(nc.psum_tensor(f"{tag}_{name}", [P, FT], F32))

        wg = [sb("wgh", [P, HC, CH, P], F32R), sb("wgl", [P, HC, CH, P], F32R)]
        wu = [sb("wuh", [P, HC, CH, P], F32R), sb("wul", [P, HC, CH, P], F32R)]
        wo = [sb("woh", [P, HC, E], F32R), sb("wol", [P, HC, E], F32R)]
        loads = []
        for n in range(0, HC, 2):
            for dram, tiles in ((w_gate, wg), (w_hid, wu)):
                loads.append((dram[:, sweep * HC + n:sweep * HC + n + 2].rearrange("p n c e -> p (n c e)"),
                              *(t[:, n:n + 2].rearrange("p n c e -> p (n c e)") for t in tiles)))
            loads.append((w_out[:, sweep * HC + n:sweep * HC + n + 2, :].rearrange("p n e -> p (n e)"),
                          *(t[:, n:n + 2].rearrange("p n e -> p (n e)") for t in wo)))
        ws = Splitter(nc, ctx, hold, tag, loads, 2 if last_sweep else 3)

        xf = sb("xf", [P, CH, FT])
        hh = [sb(f"hh{n}", [P, CH, FT], F32R) for n in range(2)]
        hl = [sb(f"hl{n}", [P, CH, FT], F32R) for n in range(2)]
        res = sb("res", [P, CH, FT])
        yt = sb("yt", [P, CH, FT]) if last_sweep else res
        ot = sb("ot", [P, CH, FT]) if last_sweep else yt
        res2 = res if last_sweep else sb("res2", [P, CH, FT])
        half, quarter = sb("half", [P, 2, FT]), sb("quarter", [P, FT])
        sd, rs = sb("sd", [P, FT]), sb("rs", [P, FT])
        gt, bt = sb("gt", [P, CH, FT // P]), sb("bt", [P, CH, FT // P])
        sqb = sb("sqb", [P, 2, FT])
        eps = sb("eps", [P, 1])
        sg, act_t = sb("sg", [P, 2, FT]), sb("act_t", [P, 2, FT])
        ah, al = sb("ah", [P, 2, FT], F32R), sb("al", [P, 2, FT], F32R)
        bank_g, bank_u = [bank("bank_g0"), bank("bank_g1")], [bank("bank_u0"), bank("bank_u1")]
        bank_y = [bank(f"bank_y{n}") for n in range(CH)]

        x_loaded, res_loaded, stored = sem("x_loaded"), sem("res_loaded"), sem("stored")
        res2_loaded, res_added = sem("res2_loaded"), sem("res_added")
        sq_ready, sum_step, sd_ready, norm_step, h_high, h_low = (sem(n) for n in ("sq_ready", "sum_step", "sd_ready", "norm_step", "h_high", "h_low"))
        turn_full, silu_done, prod_done, a_high, a_low, down_done = (sem(n) for n in ("turn_full", "silu_done", "prod_done", "a_high", "a_low", "down_done"))
        y_read, mix_step, eps_set, h_ready = sem("y_read"), sem("mix_step"), sem("eps_set"), sem("h_ready")

        TURNS = HC + 1
        NORM_AT = 3

        def pos(j, c):
            return c + 1 if c >= NORM_AT and has(j, 1) else c

        def turn(j, at):
            return 1 + TURNS * j + at

        def par(odd, at):
            return (1 + TURNS * odd + at) % 2

        def has(j, ahead):
            return not isinstance(j, int) or 0 <= j + ahead < FG

        def wait_bank_free(eng, j, at):
            back = at - 2
            if back < 0:
                if isinstance(j, int) and j == 0:
                    if back == -1:
                        need(eng, sd_ready, 1)
                    return
                j, back = j - 1, back + TURNS
            if has(j, 1) and back == NORM_AT:
                need(eng, sd_ready, j + 2)
            else:
                need(eng, prod_done, HC * j + (back - 1 if has(j, 1) and back > NORM_AT else back) + 1)

        def iterate(eng, body):
            body(0, 0)
            body(1, 1)
            with eng.Fori(2, FG - 2, 2) as j:
                body(j, 0)
                body(j + 1, 1)
            body(FG - 2, 0)
            body(FG - 1, 1)

        block = ctx.enter_context(nc.Block())

        @block.sync
        def _(sp):
            def move(n, dram, tile, out, done):
                for g in range(FT // T):
                    d = dram[bass.ds((FT // T) * n + g, 1)].rearrange("g p c t -> (g p) c t")
                    t = tile[:, :, g * T:(g + 1) * T]
                    sp.dma_start(d if out else t, t if out else d).then_inc(done, 16)

            move(0, x_in, xf, False, x_loaded)
            for n in range(6):
                ws.load(sp, n)

            def body(j, odd):
                if has(j, 1):
                    need(sp, h_low, CH * (j + 1))
                    move(j + 1, x_in, xf, False, x_loaded)
                if last_sweep:
                    need(sp, y_read, CH * j)
                else:
                    need(sp, stored, 32 * j)
                move(j, partial if last_sweep else x_in, res, False, res_loaded)
                if not last_sweep:
                    move(j, layer_in, res2, False, res2_loaded)
                if isinstance(j, int) and j == 0:
                    for n in range(6, len(loads)):
                        ws.load(sp, n)
                if last_sweep:
                    if has(j, -1):
                        need(sp, mix_step, 4 * CH * j)
                        move(j - 1, x_out, ot, True, stored)
                else:
                    need(sp, y_read, CH * (j + 1))
                    move(j, partial, yt, True, stored)

            iterate(sp, body)
            if last_sweep:
                need(sp, mix_step, 4 * CH * FG)
                move(FG - 1, x_out, ot, True, stored)
            sp.wait_ge(stored, 32 * FG)

        @block.tensor
        def _(pe):
            def mm3(out, w, x_h, x_l, first, last):
                nc.tensor.matmul(out, w[0], x_h, start=first, stop=False)
                nc.tensor.matmul(out, w[1], x_h, start=False, stop=False)
                return nc.tensor.matmul(out, w[0], x_l, start=False, stop=last)

            def norm_sum(n, b):
                need(pe, sum_step, 2 * (n + 1))
                nc.tensor.matmul(bank_g[b][:], k["ones"][:], quarter[:], start=True, stop=True).then_inc(turn_full, 1)

            norm_sum(0, 0)

            def down(j, c):
                need(pe, a_low, HC * j + c + 1)
                if isinstance(j, int) and j == 0:
                    need(pe, ws.low_done, 3 * (c // 2) + 3)
                if c == 0:
                    need(pe, y_read, CH * j)
                for o in range(CH):
                    mm = mm3(bank_y[o][:], [w[:, c, o * P:(o + 1) * P] for w in wo], ah[:, c % 2, :], al[:, c % 2, :], c == 0, c == HC - 1)
                mm.then_inc(down_done, 1)

            def body(j, odd):
                need(pe, h_low, CH * (j + 1))
                for c in range(HC):
                    if c == NORM_AT and has(j, 1):
                        wait_bank_free(pe, j, NORM_AT)
                        norm_sum(j + 1, par(odd, NORM_AT))
                    wait_bank_free(pe, j, pos(j, c))
                    b = par(odd, pos(j, c))
                    if isinstance(j, int) and j == 0:
                        need(pe, ws.low_done, 3 * (c // 2) + 2)
                    for w, bk in ((wg, bank_g[b]), (wu, bank_u[b])):
                        for e in range(CH):
                            mm = mm3(bk[:], [t[:, c, e, :] for t in w], hh[odd][:, e, :], hl[odd][:, e, :], e == 0, e == CH - 1)
                    mm.then_inc(turn_full, 1)
                    if c > 0:
                        down(j, c - 1)
                down(j, HC - 1)

            iterate(pe, body)

        @block.scalar
        def _(act):
            def squares(n):
                need(act, x_loaded, 32 * (n + 1))
                need(act, sum_step, 2 * n)
                nc.scalar.activation(half[:], xf[:, 0:2, :], ACT.Square)
                nc.scalar.activation(sqb[:], xf[:, 2:4, :], ACT.Square).then_inc(sq_ready, 1)

            def deviation(n, b, count):
                need(act, turn_full, count)
                need(act, norm_step, (1 + CH) * n)
                nc.scalar.activation(sd[:], bank_g[b][:], ACT.Sqrt, bias=eps[:, 0:1], scale=1.0 / E).then_inc(sd_ready, 1)

            def high_h(n, e, odd):
                need(act, h_ready, CH * n + e + 1)
                if e == 0 and not (isinstance(n, int) and n < 2):
                    need(act, turn_full, turn(n - 2, HC) + 1)
                nc.scalar.activation(hh[odd][:, e, :], xf[:, e, :], ACT.Copy).then_inc(h_high, 1)

            act.wait_ge(eps_set, 1)
            squares(0)
            deviation(0, 0, 1)
            for n in range(3):
                ws.high(act, n)
            for e in range(CH):
                high_h(0, e, 0)

            def body(j, odd):
                first = isinstance(j, int) and j == 0
                for c in range(HC):
                    if first and c % 2 == 0 and c + 2 < HC:
                        for n in range(3):
                            ws.high(act, 3 * (c // 2 + 1) + n)
                    if c == 0 and has(j, 1):
                        squares(j + 1)
                    n = HC * j + c
                    need(act, turn_full, turn(j, pos(j, c)) + 1)
                    need(act, prod_done, n - 1)
                    nc.scalar.activation(sg[:, c % 2, :], bank_g[par(odd, pos(j, c))][:], ACT.Silu).then_inc(silu_done, 1)
                    if c == NORM_AT - 1 and has(j, 1):
                        deviation(j + 1, par(odd, NORM_AT), turn(j, NORM_AT) + 1)
                    need(act, prod_done, n + 1)
                    need(act, down_done, n - 1)
                    nc.scalar.activation(ah[:, c % 2, :], act_t[:, c % 2, :], ACT.Copy).then_inc(a_high, 1)
                    if c >= NORM_AT + 1 and has(j, 1):
                        high_h(j + 1, c - NORM_AT - 1, 1 - odd)

            iterate(act, body)

        @block.vector
        def _(dve):
            def norm_start(n):
                need(dve, sd_ready, n + 1)
                nc.vector.tensor_copy(gt[:], k["g2"][:, :, bass.ds((FT // P) * n, FT // P)])
                nc.vector.tensor_copy(bt[:], k["b2"][:, :, bass.ds((FT // P) * n, FT // P)])
                nc.vector.reciprocal(rs[:], sd[:]).then_inc(norm_step, 1)

            def norm(n, e):
                need(dve, norm_step, (1 + CH) * n + 1)
                nc.vector.tensor_tensor(xf[:, e, :], xf[:, e, :], rs[:], ALU.mult).then_inc(norm_step, 1)
                need(dve, norm_step, (1 + CH) * n + e + 2)
                for b in range(FT // P):
                    part = xf[:, e, b * P:(b + 1) * P]
                    last = nc.vector.tensor_scalar(part, part, gt[:, e, b:b + 1], bt[:, e, b:b + 1], ALU.mult, ALU.add)
                last.then_inc(h_ready, 1)

            def low_h(n, e, odd):
                need(dve, h_high, CH * n + e + 1)
                nc.vector.tensor_tensor(hl[odd][:, e, :], xf[:, e, :], f32(hh[odd][:, e, :]), ALU.subtract).then_inc(h_low, 1)

            def add_squares(n):
                need(dve, sq_ready, n + 1)
                nc.vector.tensor_tensor(half[:], half[:], sqb[:], ALU.add).then_inc(sum_step, 1)
                need(dve, sum_step, 2 * n + 1)
                nc.vector.tensor_tensor(quarter[:], half[:, 0, :], half[:, 1, :], ALU.add).then_inc(sum_step, 1)

            def mix_row(n, i):
                at = 4 * CH * n + 4 * i
                if i == 0:
                    need(dve, stored, 32 * n)
                nc.vector.tensor_scalar(ot[:, i, :], yt[:, 0, :], k["mix"][:, 4 * i:4 * i + 1], None, ALU.mult).then_inc(mix_step, 1)
                for m in range(1, 4):
                    need(dve, mix_step, at + m)
                    nc.vector.scalar_tensor_tensor(out=ot[:, i, :], in0=yt[:, m, :], scalar=k["mix"][:, 4 * i + m:4 * i + m + 1], in1=ot[:, i, :],
                                                   op0=ALU.mult, op1=ALU.add).then_inc(mix_step, 1)

            nc.vector.memset(eps[:], 1e-6).then_inc(eps_set, 1)
            add_squares(0)
            norm_start(0)
            for e in range(CH):
                norm(0, e)
            for n in range(3):
                ws.low(dve, n)
            for e in range(CH):
                low_h(0, e, 0)

            def body(j, odd):
                first = isinstance(j, int) and j == 0
                for c in range(HC):
                    n = HC * j + c
                    if first and c % 2 == 0 and c + 2 < HC:
                        for m in range(3):
                            ws.low(dve, 3 * (c // 2 + 1) + m)
                    if c == 1 and has(j, 1):
                        add_squares(j + 1)
                    need(dve, silu_done, n + 1)
                    need(dve, a_low, n - 1)
                    nc.vector.tensor_tensor(act_t[:, c % 2, :], bank_u[par(odd, pos(j, c))][:], sg[:, c % 2, :], ALU.mult).then_inc(prod_done, 1)
                    if last_sweep and c < CH and has(j, -1):
                        mix_row(j - 1, c)
                    e = c - NORM_AT
                    if has(j, 1):
                        if e == 0:
                            norm_start(j + 1)
                        if 0 <= e < CH:
                            norm(j + 1, e)
                        if 1 <= e:
                            low_h(j + 1, e - 1, 1 - odd)
                need(dve, down_done, HC * (j + 1))
                if last_sweep:
                    need(dve, res_loaded, 32 * (j + 1))
                else:
                    need(dve, res_added, j + 1)
                if not last_sweep:
                    need(dve, stored, 32 * j)
                for o in range(CH):
                    nc.vector.tensor_tensor(yt[:, o, :], bank_y[o][:], res[:, o, :], ALU.add).then_inc(y_read, 1)
                if last_sweep:
                    need(dve, y_read, CH * (j + 1))

            iterate(dve, body)
            if last_sweep:
                for i in range(CH):
                    mix_row(FG - 1, i)

        @block.gpsimd
        def _(pool):
            def body(j, odd):
                for c in range(HC):
                    n = HC * j + c
                    if c == 4 and not last_sweep:
                        need(pool, res_loaded, 32 * (j + 1))
                        need(pool, res2_loaded, 32 * (j + 1))
                        nc.gpsimd.tensor_tensor(res[:], res[:], res2[:], ALU.add).then_inc(res_added, 1)
                    need(pool, a_high, n + 1)
                    nc.gpsimd.tensor_tensor(al[:, c % 2, :], act_t[:, c % 2, :], f32(ah[:, c % 2, :]), ALU.subtract).then_inc(a_low, 1)

            iterate(pool, body)


def build(nc, a, out):
    scratch = [nc.dram_tensor(f"resid{n}", (G, P, CH, T), F32, kind="Internal").ap() for n in range(4)]
    with ExitStack() as ctx:
        def keep(name, shape, dt=F32):
            return ctx.enter_context(nc.sbuf_tensor("keep_" + name, shape, dt))

        k = {n: keep(n, [P, CH, B]) for n in ("tanh_bias", "gain", "shift", "g1", "b1", "g2", "b2")}
        k |= {n: keep(n, [P, CH]) for n in ("bq", "bk", "bout")}
        k["bv"] = keep("bv", [P, E])
        k["bc2"] = keep("bc2", [P, NB * H])
        k["field"] = keep("field", [P, B])
        k["mix"] = keep("mix", [P, 16])
        k["any_key"] = keep("any_key", [P, 1])
        k["ones"] = keep("ones", [P, P])
        k["ident"] = keep("ident", [P, P])
        k["ident_r"], k["mask"] = (keep(n, [P, P], F32R) for n in ("ident_r", "mask"))
        k["ones_b"] = keep("ones_b", [P, P], BF16)
        k["lift"] = keep("lift", [P, 1])
        def phase(make, *args):
            hold = []
            make(nc, hold, k, *args)
            nc.clear_and_free_semaphores(hold)
            with nc.Block():
                pass

        def weight_tiles(wctx, tag, names):
            return tuple({n: wctx.enter_context(nc.sbuf_tensor(f"{tag}_w{n}{part}", [P, CH, E], F32R)) for n in names} for part in "hl")

        with ExitStack() as actx:
            def shared(name, shape, dt):
                return actx.enter_context(nc.sbuf_tensor("keep_" + name, shape, dt))

            k["kbh"] = [shared(f"kbh{b}", [P, CH, 4, P], F32R) for b in range(NB)]
            k["kbl"] = [shared(f"kbl{b}", [P, CH, 4, P], F32R) for b in range(NB)]
            for n in ("v1", "v2", "v3"):
                k[n] = shared(n, [P, NB, H, VW], BF16)
            with ExitStack() as wctx:
                wh, wl = weight_tiles(wctx, "L0", "kvqoc")
                k["wc2"] = wctx.enter_context(nc.sbuf_tensor("keep_wc2", [P, CH, 2 * H], F32R))
                early = [(a["L0_" + n], flat3(wh[n]), flat3(wl[n])) for n in "kvcqo"]
                phase(prepare, a, early)
                phase(attention, "L0", a["x"], scratch[0], wh, wl, {})
            for tag, src, dst in (("L1", scratch[0], scratch[1]), ("L2", scratch[1], scratch[2])):
                with ExitStack() as wctx:
                    wh, wl = weight_tiles(wctx, tag, "kvqo")
                    phase(attention, tag, src, dst, wh, wl, {n: a[f"{tag}_{n}"] for n in "kvqo"})
        phase(gated_mlp, 0, scratch[2], scratch[1], scratch[3], None, a["gate_w"], a["hid_w"], a["out_w"])
        phase(gated_mlp, 1, scratch[2], scratch[1], scratch[3], out, a["gate_w"], a["hid_w"], a["out_w"])


def kernel(**inputs):
    import numpy as _np
    import concourse.bacc as _bacc
    from concourse import mybir as _mybir
    from concourse.bass_utils import run_bass_kernel_spmd as _run

    def cols(w):
        w = _np.asarray(w).T
        return w.reshape(w.shape[0] // P, P, w.shape[1]).transpose(1, 0, 2)

    def flat(w):
        w = cols(w)
        return w.reshape(P, -1)

    def by_chunk(v):
        return _np.asarray(v).reshape(-1, P).T

    g = {n.replace("_cond", ""): _np.asarray(v) for n, v in inputs.items()}
    arrays = {}
    arrays["x"] = g["x"].reshape(G, T, CH, P).transpose(0, 3, 2, 1)
    arrays["cond_t"] = g["cond_256"].T
    arrays["mask"] = g["mask_SxS_bk1"]
    wqkv = g["L0_Wqkv"].reshape(3, E, E)
    bqkv = g["L0_bqkv"].reshape(3, E)
    for n, w in zip("qkvoc", (wqkv[0], wqkv[1], wqkv[2], g["L0_Wout"], g["L0_Wc1"][:, 0:E])):
        arrays["L0_" + n] = flat(w)
    arrays["L0_c2"] = cols(g["L0_Wc2"])
    for layer in ("L1", "L2"):
        for n in "qkvo":
            arrays[f"{layer}_{n}"] = flat(g[f"{layer}_W{n}"])
    arrays["w_c1c"] = g["L0_Wc1"][:, E:].T
    arrays["w_e1"] = g["L0_We1"].T
    arrays["w_e2"] = cols(g["L0_We2"])
    arrays["w_c"] = g["L1_Wc"].T
    arrays["w_gb"] = _np.stack([g[f"L2_{n}w"].T for n in ("g1", "b1", "g2", "b2")], axis=1)
    inv = _np.float32(10000.0) ** _np.repeat(_np.arange(0, E, 2, dtype=_np.float32) / _np.float32(E), 2)
    code = _np.sin(_np.arange(P, dtype=_np.float32)[:, None] / inv[None, :])
    arrays["pe_t"] = cols(code.astype(_np.float32))
    arrays["eye"] = _np.eye(P, dtype=_np.float32)
    arrays["bq_c"], arrays["bk_c"], arrays["bv"] = by_chunk(bqkv[0]), by_chunk(bqkv[1]), bqkv[2]
    arrays["bout_c"] = by_chunk(g["L0_bout"])
    arrays["bc2"] = _np.concatenate([g["L0_bc2"]] * NB)
    for n, v in (("bc1", "L0_bc1"), ("be1", "L0_be1"), ("bc", "L1_bc"), ("rms", "L1_rms_scale"), ("g1b", "L2_g1b"),
                 ("b1b", "L2_b1b"), ("g2b", "L2_g2b"), ("b2b", "L2_b2b")):
        arrays[n + "_c"] = by_chunk(g[v])
    arrays["be2"], arrays["ln_g"], arrays["ln_b"] = g["L0_be2"], g["L0_ln_g"], g["L0_ln_b"]
    for n in ("gate_w", "hid_w"):
        arrays[n] = cols(g["L2_" + n]).reshape(P, CH, HID // P, P).transpose(0, 2, 1, 3)
    arrays["out_w"] = cols(g["L2_out_w"])
    arrays["qr_t"] = g["L3_q_right"].T
    arrays["gate_t"] = g["L3_spectral_gate"].reshape(1, P).T
    arrays = {n: _np.ascontiguousarray(v) for n, v in arrays.items()}

    nc = _bacc.Bacc("TRN2", target_bir_lowering=False, num_devices=1)
    args = {n: nc.dram_tensor("in_" + n, v.shape, _mybir.dt.from_np(v.dtype), kind="ExternalInput").ap() for n, v in arrays.items()}
    out = nc.dram_tensor("out", (G, P, CH, T), F32, kind="ExternalOutput").ap()
    build(nc, args, out)
    r = _run(nc, [{"in_" + n: v for n, v in arrays.items()}], core_ids=[0])
    y = _np.asarray(r.results[0]["out"])
    return _np.ascontiguousarray(y.transpose(0, 3, 2, 1).reshape(B, P, E))
```

```python
from contextlib import ExitStack

import numpy as np

import concourse.bass as bass
from concourse import mybir


ALU = mybir.AluOpType
ACT = mybir.ActivationFunctionType
F32 = mybir.dt.float32
F32R = mybir.dt.float32r
F16 = mybir.dt.float16
BF16 = mybir.dt.bfloat16
AX_X = mybir.AxisListType.X

P = 128
B = 32
E = 512
CH = E // P
H = 16
HD = E // H
VW = HD + 2
T = 256
NB = T // P
G = B // NB
UNITS = NB * CH
SLOTS = UNITS + 4
HID = 4 * E
FT = 512
FG = B * P // FT
SWEEPS = 2
HC = HID // P // SWEEPS
SCALE = float(HD) ** -0.5
LIFT = 14 * float(np.log(2.0))
FIELD = 0.3 * 0.7
MASKED = -1e30
KB_DONE = 2 * 4 * 16


PACKED = {"cond_t": B, "be1": CH, "bc1": CH, "bc": 2 * CH, "rms": CH, "g1b": CH, "b1b": CH, "g2b": CH, "b2b": CH,
          "qr_t": 4, "gate_t": 1, "bq": CH, "bk": CH, "bout": CH, "L0_c2": CH * H, "eye": P}


def f32(ap):
    return ap.bitcast(F32)


def positive(value):
    return not (isinstance(value, int) and value <= 0)


def held(nc, hold, name):
    s = nc.alloc_semaphore(name)
    hold.append(s)
    return s


def bcast_mid(ap, n):
    return ap.unsqueeze(1).broadcast_to([ap.shape[0], n, ap.shape[1]])


def bcast_last(ap, n):
    return ap.unsqueeze(2).broadcast_to([ap.shape[0], ap.shape[1], n])


class Splitter:

    def __init__(self, nc, hold, tag, loads, stage):
        self.nc, self.loads, self.stage, self.stages = nc, loads, stage, len(stage)
        self.loaded = [held(nc, hold, f"{tag}_w_loaded{n}") for n in range(self.stages)]
        self.high_done = held(nc, hold, f"{tag}_w_high")
        self.low_done = held(nc, hold, f"{tag}_w_low")

    def load(self, sp, n):
        src = self.loads[n][0]
        if positive(n + 1 - self.stages):
            sp.wait_ge(self.low_done, n + 1 - self.stages)
        sp.dma_start(self.stage[n % self.stages][:, 0:src.shape[1]], src).then_inc(self.loaded[n % self.stages], 16)

    def high(self, act, n):
        src, high, _ = self.loads[n]
        act.wait_ge(self.loaded[n % self.stages], 16 * (n // self.stages + 1))
        self.nc.scalar.activation(high, self.stage[n % self.stages][:, 0:src.shape[1]], ACT.Copy).then_inc(self.high_done, 1)

    def low(self, dve, n):
        src, high, low = self.loads[n]
        dve.wait_ge(self.high_done, n + 1)
        self.nc.vector.tensor_tensor(low, self.stage[n % self.stages][:, 0:src.shape[1]], f32(high), ALU.subtract).then_inc(self.low_done, 1)


def flat3(t):
    return t[:].rearrange("p c e -> p (c e)")


def prepare(nc, hold, k, a, weights):
    with ExitStack() as ctx:
        def sb(name, shape, dt=F32):
            return ctx.enter_context(nc.sbuf_tensor("prep_" + name, shape, dt))

        def sem(name):
            return held(nc, hold, "prep_" + name)

        w_c1c = sb("w_c1c", [P, E])
        w_e1 = sb("w_e1", [P, E])
        w_e2 = sb("w_e2", [P, CH, E])
        w_c = sb("w_c", [P, 2 * E])
        w_gb = sb("w_gb", [P, 4, E])
        pe_t = sb("pe_t", [P, CH, P])
        col = {n: k["packed"][n] for n in ("bc1", "be1", "bc", "rms", "g1b", "b1b", "g2b", "b2b")}
        cond, qr, gate = (k["packed"][n] for n in ("cond_t", "qr_t", "gate_t"))
        w_c2 = k["packed"]["L0_c2"].rearrange("p (c h) -> p c h", c=CH)
        row_pack = sb("row_pack", [B, 3 * E])
        rows = {n: row_pack[:, m * E:(m + 1) * E] for m, n in enumerate(("be2", "ln_g", "ln_b"))}
        mask8 = sb("mask8", [P, P], mybir.dt.uint8)
        maskf = sb("maskf", [P, P])
        ones_f = sb("ones_f", [P, P])
        silu_c = sb("silu_c", [P, B])
        relu1 = sb("relu1", [P, CH, B])
        fp = sb("fp", [B, E])
        fp_t = sb("fp_t", [P, CH, B])
        sq = sb("sq", [P, E])
        s1 = sb("s1", [P, 8])
        fa = sb("fa", [B, P])
        sc1 = sb("sc1", [P, CH, B])
        lq = sb("lq", [P, 4])
        rq = sb("rq", [P, 4])
        lm = sb("lm", [P, 16])
        rm = sb("rm", [P, 16])
        tq = sb("tq", [P, 4])
        ps = [ctx.enter_context(nc.psum_tensor(f"prep_ps{n}", [P, 512], F32)) for n in range(8)]
        ws = Splitter(nc, hold, "prep", weights, [sb(f"stage{n}", [P, CH * E]) for n in range(2)])
        small_loaded, e2_loaded, late_loaded = sem("small_loaded"), sem("e2_loaded"), sem("late_loaded")
        cond_done, fp_done, gb_done, turn_done, logits_done, c_done, field_done = (
            sem(n) for n in ("cond_done", "fp_done", "gb_done", "turn_done", "logits_done", "c_done", "field_done"))
        exp_done, relu_done, root_done, deviation_done, soft_done = (sem(n) for n in ("exp_done", "relu_done", "root_done", "deviation_done", "soft_done"))
        silu_done, squares_done, variance_done, fp_normed, fp_turned, logits_shifted, field_scaled = (
            sem(n) for n in ("silu_done", "squares_done", "variance_done", "fp_normed", "fp_turned", "logits_shifted", "field_scaled"))
        dve_step = sem("dve_step")
        block = ctx.enter_context(nc.Block())
        small = [(k["pack"][:], a["pack"]), (w_e1[:], a["w_e1"]), (w_c1c[:], a["w_c1c"]), (mask8[:], a["mask"]),
                 (row_pack[:], a["row_pack"].partition_broadcast(B))]
        late = [(pe_t[:], a["pe_t"]), (w_gb[:], a["w_gb"]), (w_c[:], a["w_c"]), (k["bias_rows"][:], a["bias_rows"].partition_broadcast(P))]

        @block.sync
        def _(sp):
            for dst, src in small:
                sp.dma_start(dst, src).then_inc(small_loaded, 16)
            sp.dma_start(w_e2[:], a["w_e2"]).then_inc(e2_loaded, 16)
            for dst, src in late:
                sp.dma_start(dst, src).then_inc(late_loaded, 16)
            for n in range(len(weights)):
                ws.load(sp, n)

        @block.gpsimd
        def _(pool):
            for t in k["kbh"] + k["kbl"]:
                nc.gpsimd.memset(f32(t[:]), 0.0)
            for t in (k["v1"], k["v2"], k["v3"]):
                nc.gpsimd.memset(t[:], 1.0 if t is k["v1"] else 0.0)

        @block.tensor
        def _(pe):
            pe.wait_ge(small_loaded, 16 * len(small))
            for c in range(CH):
                nc.tensor.matmul(ps[1][:, c * B:(c + 1) * B], w_e1[:, c * P:(c + 1) * P], cond[:], start=True, stop=True)
            for c in range(CH):
                mm = nc.tensor.matmul(ps[0][:, c * B:(c + 1) * B], w_c1c[:, c * P:(c + 1) * P], cond[:], start=True, stop=True)
            mm.then_inc(cond_done, 1)
            pe.wait_ge(e2_loaded, 16)
            pe.wait_ge(relu_done, 1)
            for c in range(CH):
                mm = nc.tensor.matmul(ps[4][0:B, :], relu1[:, c, :], w_e2[:, c, :], start=(c == 0), stop=(c == CH - 1))
            mm.then_inc(fp_done, 1)
            pe.wait_ge(late_loaded, 16 * len(late))
            for n in range(4):
                for c in range(CH):
                    mm = nc.tensor.matmul(ps[2][:, (n * CH + c) * B:(n * CH + c + 1) * B], w_gb[:, n, c * P:(c + 1) * P], cond[:], start=True, stop=True)
            mm.then_inc(gb_done, 1)
            pe.wait_ge(fp_normed, 1)
            for c in range(CH):
                mm = nc.tensor.transpose(ps[5][:, c * B:(c + 1) * B], fp[:, c * P:(c + 1) * P], k["ident"][0:B, 0:B])
            mm.then_inc(turn_done, 1)
            pe.wait_ge(fp_turned, 1)
            for c in range(CH):
                mm = nc.tensor.matmul(ps[6][0:B, 0:P], fp_t[:, c, :], pe_t[:, c, :], start=(c == 0), stop=(c == CH - 1))
            mm.then_inc(logits_done, 1)
            pe.wait_ge(silu_done, 1)
            for c in range(2 * CH):
                mm = nc.tensor.matmul(ps[3][:, c * B:(c + 1) * B], w_c[:, c * P:(c + 1) * P], silu_c[:], start=True, stop=True)
            mm.then_inc(c_done, 1)
            pe.wait_ge(field_scaled, 1)
            nc.tensor.transpose(ps[7][:, 0:B], fa[:], k["ident"][0:B, 0:B]).then_inc(field_done, 1)

        @block.scalar
        def _(act):
            act.wait_ge(small_loaded, 16 * len(small))
            nc.scalar.activation(silu_c[:], cond[:], ACT.Exp, scale=-1.0).then_inc(exp_done, 1)
            act.wait_ge(cond_done, 1)
            for c in range(CH):
                last = nc.scalar.activation(relu1[:, c, :], ps[1][:, c * B:(c + 1) * B], ACT.Relu, bias=col["be1"][:, c:c + 1])
            last.then_inc(relu_done, 1)
            act.wait_ge(squares_done, 1)
            nc.scalar.activation(s1[:, 6:8], s1[:, 6:8], ACT.Sqrt).then_inc(root_done, 1)
            act.wait_ge(variance_done, 1)
            nc.scalar.activation(s1[0:B, 2:3], s1[0:B, 1:2], ACT.Sqrt).then_inc(deviation_done, 1)
            act.wait_ge(logits_shifted, 1)
            nc.scalar.activation(fa[:], fa[:], ACT.Exp, accum_out=s1[0:B, 5:6]).then_inc(soft_done, 1)
            for n in range(len(weights)):
                ws.high(act, n)

        @block.vector
        def _(dve):
            count = [0]

            def done(ins):
                count[0] += 1
                ins.then_inc(dve_step, 1)
                dve.wait_ge(dve_step, count[0])

            nc.vector.memset(k["ones"][:], 1.0)
            nc.vector.memset(k["lift"][:], LIFT)
            done(nc.vector.memset(ones_f[:], 1.0))
            nc.vector.tensor_copy(k["ones_b"][:], ones_f[:])
            dve.wait_ge(small_loaded, 16 * len(small))
            dve.wait_ge(exp_done, 1)
            done(nc.vector.tensor_scalar_add(silu_c[:], silu_c[:], 1.0))
            done(nc.vector.reciprocal(silu_c[:], silu_c[:]))
            nc.vector.tensor_tensor(silu_c[:], silu_c[:], cond[:], ALU.mult).then_inc(silu_done, 1)
            nc.vector.tensor_tensor(sq[:, 0:B], cond[:], cond[:], ALU.mult)
            done(nc.vector.tensor_tensor(sq[:, B:B + 4], qr[:], qr[:], ALU.mult))
            nc.vector.tensor_reduce(s1[:, 6:7], sq[:, 0:B], AX_X, ALU.add)
            done(nc.vector.tensor_reduce(s1[:, 7:8], sq[:, B:B + 4], AX_X, ALU.add))
            nc.vector.tensor_scalar_add(s1[:, 6:8], s1[:, 6:8], 1e-8).then_inc(squares_done, 1)
            dve.wait_ge(cond_done, 1)
            for c in range(CH):
                nc.vector.tensor_scalar_add(k["tanh_bias"][:, c, :], ps[0][:, c * B:(c + 1) * B], col["bc1"][:, c:c + 1])
            done(nc.vector.tensor_copy(k["wc2"][:, :, 0:H], w_c2[:]))
            nc.vector.tensor_tensor(k["wc2"][:, :, H:2 * H], w_c2[:], f32(k["wc2"][:, :, 0:H]), ALU.subtract)
            nc.vector.tensor_copy(k["ident_r"][:], k["ident"][:])
            done(nc.vector.tensor_copy(maskf[:], mask8[:]))
            nc.vector.tensor_scalar(k["mask"][:], maskf[:], MASKED, None, ALU.mult)
            done(nc.vector.tensor_reduce(tq[:, 0:1], maskf[:], AX_X, ALU.add))
            done(nc.vector.tensor_scalar(tq[:, 0:1], tq[:, 0:1], -1.0, float(P), ALU.mult, ALU.add))
            done(nc.vector.tensor_scalar_min(tq[:, 0:1], tq[:, 0:1], 1.0))
            done(nc.vector.reciprocal(tq[:, 1:2], tq[:, 0:1]))
            nc.vector.tensor_tensor(k["any_key"][:], tq[:, 0:1], tq[:, 1:2], ALU.mult)
            dve.wait_ge(root_done, 1)
            done(nc.vector.reciprocal(s1[:, 6:8], s1[:, 6:8]))
            nc.vector.tensor_scalar(lq[:], cond[:, 0:4], s1[:, 6:7], None, ALU.mult)
            done(nc.vector.tensor_scalar(rq[:], qr[:], s1[:, 7:8], gate[:, 0:1], ALU.mult, ALU.mult))
            sl = [[1, -1, -1, -1], [1, 1, -1, 1], [1, 1, 1, -1], [1, -1, 1, 1]]
            il = [[0, 1, 2, 3], [1, 0, 3, 2], [2, 3, 0, 1], [3, 2, 1, 0]]
            sr = [[1, 1, 1, 1], [-1, 1, -1, 1], [-1, 1, 1, -1], [-1, -1, 1, 1]]
            for i in range(4):
                for j in range(4):
                    nc.vector.tensor_scalar(lm[:, 4 * i + j:4 * i + j + 1], lq[:, il[i][j]:il[i][j] + 1], float(sl[i][j]), None, ALU.mult)
                    last = nc.vector.tensor_scalar(rm[:, 4 * i + j:4 * i + j + 1], rq[:, il[i][j]:il[i][j] + 1], float(sr[i][j]), None, ALU.mult)
            done(last)
            dve.wait_ge(fp_done, 1)
            done(nc.vector.tensor_tensor(fp[:], ps[4][0:B, :], rows["be2"][:], ALU.add))
            done(nc.vector.tensor_reduce(s1[0:B, 0:1], fp[:], AX_X, ALU.add))
            done(nc.vector.tensor_scalar(s1[0:B, 0:1], s1[0:B, 0:1], -1.0 / E, None, ALU.mult))
            done(nc.vector.tensor_scalar(fp[:], fp[:], s1[0:B, 0:1], None, ALU.add))
            done(nc.vector.tensor_tensor(sq[0:B, :], fp[:], fp[:], ALU.mult))
            done(nc.vector.tensor_reduce(s1[0:B, 1:2], sq[0:B, :], AX_X, ALU.add))
            nc.vector.tensor_scalar(s1[0:B, 1:2], s1[0:B, 1:2], 1.0 / E, 1e-5, ALU.mult, ALU.add).then_inc(variance_done, 1)
            dve.wait_ge(deviation_done, 1)
            done(nc.vector.reciprocal(s1[0:B, 3:4], s1[0:B, 2:3]))
            done(nc.vector.scalar_tensor_tensor(out=fp[:], in0=fp[:], scalar=s1[0:B, 3:4], in1=rows["ln_g"][:], op0=ALU.mult, op1=ALU.mult))
            nc.vector.tensor_tensor(fp[:], fp[:], rows["ln_b"][:], ALU.add).then_inc(fp_normed, 1)
            dve.wait_ge(gb_done, 1)
            for n, (name, bias) in enumerate((("g1", "g1b"), ("b1", "b1b"), ("g2", "g2b"), ("b2", "b2b"))):
                if n == 1:
                    dve.wait_ge(turn_done, 1)
                    nc.vector.tensor_copy(fp_t[:], ps[5][:, 0:CH * B].rearrange("p (c b) -> p c b", c=CH)).then_inc(fp_turned, 1)
                for c in range(CH):
                    o = (n * CH + c) * B
                    nc.vector.tensor_scalar_add(k[name][:, c, :], ps[2][:, o:o + B], col[bias][:, c:c + 1])
            dve.wait_ge(logits_done, 1)
            done(nc.vector.reduce_max(s1[0:B, 4:5], ps[6][0:B, 0:P], AX_X))
            nc.vector.tensor_scalar(fa[:], ps[6][0:B, 0:P], s1[0:B, 4:5], None, ALU.subtract).then_inc(logits_shifted, 1)
            for m in range(4):
                for i in range(4):
                    row = k["mix"][:, 4 * i:4 * i + 4]
                    if m == 0:
                        last = nc.vector.tensor_scalar(row, rm[:, 0:4], lm[:, 4 * i:4 * i + 1], None, ALU.mult)
                    else:
                        last = nc.vector.scalar_tensor_tensor(out=row, in0=rm[:, 4 * m:4 * m + 4], scalar=lm[:, 4 * i + m:4 * i + m + 1],
                                                              in1=row, op0=ALU.mult, op1=ALU.add)
                done(last)
            for i in range(4):
                nc.vector.tensor_scalar_add(k["mix"][:, 5 * i:5 * i + 1], k["mix"][:, 5 * i:5 * i + 1], 1.0)
            dve.wait_ge(soft_done, 1)
            done(nc.vector.reciprocal(s1[0:B, 4:5], s1[0:B, 5:6]))
            nc.vector.tensor_scalar(fa[:], fa[:], s1[0:B, 4:5], FIELD, ALU.mult, ALU.mult).then_inc(field_scaled, 1)
            dve.wait_ge(c_done, 1)
            for c in range(CH):
                nc.vector.tensor_scalar_add(k["shift"][:, c, :], ps[3][:, c * B:(c + 1) * B], col["bc"][:, c:c + 1])
            for c in range(CH):
                o = (CH + c) * B
                last = nc.vector.tensor_scalar(sc1[:, c, :], ps[3][:, o:o + B], col["bc"][:, CH + c:CH + c + 1], 1.0, ALU.add, ALU.add)
            done(last)
            for c in range(CH):
                nc.vector.tensor_scalar(k["gain"][:, c, :], sc1[:, c, :], col["rms"][:, c:c + 1], None, ALU.mult)
            dve.wait_ge(field_done, 1)
            nc.vector.tensor_copy(k["field"][:], ps[7][:, 0:B])
            for n in range(len(weights)):
                ws.low(dve, n)


def attention(nc, hold, k, tag, x_in, x_out, wh, wl, weights):
    L0, L1, L2 = (tag == t for t in ("L0", "L1", "L2"))
    with ExitStack() as ctx:
        def sb(name, shape, dt=F32):
            return ctx.enter_context(nc.sbuf_tensor(f"{tag}_{name}", shape, dt))

        def sem(name):
            return held(nc, hold, f"{tag}_{name}")

        def bank(name):
            return ctx.enter_context(nc.psum_tensor(f"{tag}_{name}", [P, 512], F32))

        order = [n for n in "kvcqo" if n in weights]

        xf = sb("xf", [P, CH, T])
        xh, xl = sb("xh", [P, CH, T], F32R), sb("xl", [P, CH, T], F32R)
        xres = sb("xres", [P, CH, T])
        qh, ql = sb("qh", [P, CH, T], F32R), sb("ql", [P, CH, T], F32R)
        kh, kl = sb("kh", [P, CH, T], F32R), sb("kl", [P, CH, T], F32R)
        kbh, kbl = k["kbh"], k["kbl"]
        v1, v2, v3 = k["v1"], k["v2"], k["v3"]
        vf = sb("vf", [P, NB, E])
        vr = sb("vr", [P, NB, E])
        shifted = sb("shifted", [P, 2, 4, P])
        top = sb("top", [P, 2, 4])
        pth, ptl = sb("pth", [P, 2, 4, P], F16), sb("ptl", [P, 2, 4, P], F16)
        rz = sb("rz", [P, 2, 8])
        of = sb("of", [P, NB, E])
        oth, otl = sb("oth", [P, CH, T], F32R), sb("otl", [P, CH, T], F32R)
        halves = [slice(0, CH // 2), slice(CH // 2, CH)]
        ws = Splitter(nc, hold, tag, [(weights[n][:, m * CH // 2 * E:(m + 1) * CH // 2 * E], flat3(wh[n][:, part]), flat3(wl[n][:, part]))
                                      for n in order for m, part in enumerate(halves)],
                      [of[:].rearrange("p b e -> p (b e)"), shifted[:].rearrange("p n h j -> p (n h j)"),
                       xres[:].rearrange("p c t -> p (c t)"), vr[:].rearrange("p b e -> p (b e)")])
        if L0:
            tf = sb("tf", [P, 2, 2, T])
            th, tl = sb("th", [P, CH, T], F32R), sb("tl", [P, CH, T], F32R)
            tb = sb("tb", [P, CH, NB])
            fd = sb("fd", [P, NB])
            cz, ce, cc, c8, cf = (sb(n, [P, NB * H]) for n in ("cz", "ce", "cc", "c8", "cf"))
        if L1:
            af = sb("af", [P, CH, T])
        if L1 or L2:
            sq = sb("sq", [P, CH, T])
            half = sb("half", [P, 2, T])
            quarter = sb("quarter", [P, T])
            sd, rs = sb("sd", [P, T]), sb("rs", [P, T])
            gt, bt = sb("gt", [P, CH, NB]), sb("bt", [P, CH, NB])
            eps = sb("eps", [P, 1])

        bank_a = [bank("bank_a0"), bank("bank_a1")]
        bank_s = [bank("bank_s0"), bank("bank_s1")]
        bank_t = [bank("bank_t0"), bank("bank_t1")]
        bank_o = bank("bank_o")
        bank_b = bank("bank_b")

        x_loaded, x_high, x_split, x_normed = sem("x_loaded"), sem("x_high"), sem("x_split"), sem("x_normed")
        res_loaded, res_ready, stored = sem("res_loaded"), sem("res_ready"), sem("stored")
        a_full, a_free = [sem("a_full0"), sem("a_full1")], [sem("a_free0"), sem("a_free1")]
        k_high, q_high = sem("k_high"), sem("q_high")
        kb_ready = [sem("kb_ready0"), sem("kb_ready1")]
        v_first, v_rest, v_second, v_split = sem("v_first"), sem("v_rest"), sem("v_second"), sem("v_split")
        t_high, t_split, tb_ready = sem("t_high"), sem("t_split"), sem("tb_ready")
        coh_sum, coh_z, coh_e, coh_step, fd_ready = sem("coh_sum"), sem("coh_z"), sem("coh_e"), sem("coh_step"), sem("fd_ready")
        s_full, top_ready, shift_done, exp_done = sem("s_full"), sem("top_ready"), sem("shift_done"), sem("exp_done")
        t_full, p_high, p_low = sem("t_full"), sem("p_high"), sem("p_low")
        pv_done, rz_step, o_free = sem("pv_done"), sem("rz_step"), sem("o_free")
        b_full, b_free, ot_high = sem("b_full"), sem("b_free"), sem("ot_high")
        sq_ready, sum_step = sem("sq_ready"), sem("sum_step")
        norm_step, eps_set, y_ready = sem("norm_step"), sem("eps_set"), sem("y_ready")

        fills = [(kind, half) for kind in ("okvcq" if L0 else "okvq") for half in range(2)]
        a_per = len(fills) // 2
        spans = [2, 1, 1, 2, 1, 1, 2, 1, 2, 3, 3, 1] if L0 else [2, 1, 1, 1, 1, 1, 1, 1, 2, 2, 2, 1]
        pieces, at = [], 0
        for n in spans:
            pieces.append([(fills[m // 2], m % 2) for m in range(at, at + n)])
            at += n
        assert at == 2 * len(fills) and len(spans) == SLOTS

        def a_turn(p, fill):
            n = fills.index(fill)
            if fill[0] == "o":
                last = isinstance(p, int) and p == G - 1
                return n % 2, a_per * G - 1 if last else a_per * (p + 2) - 2
            return n % 2, n // 2 - 1 if isinstance(p, int) and p == 0 else a_per * p - 2 + n // 2

        def a_done(p, fill):
            return a_turn(p, fill)[1] + 1

        def ended(slot):
            return [fill for fill, part in pieces[slot] if part == 1]

        def active(i, fill):
            if fill[0] == "o":
                return not (isinstance(i, int) and i < 1)
            return has(i, 1)

        def group_of(i, fill):
            return i - 1 if fill[0] == "o" else i + 1

        def b_turn(i, name):
            if L0:
                return 5 * i + ["coh", "vsum0", "ot0", "vsum1", "ot1"].index(name)
            order = ["ot0", "norm", "ot1"].index(name)
            if L1:
                return 3 * i - (1 if order or not isinstance(i, int) or i else 0) + order
            missing = 0
            if isinstance(i, int) and i >= G - 2:
                missing = i - (G - 2) + (1 if order else 0)
            return 2 + 3 * i + order - missing

        def o_turn(i, j):
            return 4 * i + j

        def value_slot(u):
            return min(u + 3, UNITS + 1)

        def split_after(s):
            return [n for n in range(s, s + 2) if s % 2 == 0 and n < len(ws.loads) and not (L2 and n < 2)]

        def iterate(eng, body):
            body(0)
            with eng.Fori(1, G - 2) as i:
                body(i)
            body(G - 2)
            body(G - 1)

        def has(i, ahead):
            return not isinstance(i, int) or i + ahead < G

        block = ctx.enter_context(nc.Block())

        @block.sync
        def _(sp):
            def load(n):
                if positive(n):
                    sp.wait_ge(x_split, n)
                sp.dma_start(xf[:], x_in[bass.ds(n, 1)].rearrange("g p c t -> (g p) c t")).then_inc(x_loaded, 16)

            def store(n):
                if L1:
                    sp.wait_ge(res_ready, n + 1)
                else:
                    for m in range(2):
                        sp.wait_ge(a_free[m], a_done(n, ("o", m)))
                sp.dma_start(x_out[bass.ds(n, 1)].rearrange("g p c t -> (g p) c t"), xres[:]).then_inc(stored, 16)

            def spread_keys(p, b):
                if positive(UNITS * (p - 1) + 4 * (b + 1)):
                    sp.wait_ge(s_full, UNITS * (p - 1) + 4 * (b + 1))
                for m in range(2):
                    sp.wait_ge(a_free[m], a_done(p, ("k", m)))
                for dst, src in ((kbh, kh), (kbl, kl)):
                    for h in range(4):
                        rows = slice(HD * h, HD * (h + 1))
                        sp.dma_start(f32(dst[b][rows, :, h, :]), f32(src[rows, :, b * P:(b + 1) * P])).then_inc(kb_ready[b], 16)

            load(0)
            for n in range(len(ws.loads)):
                if n == 4:
                    load(1)
                ws.load(sp, n)
            spread_keys(0, 0)
            spread_keys(0, 1)
            sp.wait_ge(ws.low_done, len(ws.loads))

            def load_residual(i):
                if positive(16 * i):
                    sp.wait_ge(stored, 16 * i)
                sp.dma_start(xres[:], x_in[bass.ds(i, 1)].rearrange("g p c t -> (g p) c t")).then_inc(res_loaded, 16)

            def body(i):
                if has(i, 2):
                    load(i + 2)
                if L1 and has(i, 1):
                    spread_keys(i + 1, 0)
                    spread_keys(i + 1, 1)
                if positive(i):
                    store(i - 1)
                load_residual(i)
                if not L1 and has(i, 1):
                    spread_keys(i + 1, 0)
                    spread_keys(i + 1, 1)

            iterate(sp, body)
            store(G - 1)
            sp.wait_ge(stored, 16 * G)

        @block.tensor
        def _(pe):
            def mm3(out, w_h, w_l, x_h, x_l, first=True, last=True):
                nc.tensor.matmul(out, w_h, x_h, start=first, stop=False)
                nc.tensor.matmul(out, w_l, x_h, start=False, stop=False)
                return nc.tensor.matmul(out, w_h, x_l, start=False, stop=last)

            def project(p, fill, part):
                kind, m = fill
                bk, n = a_turn(p, fill)
                if part == 0:
                    if positive(n):
                        pe.wait_ge(a_free[bk], n)
                    if isinstance(p, int) and p == 0 and kind in order and kind != "o":
                        pe.wait_ge(ws.low_done, 2 * order.index(kind) + 2)
                    if fill == ("k", 0):
                        pe.wait_ge(x_split, p + 1)
                    if fill == ("o", 0):
                        pe.wait_ge(b_free, b_turn(p, "ot1") + 1)
                if kind == "v":
                    for c in (2 * part, 2 * part + 1):
                        mm = mm3(bank_a[bk][:], xh[:, c, m * P:(m + 1) * P], xl[:, c, m * P:(m + 1) * P], wh["v"][:, c, :], wl["v"][:, c, :],
                                 first=(c == 0), last=(c == CH - 1))
                else:
                    o = 2 * m + part
                    x_h, x_l = (oth, otl) if kind == "o" else (xh, xl)
                    for c in range(CH):
                        mm = mm3(bank_a[bk][:, part * T:(part + 1) * T], wh[kind][:, c, o * P:(o + 1) * P], wl[kind][:, c, o * P:(o + 1) * P],
                                 x_h[:, c, :], x_l[:, c, :], first=(c == 0), last=(c == CH - 1))
                if part == 1:
                    mm.then_inc(a_full[bk], 1)

            def scores(i, u):
                b, c = divmod(u, CH)
                n = UNITS * i + u
                if positive(n - 1):
                    pe.wait_ge(shift_done, n - 1)
                if u == 0:
                    for m in range(2):
                        pe.wait_ge(a_free[m], a_done(i, ("q", m)))
                if c == 0:
                    pe.wait_ge(kb_ready[b], KB_DONE * (i + 1))
                out = bank_s[u % 2][:]
                q_h, q_l = qh[:, c, b * P:(b + 1) * P], ql[:, c, b * P:(b + 1) * P]
                k_h, k_l = (t[b][:, c].rearrange("p h j -> p (h j)") for t in (kbh, kbl))
                mm = mm3(out, q_h, q_l, k_h, k_l, last=not L1)
                if L1:
                    mm = nc.tensor.matmul(out.rearrange("p (h j) -> p h j", h=4), k["ident_r"][:], bcast_mid(k["mask"][:], 4), start=False, stop=True)
                mm.then_inc(s_full, 1)

            def turn_probs(i, u):
                n = UNITS * i + u
                pe.wait_ge(exp_done, n + 1)
                if positive(n - 1):
                    pe.wait_ge(p_low, n - 1)
                for h in range(4):
                    mm = nc.tensor.transpose(bank_t[u % 2][:, h * P:(h + 1) * P], shifted[:, u % 2, h, :], k["ident"][:])
                mm.then_inc(t_full, 1)

            def weigh_values(i, u):
                b, c = divmod(u, CH)
                n = UNITS * i + u
                if u == 0:
                    pe.wait_ge(v_split, i + 1)
                if u % 2 == 0:
                    if positive(o_turn(i, u // 2)):
                        pe.wait_ge(o_free, o_turn(i, u // 2))
                pe.wait_ge(p_low, n + 1)
                for h in range(4):
                    o = ((u % 2) * 4 + h) * VW
                    passes = [(p, v) for p, parts in ((pth, (v1, v2, v3)), (ptl, (v1, v2))) for v in parts]
                    for n, (p, v) in enumerate(passes):
                        mm = nc.tensor.matmul(bank_o[:, o:o + VW], p[:, u % 2, h, :], v[:, b, 4 * c + h, :], start=(n == 0), stop=(n == len(passes) - 1))
                mm.then_inc(pv_done, 1)

            def coherence(i):
                if positive(b_turn(i, "coh")):
                    pe.wait_ge(b_free, b_turn(i, "coh"))
                pe.wait_ge(t_split, 2 * (i + 1))
                for b in range(NB):
                    both = bank_b[:, 2 * b * H:2 * (b + 1) * H]
                    for c in range(CH):
                        nc.tensor.matmul(both, th[:, c, b * P:(b + 1) * P], k["wc2"][:, c, :], start=(c == 0), stop=(c == CH - 1), skip_group_check=True)
                    for c in range(CH):
                        mm = nc.tensor.matmul(both[:, 0:H], tl[:, c, b * P:(b + 1) * P], k["wc2"][:, c, 0:H], start=False, stop=(c == CH - 1), skip_group_check=True)
                mm.then_inc(b_full, 1)

            def sum_values(i, b):
                pe.wait_ge(b_free, b_turn(i, f"vsum{b}"))
                out = bank_b[:].rearrange("p (h d) -> p h d", h=H)
                for n, v in enumerate((v1, v2, v3)):
                    mm = nc.tensor.matmul(out, k["ones_b"][:], v[:, b, :, 0:HD], start=(n == 0), stop=(n == 2))
                mm.then_inc(b_full, 1)

            def turn_output(i, b):
                if positive(b_turn(i, f"ot{b}")):
                    pe.wait_ge(b_free, b_turn(i, f"ot{b}"))
                if not L0:
                    pe.wait_ge(o_free, o_turn(i, 2 * b + 1) + 1)
                for c in range(CH):
                    mm = nc.tensor.transpose(bank_b[:, c * P:(c + 1) * P], of[:, b, c * P:(c + 1) * P], k["ident"][:])
                mm.then_inc(b_full, 1)

            def norm_sum(turn, n):
                if positive(turn):
                    pe.wait_ge(b_free, turn)
                pe.wait_ge(sum_step, 2 * (n + 1))
                nc.tensor.matmul(bank_b[:, 0:T], k["ones"][:], quarter[:], start=True, stop=True).then_inc(b_full, 1)

            if L2:
                norm_sum(0, 0)
            for s in range(SLOTS):
                if s == 7 and L2:
                    norm_sum(1, 1)
                for fill, part in pieces[s]:
                    if active(-1, fill):
                        project(0, fill, part)

            def body(i):
                def project_pieces(todo):
                    for fill, part in todo:
                        if active(i, fill):
                            project(group_of(i, fill), fill, part)

                for s in range(SLOTS):
                    ahead = 1 if s in (0, UNITS, UNITS + 1, UNITS + 2) else 0
                    if s == 5 and L0:
                        sum_values(i, 0)
                    if s == 8:
                        turn_output(i, 0)
                    project_pieces(pieces[s][:ahead])
                    if s == 10:
                        turn_output(i, 1)
                    if s == 0 and L0:
                        coherence(i)
                    if s == 9 and L0:
                        sum_values(i, 1)
                    if s < UNITS:
                        scores(i, s)
                    for u in range(UNITS):
                        if value_slot(u) == s:
                            weigh_values(i, u)
                    if s == 1 and not L0:
                        project_pieces(pieces[s][ahead:])
                        ahead = len(pieces[s])
                    if 1 <= s <= UNITS:
                        turn_probs(i, s - 1)
                    project_pieces(pieces[s][ahead:])
                    if s == 8 and L1 and positive(i):
                        norm_sum(b_turn(i, "norm"), i - 1)
                    if s == 8 and L2 and has(i, 2):
                        norm_sum(b_turn(i, "norm"), i + 2)
                if isinstance(i, int) and i == 0:
                    pe.wait_ge(ws.low_done, len(ws.loads))

            iterate(pe, body)
            for m in range(2):
                for part in range(2):
                    project(G - 1, ("o", m), part)
            if L1:
                norm_sum(3 * G - 1, G - 1)

        @block.scalar
        def _(act):
            def read_fill(p, fill):
                kind, m = fill
                bk, n = a_turn(p, fill)
                if (kind == "v" and L0) or (kind == "o" and not L1):
                    return
                act.wait_ge(a_full[bk], n + 1)
                if kind == "o":
                    if m == 0:
                        act.wait_ge(res_ready, p)
                    nc.scalar.activation(af[:, 2 * m:2 * m + 2, :], bank_a[bk][:].rearrange("p (c t) -> p c t", c=2), ACT.Copy).then_inc(a_free[bk], 1)
                    if m == 1:
                        for b in range(2):
                            act.wait_ge(a_free[b], a_done(p, ("o", b)))
                        squares(p, af)
                    return
                if kind == "v":
                    if positive(p):
                        act.wait_ge(v_split, p)
                    nc.scalar.activation(vf[:, m, :], bank_a[bk][:], ACT.Copy).then_inc(a_free[bk], 1)
                    return
                src = bank_a[bk][:].rearrange("p (c t) -> p c t", c=2)
                if kind == "c":
                    if positive(2 * p + m - 1):
                        act.wait_ge(t_split, 2 * p + m - 1)
                    if m == 0:
                        act.wait_ge(tb_ready, p + 1)
                    for c in range(2):
                        for b in range(NB):
                            last = nc.scalar.activation(tf[:, m, c, b * P:(b + 1) * P], src[:, c, b * P:(b + 1) * P], ACT.Tanh, bias=tb[:, 2 * m + c, b:b + 1])
                            if c == 1 and b == NB - 1:
                                last.then_inc(a_free[bk], 1)
                    if m == 0 and positive(p):
                        act.wait_ge(b_full, b_turn(p - 1, "coh") + 1)
                    act.wait_ge(a_free[bk], n + 1)
                    nc.scalar.activation(th[:, 2 * m:2 * m + 2, :], tf[:, m], ACT.Copy).then_inc(t_high, 1)
                    return
                dst = (kh if kind == "k" else qh)
                if m == 0:
                    if kind == "k":
                        if positive(KB_DONE * p):
                            act.wait_ge(kb_ready[0], KB_DONE * p)
                            act.wait_ge(kb_ready[1], KB_DONE * p)
                    else:
                        if positive(UNITS * p):
                            act.wait_ge(s_full, UNITS * p)
                if L0:
                    bias = k["bk"] if kind == "k" else k["bq"]
                    for c in range(2):
                        last = nc.scalar.activation(dst[:, 2 * m + c, :], src[:, c, :], ACT.Identity, bias=bias[:, 2 * m + c:2 * m + c + 1])
                else:
                    last = nc.scalar.activation(dst[:, 2 * m:2 * m + 2, :], src, ACT.Copy)
                last.then_inc(k_high if kind == "k" else q_high, 1)

            def high_probs(i, u):
                n = UNITS * i + u
                act.wait_ge(t_full, n + 1)
                if positive(n - 1):
                    act.wait_ge(pv_done, n - 1)
                nc.scalar.activation(pth[:, u % 2], bank_t[u % 2][:].rearrange("p (h j) -> p h j", h=4), ACT.Copy).then_inc(p_high, 1)

            def exponentials(i, u):
                act.wait_ge(shift_done, UNITS * i + u + 1)
                nc.scalar.activation(shifted[:, u % 2], shifted[:, u % 2], ACT.Exp, bias=k["lift"][:, 0:1], scale=SCALE).then_inc(exp_done, 1)

            def high_output(i, b):
                act.wait_ge(b_full, b_turn(i, f"ot{b}") + 1)
                if b == 0:
                    if positive(i):
                        act.wait_ge(a_full[1], a_done(i - 1, ("o", 1)))
                nc.scalar.activation(oth[:, :, b * P:(b + 1) * P], bank_b[:].rearrange("p (c t) -> p c t", c=CH), ACT.Copy).then_inc(ot_high, 1)

            if not L0:
                act.wait_ge(eps_set, 1)

            def squares(n, src):
                if positive(2 * n):
                    act.wait_ge(sum_step, 2 * n)
                nc.scalar.activation(sq[:], src[:], ACT.Square).then_inc(sq_ready, 1)

            def deviation(turn, n):
                act.wait_ge(b_full, turn + 1)
                if positive(2 * n):
                    act.wait_ge(norm_step, 2 * n)
                nc.scalar.activation(sd[:], bank_b[:, 0:T], ACT.Sqrt, bias=eps[:, 0:1], scale=1.0 / E).then_inc(b_free, 1)

            def first_values(p):
                if positive(UNITS * p):
                    act.wait_ge(pv_done, UNITS * p)
                if L0 and positive(p):
                    act.wait_ge(b_full, b_turn(p - 1, "vsum1") + 1)
                for m in range(2):
                    act.wait_ge(a_free[m], a_done(p, ("v", m)))
                nc.scalar.activation(v1[:, :, :, 0:HD], vf[:].rearrange("p b (h d) -> p b h d", h=H), ACT.Copy).then_inc(v_first, 1)

            def second_values(p):
                act.wait_ge(v_rest, p + 1)
                nc.scalar.activation(v2[:, :, :, 0:HD], vr[:].rearrange("p b (h d) -> p b h d", h=H), ACT.Copy).then_inc(v_second, 1)

            def high_x(n):
                act.wait_ge(x_normed if L2 else x_loaded, n + 1 if L2 else 16 * (n + 1))
                if not (isinstance(n, int) and n == 0):
                    act.wait_ge(a_full[1], a_done(n - 1, ("q", 1)))
                nc.scalar.activation(xh[:], xf[:], ACT.Copy).then_inc(x_high, 1)

            if L2:
                act.wait_ge(x_loaded, 16)
                squares(0, xf)
                ws.high(act, 0)
                deviation(0, 0)
                ws.high(act, 1)
            high_x(0)
            for s in range(SLOTS):
                if s == 5 and L2:
                    act.wait_ge(x_loaded, 32)
                    squares(1, xf)
                if s == 7 and L2:
                    deviation(1, 1)
                for n in split_after(s):
                    ws.high(act, n)
                for fill in ended(s):
                    if active(-1, fill):
                        read_fill(0, fill)
                if s == SLOTS - 2:
                    first_values(0)
            high_x(1)

            def body(i):
                for s in range(SLOTS):
                    if s == 1 and L0:
                        act.wait_ge(coh_z, i + 1)
                        if positive(5 * i):
                            act.wait_ge(coh_step, 5 * i)
                        nc.scalar.activation(ce[:], cz[:], ACT.Exp, scale=-1.0).then_inc(coh_e, 1)
                    if s == 8:
                        high_output(i, 0)
                    if 1 < s <= UNITS or (s == 1 and L0):
                        high_probs(i, s - 1)
                    if s < UNITS:
                        exponentials(i, s)
                    if s == 1 and not L0:
                        high_probs(i, 0)
                    if s == 0:
                        second_values(i)
                    if s == 2 and L2 and has(i, 2):
                        act.wait_ge(x_loaded, 16 * (i + 3))
                        squares(i + 2, xf)
                    if s == 9 and L1 and positive(i):
                        deviation(b_turn(i, "norm"), i - 1)
                    if s == 9 and L2 and has(i, 2):
                        deviation(b_turn(i, "norm"), i + 2)
                    if s == 10:
                        high_output(i, 1)
                    for fill in ended(s):
                        if active(i, fill):
                            read_fill(group_of(i, fill), fill)
                    if s == 10 and has(i, 1):
                        first_values(i + 1)
                if has(i, 2):
                    high_x(i + 2)

            iterate(act, body)
            for m in range(2):
                read_fill(G - 1, ("o", m))
            if L1:
                deviation(3 * G - 1, G - 1)

        @block.vector
        def _(dve):
            def read_fill(p, fill):
                kind, m = fill
                bk, n = a_turn(p, fill)
                if kind == "c":
                    return
                src = bank_a[bk][:].rearrange("p (c t) -> p c t", c=2)
                if kind == "o":
                    if L1:
                        return
                    dve.wait_ge(res_loaded, 16 * (p + 1))
                    dve.wait_ge(a_full[bk], n + 1)
                    if L0:
                        for c in range(2):
                            o = 2 * m + c
                            last = nc.vector.scalar_tensor_tensor(out=xres[:, o, :], in0=src[:, c, :], scalar=k["bout"][:, o:o + 1],
                                                                  in1=xres[:, o, :], op0=ALU.add, op1=ALU.add)
                    else:
                        part = xres[:, 2 * m:2 * m + 2, :]
                        last = nc.vector.tensor_tensor(part, src, part, ALU.add)
                    last.then_inc(a_free[bk], 1)
                    return
                if kind == "v":
                    if L0:
                        dve.wait_ge(a_full[bk], n + 1)
                        if positive(p):
                            dve.wait_ge(v_split, p)
                        nc.vector.tensor_tensor(vf[:, m, :], bank_a[bk][:], k["bv"][:], ALU.add).then_inc(a_free[bk], 1)
                    return
                high, low = (kh, kl) if kind == "k" else (qh, ql)
                dve.wait_ge(k_high if kind == "k" else q_high, 2 * p + m + 1)
                if L0:
                    bias = k["bk"] if kind == "k" else k["bq"]
                    for c in range(2):
                        o = 2 * m + c
                        last = nc.vector.scalar_tensor_tensor(out=low[:, o, :], in0=src[:, c, :], scalar=bias[:, o:o + 1], in1=f32(high[:, o, :]),
                                                              op0=ALU.add, op1=ALU.subtract)
                else:
                    last = nc.vector.tensor_tensor(low[:, 2 * m:2 * m + 2, :], src, f32(high[:, 2 * m:2 * m + 2, :]), ALU.subtract)
                last.then_inc(a_free[bk], 1)

            def shift_scores(i, u):
                n = UNITS * i + u
                src = bank_s[u % 2][:].rearrange("p (h j) -> p h j", h=4)
                dve.wait_ge(s_full, n + 1)
                nc.vector.reduce_max(top[:, u % 2, :], src, AX_X).then_inc(top_ready, 1)
                dve.wait_ge(top_ready, n + 1)
                if positive(n - 1):
                    dve.wait_ge(t_full, n - 1)
                nc.vector.tensor_tensor(shifted[:, u % 2], src, bcast_last(top[:, u % 2, :], P), ALU.subtract).then_inc(shift_done, 1)

            def low_probs(i, u):
                dve.wait_ge(p_high, UNITS * i + u + 1)
                nc.vector.tensor_tensor(ptl[:, u % 2], bank_t[u % 2][:].rearrange("p (h j) -> p h j", h=4), pth[:, u % 2], ALU.subtract).then_inc(p_low, 1)

            def normalise(i, j):
                b = j // 2
                src = bank_o[:, 0:8 * VW].rearrange("p (h d) -> p h d", h=8)
                r = rz[:, j % 2, :]
                steps = 1 if L2 else 2
                dve.wait_ge(pv_done, UNITS * i + 2 * j + 2)
                nc.vector.reciprocal(r, src[:, :, HD]).then_inc(rz_step, 1)
                dve.wait_ge(rz_step, steps * (4 * i + j) + 1)
                if L0:
                    if j == 0:
                        dve.wait_ge(coh_step, 5 * (i + 1))
                    nc.vector.tensor_tensor(r, r, cf[:, b * H + (j % 2) * 8:b * H + (j % 2) * 8 + 8], ALU.mult).then_inc(rz_step, 1)
                if L1:
                    nc.vector.tensor_scalar(r, r, k["any_key"][:, 0:1], None, ALU.mult).then_inc(rz_step, 1)
                if not L2:
                    dve.wait_ge(rz_step, steps * (4 * i + j) + 2)
                if j % 2 == 0:
                    if positive(i):
                        dve.wait_ge(b_full, b_turn(i - 1, f"ot{b}") + 1)
                dst = of[:, b, (j % 2) * 256:(j % 2) * 256 + 256].rearrange("p (h d) -> p h d", h=8)
                nc.vector.tensor_tensor(dst, src[:, :, 0:HD], bcast_last(r, HD), ALU.mult).then_inc(o_free, 1)

            def add_field(i, b):
                dve.wait_ge(b_full, b_turn(i, f"vsum{b}") + 1)
                dve.wait_ge(fd_ready, i + 1)
                dve.wait_ge(o_free, o_turn(i, 2 * b + 1) + 1)
                nc.vector.scalar_tensor_tensor(out=of[:, b, :], in0=bank_b[:], scalar=fd[:, b:b + 1], in1=of[:, b, :], op0=ALU.mult, op1=ALU.add).then_inc(b_free, 1)

            def low_output(i, b):
                dve.wait_ge(ot_high, NB * i + b + 1)
                part = slice(b * P, (b + 1) * P)
                nc.vector.tensor_tensor(otl[:, :, part], bank_b[:].rearrange("p (c t) -> p c t", c=CH), f32(oth[:, :, part]), ALU.subtract).then_inc(b_free, 1)

            def add_squares(n):
                dve.wait_ge(sq_ready, n + 1)
                nc.vector.tensor_tensor(half[:], sq[:, 0:2, :], sq[:, 2:4, :], ALU.add).then_inc(sum_step, 1)
                dve.wait_ge(sum_step, 2 * n + 1)
                nc.vector.tensor_tensor(quarter[:], half[:, 0, :], half[:, 1, :], ALU.add).then_inc(sum_step, 1)

            def norm_start(n, turn, gains, biases):
                dve.wait_ge(b_free, turn + 1)
                nc.vector.tensor_copy(gt[:], gains[:, :, bass.ds(NB * n, NB)])
                nc.vector.tensor_copy(bt[:], biases[:, :, bass.ds(NB * n, NB)])
                nc.vector.reciprocal(rs[:], sd[:]).then_inc(norm_step, 1)

            def norm_scale(n, tile):
                dve.wait_ge(norm_step, 2 * n + 1)
                nc.vector.tensor_tensor(tile[:], tile[:], bcast_mid(rs[:], CH), ALU.mult).then_inc(norm_step, 1)

            def norm_end(n, tile, out_sem):
                dve.wait_ge(norm_step, 2 * n + 2)
                for c in range(CH):
                    for b in range(NB):
                        part = tile[:, c, b * P:(b + 1) * P]
                        last = nc.vector.tensor_scalar(part, part, gt[:, c, b:b + 1], bt[:, c, b:b + 1], ALU.mult, ALU.add)
                last.then_inc(out_sem, 1)

            if L1 or L2:
                nc.vector.memset(eps[:], 1e-6).then_inc(eps_set, 1)
            if L2:
                add_squares(0)
                ws.low(dve, 0)
                norm_start(0, 0, k["g1"], k["b1"])
                norm_scale(0, xf)
                norm_end(0, xf, x_normed)
            dve.wait_ge(x_high, 1)
            nc.vector.tensor_tensor(xl[:], xf[:], f32(xh[:]), ALU.subtract).then_inc(x_split, 1)
            if L2:
                ws.low(dve, 1)
            if L0:
                nc.vector.tensor_copy(tb[:], k["tanh_bias"][:, :, 0:NB]).then_inc(tb_ready, 1)
            for s in range(SLOTS):
                if s == 6 and L2:
                    add_squares(1)
                for n in split_after(s):
                    ws.low(dve, n)
                for fill in ended(s):
                    if active(-1, fill):
                        read_fill(0, fill)
                if s == 7 and L2:
                    norm_start(1, 1, k["g1"], k["b1"])
                    norm_scale(1, xf)
                    norm_end(1, xf, x_normed)

            def body(i):
                first = isinstance(i, int) and i == 0
                for s in range(SLOTS):
                    if s < UNITS:
                        shift_scores(i, s)
                    if s == 8:
                        low_output(i, 0)
                    if s == 9 and L1 and not first:
                        norm_start(i - 1, b_turn(i, "norm"), k["gain"], k["shift"])
                    if s == 9 and L2 and has(i, 2):
                        norm_start(i + 2, b_turn(i, "norm"), k["g1"], k["b1"])
                    if s in (4, 6, 8, 9):
                        normalise(i, (4, 6, 8, 9).index(s))
                    if 1 <= s <= UNITS:
                        low_probs(i, s - 1)
                    if s == 0 and L0:
                        dve.wait_ge(b_full, b_turn(i, "coh") + 1)
                        nc.vector.tensor_copy(fd[:], k["field"][:, bass.ds(NB * i, NB)]).then_inc(fd_ready, 1)
                        if positive(i):
                            dve.wait_ge(coh_e, i)
                        z = bank_b[:, 0:2 * NB * H].rearrange("p (b s h) -> p b s h", b=NB, s=2)
                        cz3, bias3 = (t[:].rearrange("p (b h) -> p b h", b=NB) for t in (cz, k["bc2"]))
                        nc.vector.tensor_tensor(cz3, z[:, :, 0, :], bias3, ALU.add).then_inc(coh_sum, 1)
                        dve.wait_ge(coh_sum, i + 1)
                        nc.vector.tensor_tensor(cz3, z[:, :, 1, :], cz3, ALU.add).then_inc(b_free, 1)
                        dve.wait_ge(b_free, b_turn(i, "coh") + 1)
                        nc.vector.tensor_scalar_max(cz[:], cz[:], -88.0).then_inc(coh_z, 1)
                    if s == 3 and L0:
                        dve.wait_ge(coh_e, i + 1)
                        nc.vector.tensor_scalar_add(ce[:], ce[:], 1.0).then_inc(coh_step, 1)
                        dve.wait_ge(coh_step, 5 * i + 1)
                        nc.vector.reciprocal(cc[:], ce[:]).then_inc(coh_step, 1)
                        dve.wait_ge(coh_step, 5 * i + 2)
                        nc.vector.tensor_scalar_add(c8[:], cc[:], 1e-8).then_inc(coh_step, 1)
                        dve.wait_ge(coh_step, 5 * i + 3)
                        nc.vector.reciprocal(c8[:], c8[:]).then_inc(coh_step, 1)
                        dve.wait_ge(coh_step, 5 * i + 4)
                        nc.vector.scalar_tensor_tensor(out=cf[:], in0=cc[:], scalar=1.0 - FIELD, in1=c8[:], op0=ALU.mult, op1=ALU.mult).then_inc(coh_step, 1)
                    if s == 6 and L0:
                        add_field(i, 0)
                    if s == 9 and L0:
                        add_field(i, 1)
                    if s == 10:
                        low_output(i, 1)
                    if s == 6 and L1 and not first:
                        add_squares(i - 1)
                    if s == 9 and L1 and not first:
                        norm_scale(i - 1, af)
                        norm_end(i - 1, af, y_ready)
                    if s == 5 and L2 and has(i, 2):
                        add_squares(i + 2)
                    if s == 9 and L2 and has(i, 2):
                        norm_scale(i + 2, xf)
                        norm_end(i + 2, xf, x_normed)
                    if s == 7 and L0 and has(i, 1):
                        dve.wait_ge(a_free[0], a_done(i, ("c", 0)))
                        dve.wait_ge(a_free[1], a_done(i, ("c", 1)))
                        nc.vector.tensor_copy(tb[:], k["tanh_bias"][:, :, bass.ds(NB * (i + 1), NB)]).then_inc(tb_ready, 1)
                    for fill in ended(s):
                        if active(i, fill):
                            read_fill(group_of(i, fill), fill)

            iterate(dve, body)
            for m in range(2):
                read_fill(G - 1, ("o", m))
            if L1:
                add_squares(G - 1)
                norm_start(G - 1, 3 * G - 1, k["gain"], k["shift"])
                norm_scale(G - 1, af)
                norm_end(G - 1, af, y_ready)

        @block.gpsimd
        def _(pool):
            def low_x(n):
                pool.wait_ge(x_high, n + 1)
                nc.gpsimd.tensor_tensor(xl[:], xf[:], f32(xh[:]), ALU.subtract).then_inc(x_split, 1)

            def parts(t):
                return t[:].rearrange("p b (h d) -> p b h d", h=H)

            def rest_of_values(p):
                pool.wait_ge(v_first, p + 1)
                nc.gpsimd.tensor_tensor(parts(vr), parts(vf), v1[:, :, :, 0:HD], ALU.subtract).then_inc(v_rest, 1)

            def third_values(p):
                pool.wait_ge(v_second, p + 1)
                nc.gpsimd.tensor_tensor(v3[:, :, :, 0:HD], parts(vr), v2[:, :, :, 0:HD], ALU.subtract).then_inc(v_split, 1)

            def low_t(p):
                for m in range(2):
                    pool.wait_ge(t_high, 2 * p + m + 1)
                    nc.gpsimd.tensor_tensor(tl[:, 2 * m:2 * m + 2, :], tf[:, m], f32(th[:, 2 * m:2 * m + 2, :]), ALU.subtract).then_inc(t_split, 1)

            if L0:
                low_t(0)
            pool.wait_ge(ws.low_done, len(ws.loads))
            rest_of_values(0)
            low_x(1)

            def body(i):
                third_values(i)
                if has(i, 1):
                    if L0:
                        low_t(i + 1)
                    rest_of_values(i + 1)
                if L1 and positive(i):
                    add_residual(i - 1)
                if has(i, 2):
                    low_x(i + 2)

            def add_residual(n):
                pool.wait_ge(y_ready, n + 1)
                pool.wait_ge(res_loaded, 16 * (n + 1))
                nc.gpsimd.tensor_tensor(xres[:], xres[:], af[:], ALU.add).then_inc(res_ready, 1)

            iterate(pool, body)
            if L1:
                add_residual(G - 1)


def gated_mlp(nc, hold, k, x_in, layer_in, partial, x_out, w_gate, w_hid, w_out):
    tag = "mlp"
    groups = SWEEPS * FG
    with ExitStack() as ctx:
        def sb(name, shape, dt=F32):
            return ctx.enter_context(nc.sbuf_tensor(f"{tag}_{name}", shape, dt))

        def sem(name):
            return held(nc, hold, f"{tag}_{name}")

        def bank(name):
            return ctx.enter_context(nc.psum_tensor(f"{tag}_{name}", [P, FT], F32))

        wg = [sb("wgh", [P, HC, CH, P], F32R), sb("wgl", [P, HC, CH, P], F32R)]
        wu = [sb("wuh", [P, HC, CH, P], F32R), sb("wul", [P, HC, CH, P], F32R)]
        wo = [sb("woh", [P, HC, E], F32R), sb("wol", [P, HC, E], F32R)]
        loads = []
        for n in range(0, SWEEPS * HC, 2):
            at = n % HC
            for dram, tiles in ((w_gate, wg), (w_hid, wu)):
                loads.append((dram[:, n:n + 2].rearrange("p n c e -> p (n c e)"), *(t[:, at:at + 2].rearrange("p n c e -> p (n c e)") for t in tiles)))
            loads.append((w_out[:, n:n + 2, :].rearrange("p n e -> p (n e)"), *(t[:, at:at + 2].rearrange("p n e -> p (n e)") for t in wo)))
        per_sweep = len(loads) // SWEEPS

        xf = sb("xf", [P, CH, FT])
        hh = [sb(f"hh{n}", [P, CH, FT], F32R) for n in range(2)]
        hl = [sb(f"hl{n}", [P, CH, FT], F32R) for n in range(2)]
        res = sb("res", [P, CH, FT])
        yt = sb("yt", [P, CH, FT])
        ot = sb("ot", [P, CH, FT])
        ws = Splitter(nc, hold, tag, loads, [sb(f"stage{n}", [P, 2 * E]) for n in range(2)] +
                      [ot[:, n:n + 2].rearrange("p c t -> p (c t)") for n in (0, 2)])
        half, quarter = sb("half", [P, 2, FT]), sb("quarter", [P, FT])
        sd, rs = sb("sd", [P, FT]), sb("rs", [P, FT])
        gt, bt = sb("gt", [P, CH, FT // P]), sb("bt", [P, CH, FT // P])
        sqb = sb("sqb", [P, 2, FT])
        eps = sb("eps", [P, 1])
        sg, act_t = sb("sg", [P, 2, FT]), sb("act_t", [P, 2, FT])
        ah, al = sb("ah", [P, 2, FT], F32R), sb("al", [P, 2, FT], F32R)
        bank_g, bank_u = [bank("bank_g0"), bank("bank_g1")], [bank("bank_u0"), bank("bank_u1")]
        bank_y = [bank(f"bank_y{n}") for n in range(CH)]

        x_loaded, res_loaded, stored = sem("x_loaded"), sem("res_loaded"), sem("stored")
        layer_loaded, res_added = sem("layer_loaded"), sem("res_added")
        sq_ready, sum_step, sd_ready, norm_step, h_high, h_low = (sem(n) for n in ("sq_ready", "sum_step", "sd_ready", "norm_step", "h_high", "h_low"))
        turn_full, silu_done, prod_done, a_high, a_low, down_done = (sem(n) for n in ("turn_full", "silu_done", "prod_done", "a_high", "a_low", "down_done"))
        y_read, mix_step, eps_set, h_ready = sem("y_read"), sem("mix_step"), sem("eps_set"), sem("h_ready")
        row_begun = sem("row_begun")

        TURNS = HC + 1
        NORM_AT = 2

        def pos(j, c):
            return c + 1 if c >= NORM_AT and has(j, 1) else c

        def turn(j, at):
            return 1 + TURNS * j + at

        def par(odd, at):
            return (1 + TURNS * odd + at) % 2

        def has(j, ahead):
            return not isinstance(j, int) or 0 <= j + ahead < groups

        def second(j):
            return j >= FG if isinstance(j, int) else in_second[0]

        def index(j):
            return j % FG if isinstance(j, int) else j - FG if in_second[0] else j

        def wait_bank_free(eng, j, at):
            back = at - 2
            if back < 0:
                if isinstance(j, int) and j == 0:
                    if back == -1:
                        eng.wait_ge(sd_ready, 1)
                    return
                j, back = j - 1, back + TURNS
            if has(j, 1) and back == NORM_AT:
                eng.wait_ge(sd_ready, j + 2)
            else:
                eng.wait_ge(prod_done, HC * j + (back - 1 if has(j, 1) and back > NORM_AT else back) + 1)

        in_second = [False]

        def iterate(eng, body):
            for sweep in range(SWEEPS):
                begin = sweep * FG
                in_second[0] = sweep == 1
                body(begin, 0)
                body(begin + 1, 1)
                with eng.Fori(begin + 2, begin + FG - 2, 2) as j:
                    body(j, 0)
                    body(j + 1, 1)
                body(begin + FG - 2, 0)
                body(begin + FG - 1, 1)

        def replaced(j, c):
            if not isinstance(j, int) or j not in (FG - 1, FG):
                return []
            c = c + HC * (j - (FG - 1))
            if c % 2 == 0:
                return [per_sweep + 3 * (c // 2 - 1) + n for n in range(2)] if 2 <= c <= HC else []
            return [per_sweep + 3 * (c // 2 - 1) + 2] if 3 <= c <= HC + 1 else []

        block = ctx.enter_context(nc.Block())

        @block.sync
        def _(sp):
            def move(n, dram, tile, out, done):
                for g in range(FT // T):
                    d = dram[bass.ds((FT // T) * n + g, 1)].rearrange("g p c t -> (g p) c t")
                    t = tile[:, :, g * T:(g + 1) * T]
                    sp.dma_start(d if out else t, t if out else d).then_inc(done, 16)

            move(0, x_in, xf, False, x_loaded)
            for n in range(6):
                ws.load(sp, n)

            def body(j, odd):
                if has(j, 1):
                    sp.wait_ge(h_low, CH * (j + 1))
                    move(index(j + 1), x_in, xf, False, x_loaded)
                if isinstance(j, int) and j == FG:
                    ws.load(sp, 2 * per_sweep - 2)
                if positive(j):
                    sp.wait_ge(y_read, CH * j)
                    if not second(j) or (isinstance(j, int) and j == FG):
                        move(index(j - 1), partial, res, True, stored)
                        sp.wait_ge(stored, 32 * j)
                if second(j):
                    move(index(j), partial, res, False, res_loaded)
                else:
                    move(j, x_in, res, False, res_loaded)
                    move(j, layer_in, yt, False, layer_loaded)
                if isinstance(j, int) and j == 0:
                    for n in range(6, per_sweep):
                        ws.load(sp, n)
                if isinstance(j, int) and j == FG - 1:
                    for n in range(per_sweep, 2 * per_sweep - 2):
                        ws.load(sp, n)
                if isinstance(j, int) and j == FG:
                    ws.load(sp, 2 * per_sweep - 1)
                elif second(j):
                    sp.wait_ge(mix_step, 4 * CH * (j - FG))
                    move(index(j - 1), x_out, ot, True, stored)

            iterate(sp, body)
            for i in range(CH):
                sp.wait_ge(mix_step, 4 * CH * (FG - 1) + 3 * (i + 1))
                for g in range(FT // T):
                    sp.dma_start(x_out[G - FT // T + g, :, i, :], ot[:, i, g * T:(g + 1) * T]).then_inc(stored, 16)
            sp.wait_ge(stored, 32 * (groups - 1) + 32 * CH)

        @block.tensor
        def _(pe):
            def mm3(out, w, x_h, x_l, first, last):
                nc.tensor.matmul(out, w[0], x_h, start=first, stop=False)
                nc.tensor.matmul(out, w[1], x_h, start=False, stop=False)
                return nc.tensor.matmul(out, w[0], x_l, start=False, stop=last)

            def norm_sum(n, b):
                pe.wait_ge(sum_step, 2 * (n + 1))
                nc.tensor.matmul(bank_g[b][:], k["ones"][:], quarter[:], start=True, stop=True).then_inc(turn_full, 1)

            norm_sum(0, 0)

            def down(j, c):
                pe.wait_ge(a_low, HC * j + c + 1)
                if isinstance(j, int) and j in (0, FG):
                    pe.wait_ge(ws.low_done, (per_sweep if j else 0) + 3 * (c // 2) + 3)
                if c == 0:
                    if positive(CH * j):
                        pe.wait_ge(y_read, CH * j)
                for o in range(CH):
                    mm = mm3(bank_y[o][:], [w[:, c, o * P:(o + 1) * P] for w in wo], ah[:, c % 2, :], al[:, c % 2, :], c == 0, c == HC - 1)
                mm.then_inc(down_done, 1)

            def body(j, odd):
                at_once = isinstance(j, int) and j == 0
                if not at_once:
                    pe.wait_ge(h_low, CH * (j + 1))
                for c in range(HC):
                    if c == NORM_AT and has(j, 1):
                        wait_bank_free(pe, j, NORM_AT)
                        norm_sum(j + 1, par(odd, NORM_AT))
                    wait_bank_free(pe, j, pos(j, c))
                    b = par(odd, pos(j, c))
                    if isinstance(j, int) and j in (0, FG):
                        pe.wait_ge(ws.low_done, (per_sweep if j else 0) + 3 * (c // 2) + (1 if at_once and c == 0 else 2))
                    for w, bk in ((wg, bank_g[b]), (wu, bank_u[b])):
                        for e in range(CH):
                            if at_once and c == 0 and w is wg:
                                pe.wait_ge(h_low, e + 1)
                            if at_once and c == 0 and w is wu and e == 0:
                                pe.wait_ge(ws.low_done, 2)
                            mm = mm3(bk[:], [t[:, c, e, :] for t in w], hh[odd][:, e, :], hl[odd][:, e, :], e == 0, e == CH - 1)
                    mm.then_inc(turn_full, 1)
                    if c > 0:
                        down(j, c - 1)
                    elif positive(j):
                        down(j - 1, HC - 1)

            iterate(pe, body)
            down(groups - 1, HC - 1)

        @block.scalar
        def _(act):
            def squares(n):
                act.wait_ge(x_loaded, 32 * (n + 1))
                if positive(2 * n):
                    act.wait_ge(sum_step, 2 * n)
                nc.scalar.activation(half[:], xf[:, 0:2, :], ACT.Square)
                nc.scalar.activation(sqb[:], xf[:, 2:4, :], ACT.Square).then_inc(sq_ready, 1)

            def deviation(n, b, count):
                act.wait_ge(turn_full, count)
                if positive((1 + CH) * n):
                    act.wait_ge(norm_step, (1 + CH) * n)
                nc.scalar.activation(sd[:], bank_g[b][:], ACT.Sqrt, bias=eps[:, 0:1], scale=1.0 / E).then_inc(sd_ready, 1)

            def high_h(n, e, odd):
                act.wait_ge(h_ready, CH * n + e + 1)
                if e == 0 and not (isinstance(n, int) and n < 2):
                    act.wait_ge(turn_full, turn(n - 2, HC) + 1)
                nc.scalar.activation(hh[odd][:, e, :], xf[:, e, :], ACT.Copy).then_inc(h_high, 1)

            act.wait_ge(eps_set, 1)
            squares(0)
            deviation(0, 0, 1)
            for n in range(2):
                ws.high(act, n)
            for e in range(CH):
                high_h(0, e, 0)
            ws.high(act, 2)

            def body(j, odd):
                first = isinstance(j, int) and j == 0
                for c in range(HC):
                    if first and c % 2 == 0 and c + 2 < HC:
                        for n in range(3):
                            ws.high(act, 3 * (c // 2 + 1) + n)
                    n = HC * j + c
                    act.wait_ge(turn_full, turn(j, pos(j, c)) + 1)
                    if positive(n - 1):
                        act.wait_ge(prod_done, n - 1)
                    nc.scalar.activation(sg[:, c % 2, :], bank_g[par(odd, pos(j, c))][:], ACT.Silu).then_inc(silu_done, 1)
                    if c == NORM_AT - 1 and has(j, 1):
                        deviation(j + 1, par(odd, NORM_AT), turn(j, NORM_AT) + 1)
                    act.wait_ge(prod_done, n + 1)
                    if positive(n - 1):
                        act.wait_ge(down_done, n - 1)
                    nc.scalar.activation(ah[:, c % 2, :], act_t[:, c % 2, :], ACT.Copy).then_inc(a_high, 1)
                    for m in replaced(j, c):
                        pair = (m - per_sweep) // 3
                        if m % 3 < 2:
                            act.wait_ge(turn_full, turn(FG - 1, pos(FG - 1, 2 * pair + 1)) + 1)
                        else:
                            act.wait_ge(down_done, HC * (FG - 1) + 2 * pair + 2)
                        ws.high(act, m)
                    if c == 0 and has(j, 1):
                        squares(j + 1)
                    if NORM_AT + 1 <= c <= NORM_AT + CH and has(j, 1):
                        high_h(j + 1, c - NORM_AT - 1, 1 - odd)

            iterate(act, body)
            act.wait_ge(stored, 32 * (groups - 1))
            act.wait_ge(y_read, CH * (groups - 1) + 1)
            for i in range(CH):
                nc.scalar.activation(ot[:, i, :], yt[:, 0, :], ACT.Copy, scale=k["mix"][:, 4 * i:4 * i + 1]).then_inc(row_begun, 1)

        @block.vector
        def _(dve):
            def norm_start(n):
                dve.wait_ge(sd_ready, n + 1)
                nc.vector.tensor_copy(gt[:], k["g2"][:, :, bass.ds((FT // P) * index(n), FT // P)])
                nc.vector.tensor_copy(bt[:], k["b2"][:, :, bass.ds((FT // P) * index(n), FT // P)])
                nc.vector.reciprocal(rs[:], sd[:]).then_inc(norm_step, 1)

            def norm(n, e):
                dve.wait_ge(norm_step, (1 + CH) * n + 1)
                nc.vector.tensor_tensor(xf[:, e, :], xf[:, e, :], rs[:], ALU.mult).then_inc(norm_step, 1)
                dve.wait_ge(norm_step, (1 + CH) * n + e + 2)
                for b in range(FT // P):
                    part = xf[:, e, b * P:(b + 1) * P]
                    last = nc.vector.tensor_scalar(part, part, gt[:, e, b:b + 1], bt[:, e, b:b + 1], ALU.mult, ALU.add)
                last.then_inc(h_ready, 1)

            def low_h(n, e, odd):
                dve.wait_ge(h_high, CH * n + e + 1)
                nc.vector.tensor_tensor(hl[odd][:, e, :], xf[:, e, :], f32(hh[odd][:, e, :]), ALU.subtract).then_inc(h_low, 1)

            def add_squares(n):
                dve.wait_ge(sq_ready, n + 1)
                nc.vector.tensor_tensor(half[:], half[:], sqb[:], ALU.add).then_inc(sum_step, 1)
                dve.wait_ge(sum_step, 2 * n + 1)
                nc.vector.tensor_tensor(quarter[:], half[:, 0, :], half[:, 1, :], ALU.add).then_inc(sum_step, 1)

            def mix_row(n, i):
                at = 4 * CH * (n - FG) + 4 * i
                if i == 0:
                    dve.wait_ge(stored, 32 * n)
                nc.vector.tensor_scalar(ot[:, i, :], yt[:, 0, :], k["mix"][:, 4 * i:4 * i + 1], None, ALU.mult).then_inc(mix_step, 1)
                for m in range(1, 4):
                    dve.wait_ge(mix_step, at + m)
                    nc.vector.scalar_tensor_tensor(out=ot[:, i, :], in0=yt[:, m, :], scalar=k["mix"][:, 4 * i + m:4 * i + m + 1], in1=ot[:, i, :],
                                                   op0=ALU.mult, op1=ALU.add).then_inc(mix_step, 1)

            def read_sums(j, sweep):
                dve.wait_ge(down_done, HC * (j + 1))
                if sweep == 0:
                    dve.wait_ge(res_added, j + 1)
                else:
                    dve.wait_ge(res_loaded, 32 * (j + 1))
                for o in range(CH):
                    nc.vector.tensor_tensor((yt if sweep else res)[:, o, :], bank_y[o][:], res[:, o, :], ALU.add).then_inc(y_read, 1)
                if sweep == 1:
                    dve.wait_ge(y_read, CH * (j + 1))

            nc.vector.memset(eps[:], 1e-6).then_inc(eps_set, 1)
            add_squares(0)
            norm_start(0)
            for e in range(CH):
                norm(0, e)
                if e == 0:
                    ws.low(dve, 0)
            for n in range(1, 3):
                ws.low(dve, n)

            def body(j, odd):
                first = isinstance(j, int) and j == 0
                for c in range(HC):
                    n = HC * j + c
                    if first and c % 2 == 0 and c + 2 < HC:
                        for m in range(3):
                            ws.low(dve, 3 * (c // 2 + 1) + m)
                    if c == 1 and has(j, 1):
                        add_squares(j + 1)
                    dve.wait_ge(silu_done, n + 1)
                    if positive(n - 1):
                        dve.wait_ge(a_low, n - 1)
                    nc.vector.tensor_tensor(act_t[:, c % 2, :], bank_u[par(odd, pos(j, c))][:], sg[:, c % 2, :], ALU.mult).then_inc(prod_done, 1)
                    mixes = second(j) and not (isinstance(j, int) and j == FG)
                    if c == 0 and positive(j):
                        read_sums(j - 1, int(mixes))
                    if 1 <= c <= CH and mixes:
                        mix_row(j - 1, c - 1)
                    for m in replaced(j, c):
                        ws.low(dve, m)
                    e = c - NORM_AT
                    if has(j, 1):
                        if e == 0:
                            norm_start(j + 1)
                        if 0 <= e < CH:
                            norm(j + 1, e)
                        if 1 <= e <= CH:
                            low_h(j + 1, e - 1, 1 - odd)

            iterate(dve, body)
            read_sums(groups - 1, 1)
            for i in range(CH):
                dve.wait_ge(row_begun, i + 1)
                for m in range(1, 4):
                    if m > 1:
                        dve.wait_ge(mix_step, 4 * CH * (FG - 1) + 3 * i + m - 1)
                    nc.vector.scalar_tensor_tensor(out=ot[:, i, :], in0=yt[:, m, :], scalar=k["mix"][:, 4 * i + m:4 * i + m + 1], in1=ot[:, i, :],
                                                   op0=ALU.mult, op1=ALU.add).then_inc(mix_step, 1)

        @block.gpsimd
        def _(pool):
            for e in range(CH):
                pool.wait_ge(h_high, e + 1)
                nc.gpsimd.tensor_tensor(hl[0][:, e, :], xf[:, e, :], f32(hh[0][:, e, :]), ALU.subtract).then_inc(h_low, 1)

            def body(j, odd):
                for c in range(HC):
                    n = HC * j + c
                    if c == 5 and not second(j):
                        pool.wait_ge(res_loaded, 32 * (j + 1))
                        pool.wait_ge(layer_loaded, 32 * (j + 1))
                        nc.gpsimd.tensor_tensor(res[:], res[:], yt[:], ALU.add).then_inc(res_added, 1)
                    pool.wait_ge(a_high, n + 1)
                    nc.gpsimd.tensor_tensor(al[:, c % 2, :], act_t[:, c % 2, :], f32(ah[:, c % 2, :]), ALU.subtract).then_inc(a_low, 1)

            iterate(pool, body)


def build(nc, a, out):
    scratch = [nc.dram_tensor(f"resid{n}", (G, P, CH, T), F32, kind="Internal").ap() for n in range(4)]
    with ExitStack() as ctx:
        def keep(name, shape, dt=F32):
            return ctx.enter_context(nc.sbuf_tensor("keep_" + name, shape, dt))

        k = {n: keep(n, [P, CH, B]) for n in ("tanh_bias", "gain", "shift", "g1", "b1", "g2", "b2")}
        k["pack"] = keep("pack", [P, sum(PACKED.values())])
        starts = np.cumsum([0] + list(PACKED.values()))
        k["packed"] = {n: k["pack"][:, int(o):int(o) + w] for (n, w), o in zip(PACKED.items(), starts)}
        k |= {n: k["packed"][n] for n in ("bq", "bk", "bout")}
        k["ident"] = k["packed"]["eye"]
        k["bias_rows"] = keep("bias_rows", [P, E + NB * H])
        k["bv"], k["bc2"] = k["bias_rows"][:, 0:E], k["bias_rows"][:, E:]
        k["field"] = keep("field", [P, B])
        k["mix"] = keep("mix", [P, 16])
        k["any_key"] = keep("any_key", [P, 1])
        k["ones"] = keep("ones", [P, P])
        k["ident_r"], k["mask"] = (keep(n, [P, P], F32R) for n in ("ident_r", "mask"))
        k["ones_b"] = keep("ones_b", [P, P], BF16)
        k["lift"] = keep("lift", [P, 1])

        def phase(make, *args):
            hold = []
            make(nc, hold, k, *args)
            nc.clear_and_free_semaphores(hold)
            with nc.Block():
                pass

        def weight_tiles(wctx, tag, names):
            return tuple({n: wctx.enter_context(nc.sbuf_tensor(f"{tag}_w{n}{part}", [P, CH, E], F32R)) for n in names} for part in "hl")

        with ExitStack() as actx:
            def shared(name, shape, dt):
                return actx.enter_context(nc.sbuf_tensor("keep_" + name, shape, dt))

            k["kbh"] = [shared(f"kbh{b}", [P, CH, 4, P], F32R) for b in range(NB)]
            k["kbl"] = [shared(f"kbl{b}", [P, CH, 4, P], F32R) for b in range(NB)]
            for n in ("v1", "v2", "v3"):
                k[n] = shared(n, [P, NB, H, VW], BF16)
            with ExitStack() as wctx:
                wh, wl = weight_tiles(wctx, "L0", "kvqoc")
                k["wc2"] = wctx.enter_context(nc.sbuf_tensor("keep_wc2", [P, CH, 2 * H], F32R))
                early = [(a["L0_" + n], flat3(wh[n]), flat3(wl[n])) for n in "kv"]
                phase(prepare, a, early)
                phase(attention, "L0", a["x"], scratch[0], wh, wl, {n: a["L0_" + n] for n in "cqo"})
            for tag, src, dst in (("L1", scratch[0], scratch[1]), ("L2", scratch[1], scratch[2])):
                with ExitStack() as wctx:
                    wh, wl = weight_tiles(wctx, tag, "kvqo")
                    phase(attention, tag, src, dst, wh, wl, {n: a[f"{tag}_{n}"] for n in "kvqo"})
        phase(gated_mlp, scratch[2], scratch[1], scratch[3], out, a["gate_w"], a["hid_w"], a["out_w"])


def kernel(**inputs):
    import numpy as _np
    import concourse.bacc as _bacc
    from concourse import mybir as _mybir
    from concourse.bass_utils import run_bass_kernel_spmd as _run

    def cols(w):
        w = _np.asarray(w).T
        return w.reshape(w.shape[0] // P, P, w.shape[1]).transpose(1, 0, 2)

    def flat(w):
        w = cols(w)
        return w.reshape(P, -1)

    def by_chunk(v):
        return _np.asarray(v).reshape(-1, P).T

    g = {n.replace("_cond", ""): _np.asarray(v) for n, v in inputs.items()}
    arrays = {}
    arrays["x"] = g["x"].reshape(G, T, CH, P).transpose(0, 3, 2, 1)
    small = {"cond_t": g["cond_256"].T}
    arrays["mask"] = g["mask_SxS_bk1"]
    wqkv = g["L0_Wqkv"].reshape(3, E, E)
    bqkv = g["L0_bqkv"].reshape(3, E)
    for n, w in zip("qkvoc", (wqkv[0], wqkv[1], wqkv[2], g["L0_Wout"], g["L0_Wc1"][:, 0:E])):
        arrays["L0_" + n] = flat(w)
    small["L0_c2"] = flat(g["L0_Wc2"])
    for layer in ("L1", "L2"):
        for n in "qkvo":
            arrays[f"{layer}_{n}"] = flat(g[f"{layer}_W{n}"])
    arrays["w_c1c"] = g["L0_Wc1"][:, E:].T
    arrays["w_e1"] = g["L0_We1"].T
    arrays["w_e2"] = cols(g["L0_We2"])
    arrays["w_c"] = g["L1_Wc"].T
    arrays["w_gb"] = _np.stack([g[f"L2_{n}w"].T for n in ("g1", "b1", "g2", "b2")], axis=1)
    inv = _np.float32(10000.0) ** _np.repeat(_np.arange(0, E, 2, dtype=_np.float32) / _np.float32(E), 2)
    code = _np.sin(_np.arange(P, dtype=_np.float32)[:, None] / inv[None, :])
    arrays["pe_t"] = cols(code.astype(_np.float32))
    small["eye"] = _np.eye(P, dtype=_np.float32)
    small["bq"], small["bk"] = by_chunk(bqkv[0]), by_chunk(bqkv[1])
    small["bout"] = by_chunk(g["L0_bout"])
    arrays["bias_rows"] = _np.concatenate([bqkv[2]] + [g["L0_bc2"]] * NB)
    for n, v in (("bc1", "L0_bc1"), ("be1", "L0_be1"), ("bc", "L1_bc"), ("rms", "L1_rms_scale"), ("g1b", "L2_g1b"),
                 ("b1b", "L2_b1b"), ("g2b", "L2_g2b"), ("b2b", "L2_b2b")):
        small[n] = by_chunk(g[v])
    arrays["row_pack"] = _np.concatenate([g["L0_be2"], g["L0_ln_g"], g["L0_ln_b"]])
    for n in ("gate_w", "hid_w"):
        arrays[n] = cols(g["L2_" + n]).reshape(P, CH, HID // P, P).transpose(0, 2, 1, 3)
    arrays["out_w"] = cols(g["L2_out_w"])
    small["qr_t"] = g["L3_q_right"].T
    small["gate_t"] = g["L3_spectral_gate"].reshape(1, P).T
    arrays["pack"] = _np.concatenate([small[n] for n in PACKED], axis=1)
    arrays = {n: _np.ascontiguousarray(v) for n, v in arrays.items()}

    nc = _bacc.Bacc("TRN2", target_bir_lowering=False, num_devices=1)
    args = {n: nc.dram_tensor("in_" + n, v.shape, _mybir.dt.from_np(v.dtype), kind="ExternalInput").ap() for n, v in arrays.items()}
    out = nc.dram_tensor("out", (G, P, CH, T), F32, kind="ExternalOutput").ap()
    build(nc, args, out)
    r = _run(nc, [{"in_" + n: v for n, v in arrays.items()}], core_ids=[0])
    y = _np.asarray(r.results[0]["out"])
    return _np.ascontiguousarray(y.transpose(0, 3, 2, 1).reshape(B, P, E))
```
